# Optimizing a Trainium2 kernel written in Bass

```python
import numpy as np
import jax
import jax.numpy as jnp

def _softmax(x, axis=-1):
    return jax.nn.softmax(x, axis=axis)
def _gelu(x):
    return jax.nn.gelu(x, approximate=True)
def _silu(x):
    return jax.nn.silu(x)
def _sigmoid(x):
    return jax.nn.sigmoid(x)
def _layernorm(x, axis=-1, eps=1e-5):
    m = jnp.mean(x, axis=axis, keepdims=True)
    v = jnp.var(x, axis=axis, keepdims=True)
    return (x - m) / jnp.sqrt(v + eps)
def _scatter_add(tgt, idx, src, axis=0):
    return tgt.at[idx].add(src)
def _segment_sum(src, seg, n):
    return jax.ops.segment_sum(src, seg, n)

kernel_name = 'mk_conv_attn_hybrid_d2_conv_nhwc128_c7994d'

def setup_inputs(seed: int = 0):
    np.random.seed(seed)
    _w = jnp.asarray
    def _rec_inputs():
        import jax
        import jax.numpy as jnp
        _gk = jax.random.key(seed)
        x = -0.0005207 + 1.001 * jax.random.normal(jax.random.fold_in(_gk, 1), (4, 32, 128, 128), jnp.float32)
        return x
    x = _rec_inputs()
    def _L0_conv_setup():
        import jax, jax.numpy as jnp
        import numpy as np
        N_HEADS = 32
        EPS = 1e-05

        def _inorm(x, w=None, b=None):
            mu = jnp.mean(x, axis=(-2, -1), keepdims=True)
            var = jnp.var(x, axis=(-2, -1), keepdims=True)
            y = (x - mu) * jax.lax.rsqrt(var + EPS)
            if w is not None:
                y = y * w[None, :, None, None] + b[None, :, None, None]
            return y

        def _fourier_resize(x, oh, ow):
            B, C, H, W = x.shape
            if (oh, ow) == (H, W):
                return x
            X = jnp.fft.rfft2(x, norm='forward')
            kh = min(H, oh) // 2
            kw = min(W // 2 + 1, ow // 2 + 1)
            out = jnp.zeros((B, C, oh, ow // 2 + 1), dtype=X.dtype)
            out = out.at[:, :, :kh, :kw].set(X[:, :, :kh, :kw])
            out = out.at[:, :, -kh:, :kw].set(X[:, :, -kh:, :kw])
            return jnp.fft.irfft2(out, s=(oh, ow), norm='forward')

        def _spectral_conv(x, w2, oh, ow):
            w = w2[..., 0] + 1j * w2[..., 1]
            mh = w.shape[2] // 2
            mw = w.shape[3]
            X = jnp.fft.rfft2(x, norm='forward')
            Xk = jnp.concatenate([X[:, :, :mh, :mw], X[:, :, -mh:, :mw]], axis=2)
            Yk = jnp.einsum('bixy,ioxy->boxy', Xk, w)
            B = x.shape[0]
            O = w.shape[1]
            out = jnp.zeros((B, O, oh, ow // 2 + 1), dtype=Yk.dtype)
            out = out.at[:, :, :mh, :mw].set(Yk[:, :, :mh])
            out = out.at[:, :, -mh:, :mw].set(Yk[:, :, mh:])
            return jnp.fft.irfft2(out, s=(oh, ow), norm='forward')

        def _fno_layer(x, conv_w, skip_w, oh, ow, inner_norm=False, act=False):
            skip = jnp.einsum('bixy,oi->boxy', x, skip_w)
            skip = _fourier_resize(skip, oh, ow)
            xf = _spectral_conv(x, conv_w, oh, ow)
            if inner_norm:
                xf = _inorm(xf)
            y = xf + skip
            if act:
                y = jax.nn.gelu(y, approximate=False)
            return y
        key = jax.random.key(seed)
        ks = jax.random.split(key, 16)
        B, T, H, W = (4, 32, 128, 128)

        def cw(k, ci, co, mh2, mw):
            scale = 1.0 / (ci * co)
            return scale * jax.random.normal(k, (ci, co, mh2, mw, 2), jnp.float32)

        def sw(k, co, ci):
            return jax.random.normal(k, (co, ci), jnp.float32) / np.float32(np.sqrt(ci))
        one = jnp.ones((1,), jnp.float32)
        zero = jnp.zeros((1,), jnp.float32)
        return dict(x=jax.random.normal(ks[0], (B, T, H, W), jnp.float32), norm1_w=one, norm1_b=zero, Kcw=cw(ks[1], 1, N_HEADS, 32, 17), Ksw=sw(ks[2], N_HEADS, 1), Qcw=cw(ks[3], 1, N_HEADS, 32, 17), Qsw=sw(ks[4], N_HEADS, 1), Vcw=cw(ks[5], 1, N_HEADS, 32, 17), Vsw=sw(ks[6], N_HEADS, 1), Pcw=cw(ks[7], N_HEADS, 1, 64, 33), Psw=sw(ks[8], 1, N_HEADS), attn_w=one, attn_b=zero, norm2_w=one, norm2_b=zero, m0cw=cw(ks[9], 1, 1, 64, 33), m0sw=sw(ks[10], 1, 1), m1cw=cw(ks[11], 1, 1, 64, 33), m1sw=sw(ks[12], 1, 1), mon_w=one, mon_b=zero)
    _L0_conv_all = _L0_conv_setup()
    _L0_conv_in = {k: v for k, v in _L0_conv_all.items() if k in ('norm1_w', 'norm1_b', 'Kcw', 'Ksw', 'Qcw', 'Qsw', 'Vcw', 'Vsw', 'Pcw', 'Psw', 'attn_w', 'attn_b', 'norm2_w', 'norm2_b', 'm0cw', 'm0sw', 'm1cw', 'm1sw', 'mon_w', 'mon_b', )}
    del _L0_conv_all

    def _L1_attn_setup():
        import jax, jax.numpy as jnp
        import numpy as np
        B, T, C = (16, 2048, 128)
        HEAD_SIZE = 128
        key = jax.random.key(seed)
        k1, k2, k3, k4 = jax.random.split(key, 4)
        x = jax.random.normal(k1, (B, T, C), dtype=jnp.float32)
        scale = (1.0 / np.sqrt(C)).astype(np.float32)
        Wq = jax.random.normal(k2, (HEAD_SIZE, C), dtype=jnp.float32) * scale
        Wk = jax.random.normal(k3, (HEAD_SIZE, C), dtype=jnp.float32) * scale
        Wv = jax.random.normal(k4, (HEAD_SIZE, C), dtype=jnp.float32) * scale
        return {'x': x, 'Wq': Wq, 'Wk': Wk, 'Wv': Wv}
    _L1_attn_all = _L1_attn_setup()
    _L1_attn_in = {k: v for k, v in _L1_attn_all.items() if k in ('Wq', 'Wk', 'Wv', )}
    del _L1_attn_all

    def _L1_ffn_setup():
        import jax, jax.numpy as jnp
        import numpy as np
        B, S, D, E, H, O, K = (512, 2048, 128, 64, 512, 128, 8)
        key = jax.random.key(seed)
        k0, k1, k2, k3 = jax.random.split(key, 4)
        x = jax.random.normal(k0, (B, S, D), dtype=jnp.float32)
        gate_w = jax.random.normal(k1, (E, D), dtype=jnp.float32) * (1.0 / np.sqrt(D))
        gate_b = jnp.zeros((E,), dtype=jnp.float32)
        weight1 = jax.random.uniform(k2, (E, D + 1, H), dtype=jnp.float32, minval=-1.0, maxval=1.0) * (1.0 / np.sqrt(D + 1))
        weight2 = jax.random.uniform(k3, (E, H + 1, O), dtype=jnp.float32, minval=-1.0, maxval=1.0) * (1.0 / np.sqrt(H + 1))
        return {'x': x, 'gate_w': gate_w, 'gate_b': gate_b, 'weight1': weight1, 'weight2': weight2}
    _L1_ffn_all = _L1_ffn_setup()
    _L1_ffn_in = {k: v for k, v in _L1_ffn_all.items() if k in ('gate_w', 'gate_b', 'weight1', 'weight2', )}
    del _L1_ffn_all

    return {
        "x": x,
        "L0_conv_norm1_w": _L0_conv_in["norm1_w"],
        "L0_conv_norm1_b": _L0_conv_in["norm1_b"],
        "L0_conv_Kcw": _L0_conv_in["Kcw"],
        "L0_conv_Ksw": _L0_conv_in["Ksw"],
        "L0_conv_Qcw": _L0_conv_in["Qcw"],
        "L0_conv_Qsw": _L0_conv_in["Qsw"],
        "L0_conv_Vcw": _L0_conv_in["Vcw"],
        "L0_conv_Vsw": _L0_conv_in["Vsw"],
        "L0_conv_Pcw": _L0_conv_in["Pcw"],
        "L0_conv_Psw": _L0_conv_in["Psw"],
        "L0_conv_attn_w": _L0_conv_in["attn_w"],
        "L0_conv_attn_b": _L0_conv_in["attn_b"],
        "L0_conv_norm2_w": _L0_conv_in["norm2_w"],
        "L0_conv_norm2_b": _L0_conv_in["norm2_b"],
        "L0_conv_m0cw": _L0_conv_in["m0cw"],
        "L0_conv_m0sw": _L0_conv_in["m0sw"],
        "L0_conv_m1cw": _L0_conv_in["m1cw"],
        "L0_conv_m1sw": _L0_conv_in["m1sw"],
        "L0_conv_mon_w": _L0_conv_in["mon_w"],
        "L0_conv_mon_b": _L0_conv_in["mon_b"],
        "L1_attn_Wq": _L1_attn_in["Wq"],
        "L1_attn_Wk": _L1_attn_in["Wk"],
        "L1_attn_Wv": _L1_attn_in["Wv"],
        "L1_ffn_gate_w": _L1_ffn_in["gate_w"],
        "L1_ffn_gate_b": _L1_ffn_in["gate_b"],
        "L1_ffn_weight1": _L1_ffn_in["weight1"],
        "L1_ffn_weight2": _L1_ffn_in["weight2"],
    }

def reference(x, L0_conv_norm1_w, L0_conv_norm1_b, L0_conv_Kcw, L0_conv_Ksw, L0_conv_Qcw, L0_conv_Qsw, L0_conv_Vcw, L0_conv_Vsw, L0_conv_Pcw, L0_conv_Psw, L0_conv_attn_w, L0_conv_attn_b, L0_conv_norm2_w, L0_conv_norm2_b, L0_conv_m0cw, L0_conv_m0sw, L0_conv_m1cw, L0_conv_m1sw, L0_conv_mon_w, L0_conv_mon_b, L1_attn_Wq, L1_attn_Wk, L1_attn_Wv, L1_ffn_gate_w, L1_ffn_gate_b, L1_ffn_weight1, L1_ffn_weight2):
    import jax
    import jax.numpy as jnp
    def _L0_conv_ref(x, norm1_w, norm1_b, Kcw, Ksw, Qcw, Qsw, Vcw, Vsw, Pcw, Psw, attn_w, attn_b, norm2_w, norm2_b, m0cw, m0sw, m1cw, m1sw, mon_w, mon_b):
        import jax, jax.numpy as jnp
        import numpy as np
        N_HEADS = 32
        EPS = 1e-05

        def _inorm(x, w=None, b=None):
            mu = jnp.mean(x, axis=(-2, -1), keepdims=True)
            var = jnp.var(x, axis=(-2, -1), keepdims=True)
            y = (x - mu) * jax.lax.rsqrt(var + EPS)
            if w is not None:
                y = y * w[None, :, None, None] + b[None, :, None, None]
            return y

        def _fourier_resize(x, oh, ow):
            B, C, H, W = x.shape
            if (oh, ow) == (H, W):
                return x
            X = jnp.fft.rfft2(x, norm='forward')
            kh = min(H, oh) // 2
            kw = min(W // 2 + 1, ow // 2 + 1)
            out = jnp.zeros((B, C, oh, ow // 2 + 1), dtype=X.dtype)
            out = out.at[:, :, :kh, :kw].set(X[:, :, :kh, :kw])
            out = out.at[:, :, -kh:, :kw].set(X[:, :, -kh:, :kw])
            return jnp.fft.irfft2(out, s=(oh, ow), norm='forward')

        def _spectral_conv(x, w2, oh, ow):
            w = w2[..., 0] + 1j * w2[..., 1]
            mh = w.shape[2] // 2
            mw = w.shape[3]
            X = jnp.fft.rfft2(x, norm='forward')
            Xk = jnp.concatenate([X[:, :, :mh, :mw], X[:, :, -mh:, :mw]], axis=2)
            Yk = jnp.einsum('bixy,ioxy->boxy', Xk, w)
            B = x.shape[0]
            O = w.shape[1]
            out = jnp.zeros((B, O, oh, ow // 2 + 1), dtype=Yk.dtype)
            out = out.at[:, :, :mh, :mw].set(Yk[:, :, :mh])
            out = out.at[:, :, -mh:, :mw].set(Yk[:, :, mh:])
            return jnp.fft.irfft2(out, s=(oh, ow), norm='forward')

        def _fno_layer(x, conv_w, skip_w, oh, ow, inner_norm=False, act=False):
            skip = jnp.einsum('bixy,oi->boxy', x, skip_w)
            skip = _fourier_resize(skip, oh, ow)
            xf = _spectral_conv(x, conv_w, oh, ow)
            if inner_norm:
                xf = _inorm(xf)
            y = xf + skip
            if act:
                y = jax.nn.gelu(y, approximate=False)
            return y
        B, T, H, W = x.shape
        Hs, Ws = (H // 2, W // 2)
        temperature = 1.0
        xa = x.reshape(B * T, 1, H, W)
        xn = _inorm(xa, norm1_w, norm1_b)
        k = _fno_layer(xn, Kcw, Ksw, Hs, Ws)
        q = _fno_layer(xn, Qcw, Qsw, Hs, Ws)
        v = _fno_layer(xn, Vcw, Vsw, H, W)
        nh = k.shape[1]
        kf = k.reshape(B, T, nh, Hs * Ws).transpose(0, 2, 1, 3)
        qf = q.reshape(B, T, nh, Hs * Ws).transpose(0, 2, 1, 3)
        vf = v.reshape(B, T, nh, H * W).transpose(0, 2, 1, 3)
        scores = jnp.einsum('bntk,bnsk->bnts', qf, kf) / (np.float32(np.sqrt(Hs * Ws)) * temperature)
        p_attn = jax.nn.softmax(scores, axis=-1)
        av = jnp.einsum('bnts,bnsk->bntk', p_attn, vf)
        av = av.reshape(B, nh, T, H, W).transpose(0, 2, 1, 3, 4).reshape(B * T, nh, H, W)
        p = _fno_layer(av, Pcw, Psw, H, W)
        a = _inorm(p + xa, attn_w, attn_b)
        an = _inorm(a, norm2_w, norm2_b)
        m = _fno_layer(an, m0cw, m0sw, H, W, inner_norm=True, act=True)
        m = _fno_layer(m, m1cw, m1sw, H, W, inner_norm=True, act=False)
        out = _inorm(m, mon_w, mon_b) + a
        return out.reshape(B, T, H, W)

    def _L1_attn_ref(x, Wq, Wk, Wv):
        import jax, jax.numpy as jnp
        import numpy as np
        B, T, C = (16, 2048, 128)
        HEAD_SIZE = 128
        Bd, Td, Cd = x.shape
        q = jnp.einsum('btc,hc->bth', x, Wq)
        k = jnp.einsum('btc,hc->bth', x, Wk)
        v = jnp.einsum('btc,hc->bth', x, Wv)
        scores = jnp.einsum('bth,bsh->bts', q, k) * Cd ** (-0.5)
        causal = jnp.tril(jnp.ones((Td, Td), dtype=bool))
        scores = jnp.where(causal, scores, -jnp.inf)
        attn = jax.nn.softmax(scores, axis=-1)
        out = jnp.einsum('bts,bsh->bth', attn, v)
        return out

    def _L1_ffn_ref(x, gate_w, gate_b, weight1, weight2):
        import jax, jax.numpy as jnp
        import numpy as np
        B, S, D, E, H, O, K = (512, 2048, 128, 64, 512, 128, 8)
        Bn, Sn, Dn = x.shape
        logits = jnp.einsum('bsd,ed->bse', x, gate_w) + gate_b
        probs = jax.nn.softmax(logits, axis=1)
        vals, idx = jax.lax.top_k(probs.transpose(0, 2, 1), K)
        topv = vals.transpose(0, 2, 1)
        topi = idx.transpose(0, 2, 1)
        flat_idx = topi.reshape(Bn, K * E)
        gathered = jnp.take_along_axis(x, flat_idx[:, :, None], axis=1)
        gathered = gathered.reshape(Bn, K, E, Dn)
        pooled = jnp.einsum('bked,bke->bed', gathered, topv)
        ones = jnp.ones((E, Bn, 1), dtype=x.dtype)
        h = jnp.concatenate([pooled.transpose(1, 0, 2), ones], axis=-1)
        h = jax.nn.gelu(jnp.einsum('ebd,edh->ebh', h, weight1), approximate=False)
        h = jnp.concatenate([h, ones], axis=-1)
        out = jnp.einsum('ebh,eho->ebo', h, weight2)
        out = out.transpose(1, 0, 2)
        weighted = jnp.einsum('beo,bke->bkeo', out, topv).reshape(Bn, K * E, O)
        outputs = jnp.zeros((Bn, Sn, O), dtype=x.dtype)
        outputs = outputs.at[jnp.arange(Bn)[:, None], flat_idx].add(weighted)
        return outputs

    def _gn(v, G=32, eps=1e-5):
        B_, H_, W_, C_ = v.shape
        g = v.reshape(B_, H_, W_, G, C_ // G)
        m = jnp.mean(g, axis=(1, 2, 4), keepdims=True)
        s = jnp.var(g, axis=(1, 2, 4), keepdims=True)
        return ((g - m) / jnp.sqrt(s + eps)).reshape(v.shape)

    def _ln_c(v, eps=1e-6):
        m = jnp.mean(v, axis=-1, keepdims=True)
        s = jnp.var(v, axis=-1, keepdims=True)
        return (v - m) / jnp.sqrt(s + eps)

    def _ln_t(v, eps=1e-5):
        m = jnp.mean(v, axis=-1, keepdims=True)
        s = jnp.var(v, axis=-1, keepdims=True)
        return (v - m) / jnp.sqrt(s + eps)

    def _to_tokens(v):
        B_, H_, W_, C_ = v.shape
        return v.reshape(B_, H_ * W_, C_)
    def _from_tokens(t, like):
        return t.reshape(like.shape)

    x = x + _L0_conv_ref(_gn(x), L0_conv_norm1_w, L0_conv_norm1_b, L0_conv_Kcw, L0_conv_Ksw, L0_conv_Qcw, L0_conv_Qsw, L0_conv_Vcw, L0_conv_Vsw, L0_conv_Pcw, L0_conv_Psw, L0_conv_attn_w, L0_conv_attn_b, L0_conv_norm2_w, L0_conv_norm2_b, L0_conv_m0cw, L0_conv_m0sw, L0_conv_m1cw, L0_conv_m1sw, L0_conv_mon_w, L0_conv_mon_b)
    t = _to_tokens(x)
    t = t + _L1_attn_ref(_ln_t(t), L1_attn_Wq, L1_attn_Wk, L1_attn_Wv)
    t = t + _L1_ffn_ref(_ln_t(t), L1_ffn_gate_w, L1_ffn_gate_b, L1_ffn_weight1, L1_ffn_weight2)
    x = _from_tokens(t, x)
    return x


_drawn_inputs = setup_inputs


def setup_inputs(seed=0):
    import zlib

    import numpy as np

    out = dict(_drawn_inputs(seed))
    spreads = {'L1_ffn_gate_b': (0.0, 2.0)}
    factors = {'L0_conv_Kcw': 32.558,
     'L0_conv_Qcw': 8.0,
     'L0_conv_Vcw': 8.0,
     'L0_conv_Psw': 3.549,
     'L1_ffn_gate_w': 8.0,
     'L1_ffn_weight1': 8.0,
     'L1_ffn_weight2': 8.0}
    for name, (base, spread) in spreads.items():
        noise = np.random.default_rng([zlib.crc32(name.encode()), seed]).standard_normal(out[name].shape)
        drawn = base * np.exp(spread * noise) if base else spread * noise
        out[name] = jnp.asarray(drawn.astype(out[name].dtype))
    for name, factor in factors.items():
        out[name] = (out[name] * factor).astype(out[name].dtype)
    return out
```

```python
import numpy as np
import concourse.bass as bass
from concourse import mybir
from contextlib import ExitStack

F32 = mybir.dt.float32
ALU = mybir.AluOpType
ACT = mybir.ActivationFunctionType
AX = mybir.AxisListType

B, T, H, W = 4, 32, 128, 128
N = B * T
NH = 32
KY, KX = 64, 33
M = KY * KX
LK, LX = 32, 17
ML = LK * LX
NLC = -(-ML // 128)
NR = 6
MR = M // NR
NQ = 8
GW, GE = 4, 16384
EPS = 1e-5
TOK = H * T
NT = T
D = W
EX, HID, TOPK = 64, 512, 8
EG = 4
NEG = -1e30
SCALE = float(D) ** -0.5

CONST_LAYOUT = [("ident", 128), ("ones", 128), ("group", 128), ("mask", 128), ("fh", 66), ("fwr", 132), ("fwi", 132),
                ("ih", 128), ("iw", 128)]


def shape_constants():
    ky = np.concatenate([np.arange(32), np.arange(-32, 0)])
    kx = np.arange(KX)
    p = np.arange(128)
    c = {}
    c["ident"] = np.eye(128)
    c["ones"] = np.full((128, 128), 1.0 / 128)
    c["group"] = (p[:, None] // GW == p[None, :] // GW) / float(GW * T)
    c["mask"] = np.where(p[None, :] > p[:, None], NEG, 0.0)
    a = 2 * np.pi * np.outer(p, kx) / 128
    c["fh"] = np.concatenate([np.cos(a), -np.sin(a)], 1) / 128
    co, si = np.cos(a) / 128, np.sin(a) / 128
    c["fwr"] = np.concatenate([co, -si, co, -si], 1)
    c["fwi"] = np.concatenate([si, co, -si, -co], 1)
    b = 2 * np.pi * np.outer(ky, p) / 128
    c["ih"] = np.concatenate([np.cos(b), -np.sin(b)], 0)
    twice = np.where(kx == 0, 1.0, 2.0)[:, None]
    a = 2 * np.pi * np.outer(kx, p) / 128
    iw = np.zeros((128, 128))
    iw[0:2 * KX] = np.concatenate([twice * np.cos(a), -twice * np.sin(a)], 0)
    c["iw"] = iw
    return np.concatenate([c[n] for n, _ in CONST_LAYOUT], 1).astype(np.float32)


class Steps:

    def __init__(self, eng, sem):
        self.eng, self.sem, self.base, self.n = eng, sem, 0, 0

    def later(self, ins):
        self.n += 1
        ins.then_inc(self.sem, 1)
        self.eng.wait_ge(self.sem, self.base + self.n)


def conv_attn_hybrid(nc, io, out):
    with ExitStack() as ctx:
        def sb(name, shape):
            return ctx.enter_context(nc.sbuf_tensor(name, shape, F32))

        sems = {}

        def sem(name):
            if name not in sems:
                sems[name] = ctx.enter_context(nc.semaphore(name))
            return sems[name]

        CW = sum(w for _, w in CONST_LAYOUT)
        U = sb("U", [128, N, W])
        V = sb("V", [128, 128 * 128])
        A = sb("A", [128, N, 2 * KX])
        Z = sb("Z", [128, 3, M])
        DB = sb("DB", [128, 3, 512])
        CST = sb("CST", [128, CW])
        ST = sb("ST", [128, N, 6])
        MI = sb("MI", [128, 2128])
        PS = ctx.enter_context(nc.psum_tensor("PS", [128, 8, 512], F32))
        e_dram = nc.dram_tensor("e_planes", (NR, NH, 3, MR), F32, kind="Internal").ap()
        x_dram = nc.dram_tensor("x_planes", (NR, N, 3, MR), F32, kind="Internal").ap()
        m_dram = nc.dram_tensor("masks", (B, EX, TOK), F32, kind="Internal").ap()

        cst, o = {}, 0
        for name, w in CONST_LAYOUT:
            cst[name] = CST[:, o:o + w]
            o += w
        ident, ones = cst["ident"], cst["ones"]
        Uf = U[:].rearrange("p n w -> p (n w)")
        Af = A[:].rearrange("p n k -> p (n k)")
        Vn = V[:].rearrange("p (n w) -> p n w", w=W)
        Zk = Z[:].rearrange("p c (k x) -> p c k x", x=KX)

        at = [0]

        def mi(width):
            at[0] += width
            assert at[0] <= 2128
            return MI[:, at[0] - width:at[0]]

        CT = mi(3 * NLC * NH).rearrange("p (c k n) -> p c k n", c=3, k=NLC)
        headw = mi(4 * NH).rearrange("p (c n) -> p c n", c=4)
        headc = mi(4)
        par = mi(12)
        PAR = {n: par[:, i:i + 1] for i, n in enumerate(
            ["norm1_w", "norm1_b", "attn_w", "attn_b", "norm2_w", "norm2_b", "mon_w", "mon_b", "m0sw", "m1sw"])}
        rim, cim = mi(128), mi(128)
        alpha, beta, istat = mi(1), mi(1), mi(4)
        Gd = mi(32)
        Pb = mi(32)
        qk = mi(NH)
        pv = mi(NH)
        G8, rc = mi(8), mi(16)
        Pbt, Mt = (ST[:].rearrange("p n k -> p (n k)")[:, 128 * i:128 * i + 128] for i in range(2))
        rmx = mi(NH)
        lay = mi(8)
        WS = mi(8 * 128).rearrange("p (k n) -> p k n", k=8)

        XN = Uf[:, 0:3072].rearrange("p (c i w) -> p c i w", c=3, i=8)
        XQ = Uf[:, 3072:5120].rearrange("p (c i w) -> p c i w", c=2, i=8)
        XE = Uf[:, 0:2 * M].rearrange("p (c m) -> p c m", c=2)
        XEk = Uf[:, 0:2 * M].rearrange("p (c k x) -> p c k x", c=2, x=KX)
        XL = Uf[:, 4224:5312].rearrange("p (c m) -> p c m", c=2)
        XET = Uf[:, 5376:9600].rearrange("p (k n) -> p k n", n=N)
        XLT = Uf[:, 9600:10880].rearrange("p (c k n) -> p c k n", c=2, k=NLC)
        ZP = [Uf[:, o:o + 2048].rearrange("p (n s) -> p n s", n=16) for o in (0, 2048, 5376, 7424)]
        SD = Uf[:, 12928:13952].rearrange("p (n s) -> p n s", n=NH)
        SE = Uf[:, 13952:14976].rearrange("p (n s) -> p n s", n=NH)
        PT = Uf[:, 8448:9472].rearrange("p (g s) -> p g s", g=NQ)
        EB = Uf[:, 9600:12768].rearrange("p (c k m) -> p c k m", c=3, k=3)
        YB = Uf[:, 0:8448].rearrange("p (c b k m) -> p c b k m", c=2, b=B, k=3)
        XR = Af.rearrange("p (c b k m) -> p c b k m", c=2, b=B, k=3)
        SG = Uf[:, 10880:12928].rearrange("p (k n) -> p k n", n=128)
        SG2 = SG[:, 0, :]
        MV = WS[:, 0:2, :].rearrange("p k n -> p (k n)")
        root_args = [rc[:, 0:4], istat[:, 2:3], WS[:, 3, :], WS[:, 5, :], lay[:, 2:3], lay[:, 2:3], WS[:, 3, :]]
        XS = Af[:, 0:M]

        WP = V[0:NH, 0:2 * M].rearrange("p (k x c) -> p k x c", k=KY, c=2)
        QKV = V[0:NH, 4224:7488].rearrange("p (w k x c) -> p w k x c", w=3, k=LK, c=2)
        P3 = V[0:NH, 7488:13824].rearrange("p (k m) -> p k m", k=3)
        CR = V[0:NH, 13824:14368]
        CI = V[0:NH, 14368:14912]
        T1 = V[0:NH, 14912:15456]
        T2 = V[0:NH, 15456:16000]

        x_nat = io["x"].rearrange("b t h w -> h (b t) w")
        x_img = io["x"].rearrange("b t h w -> (b t) (h w)")
        out_nat = out.rearrange("b t h w -> h (b t) w")

        QT = V[:, 0:TOK]
        KT = V[:, TOK:2 * TOK]
        VV = V[:, 2 * TOK:3 * TOK].rearrange("p (t d) -> p t d", d=D)
        XT = V[:, 3 * TOK:4 * TOK]
        AF = [Af, Z[:].rearrange("p c m -> p (c m)")]
        SR = [Af[:, 0:TOK], Af[:, TOK:2 * TOK]]
        XO = AF[1][:, 0:TOK].rearrange("p (t d) -> p t d", d=D)
        WT3 = AF[1][:, 4096:4096 + 384].rearrange("p (c h) -> p c h", c=3)
        WN3 = AF[1][:, 4480:4864].rearrange("p (c h) -> p c h", c=3)
        PTB = DB
        bmax = AF[1][:, 4864:4880]
        mraw, nmax, rsum, rden = (AF[1][:, 4880 + 2 * i:4882 + 2 * i] for i in range(4))
        gmx = AF[1][:, 4888:4892]
        tkr = AF[1][:, 4896:5024]
        tkn = AF[1][:, 5024:5152]
        gwT = AF[1][:, 5152:5216]
        gwn = AF[1][0:EX, 5216:5344]
        gb2 = AF[1][:, 5344:5345]
        top8 = AF[1][:, 5352:5360]
        poolT = AF[1][:, 5360:5616].rearrange("p (b e) -> p b e", b=B)
        b2n = AF[1][0:EX, 5616:5744]
        outE = AF[1][0:EX, 5744:6256].rearrange("p (b o) -> p b o", b=B)

        NF2, NTR, NIM = 11, 17, 32
        CH = NT * (NT // 4 + 1) // 2

        blocks = [i // 4 + 1 for i in range(NT)]
        first = [sum(blocks[:i]) for i in range(NT)]
        XL2 = V[:, 0:2 * TOK].rearrange("p (t d) -> p t d", d=D)
        XT2 = V[:, 2 * TOK:4 * TOK]
        MN = V[:, 2 * TOK:3 * TOK].rearrange("p (t e) -> p t e", e=2 * EX)
        LG, LR = Af[:, 0:TOK], Af[:, TOK:2 * TOK]
        W1B = V[:, 0:8192].rearrange("p (c e h) -> p c e h", c=4, e=EG)
        W2B = V[:, 8192:16384].rearrange("p (c e k o) -> p c e k o", c=4, e=EG, k=4)
        B1T = MI[:, 0:EX * 4].rearrange("p (e k) -> p e k", k=4)
        HB = WS[:, 2, :].rearrange("p (c x) -> p c x", c=2)
        HG = WS[:, 3, :].rearrange("p (c x) -> p c x", c=2)
        OT = WS[:, 4:6, :].rearrange("p k n -> p (k n)").rearrange("p (b e) -> p b e", b=B)
        GZ = WS[:, 6:8, :]
        MTB = Af[0:EX, 0:2 * TOK].rearrange("p (c t) -> p c t", c=2)
        NG = EX // EG

        def sync_l1(sp):
            for b2 in range(2):
                sp.dma_start(gb2[EX * b2:EX * b2 + EX], io["L1_ffn_gate_b"].unsqueeze(1)).then_inc(sem("l1w_in"), 16)
            sp.wait_ge(sem("l1_start"), 1)
            sp.dma_start(B1T, io["L1_ffn_weight1"][:, D, :].rearrange("e (p k) -> p e k", k=4)).then_inc(sem("b1_in"), 16)
            for q in range(2):
                sp.wait_ge(sem("gate_ready"), q + 1)
                sp.dma_start(m_dram[2 * q:2 * q + 2].rearrange("b e t -> (b e) t"), LG).then_inc(sem("m_out"), 16)
            sp.wait_ge(sem("pool_mm"), 2)
            for g in range(NG):
                if g >= 4:
                    sp.wait_ge(sem("e2_mm"), g - 3)
                e = slice(EG * g, EG * g + EG)
                sp.dma_start(W1B[:, g % 4], io["L1_ffn_weight1"][e, 0:D, :].rearrange("e d h -> d e h")).then_inc(sem(f"ew_in{g % 4}"), 16)
                sp.dma_start(W2B[:, g % 4].rearrange("p e k o -> p e (k o)"),
                             io["L1_ffn_weight2"][e, 0:HID, :].rearrange("e (p k) o -> p e (k o)", k=4)).then_inc(sem(f"ew_in{g % 4}"), 16)
            sp.wait_ge(sem("m_out"), 32)
            for b in range(B):
                if b >= 2:
                    sp.wait_ge(sem("fin_mm"), 8 * (b - 1))
                sp.dma_start(MTB[:, b % 2], m_dram[b]).then_inc(sem(f"mt_in{b % 2}"), 16)
                if b >= 1:
                    store(sp, b - 1)
            store(sp, B - 1)
            sp.wait_ge(sem("out_done"), 16 * 2 * B)

        def store(sp, b):
            for h in range(2):
                sp.wait_ge(sem("fin_ready"), 8 * b + 4 * h + 4)
                i = T * b + 16 * h
                sp.dma_start(out_nat[:, i:i + 16, :], U[:, i:i + 16, :]).then_inc(sem("out_done"), 16)

        def tensor_l1(pe):
            pe.wait_ge(sem("l1w_in"), 16 * 7)
            pe.wait_ge(sem("x1_ready"), 16)
            for i in range(3):
                pe.transpose(PS[:, 0, 128 * i:128 * i + 128], WN3[:, i, :], ident)
            pe.transpose(PS[:, 0, 384:384 + EX], gwn, ident[0:EX, 0:EX]).then_inc(sem("wt_mm"), 1)
            pe.wait_ge(sem("wt_ready"), 1)

            with pe.Fori(0, B) as b:
                pe.wait_ge(sem("tokens_ready"), b + 1)
                for g in range(32):
                    if g >= 4:
                        pe.wait_ge(sem(f"pre_ev{g % 2}"), b * 16 + (g - 4) // 2 + 1)
                    if g == 8:
                        pe.wait_ge(sem("pre_ev0"), b * 16 + 4)
                        pe.wait_ge(sem("pre_ev1"), b * 16 + 4)
                    o = PS[:, g % 4, :]
                    k = g % 8
                    if g < 8:
                        for j in range(4):
                            mm = pe.transpose(o[:, 128 * j:128 * j + 128], XO[:, 4 * k + j, :], ident)
                    elif g < 24:
                        mm = pe.matmul(o, WT3[:, g // 8 - 1, :], XT[:, 512 * k:512 * k + 512], start=True, stop=True)
                    else:
                        for j in range(4):
                            mm = pe.matmul(o[:, 128 * j:128 * j + 128], XT[:, 512 * k + 128 * j:512 * k + 128 * j + 128],
                                           WT3[:, 2, :], start=True, stop=True)
                    mm.then_inc(sem("pre_mm"), 1)
                pe.wait_ge(sem("pre_ev0"), b * 16 + 16)
                pe.wait_ge(sem("pre_ev1"), b * 16 + 16)

                def scores(i):
                    for j in range(blocks[i]):
                        c = first[i] + j
                        w = min(512, 128 * (i + 1) - 512 * j)
                        if c >= 3:
                            pe.wait_ge(sem("sc_ev"), b * CH + c - 2)
                        last = j == blocks[i] - 1
                        mm = pe.matmul(PS[:, c % 3, 0:w], QT[:, 128 * i:128 * i + 128], KT[:, 512 * j:512 * j + w], start=True, stop=not last)
                        if last:
                            mm = pe.matmul(PS[:, c % 3, w - 128:w], ident, cst["mask"], start=False, stop=True)
                        mm.then_inc(sem("sc_mm"), 1)

                def turn(i, j):
                    c = first[i] + j
                    if c >= 3:
                        pe.wait_ge(sem(f"t_ev{(c - 3) % 2}"), b * (CH // 2) + (c - 3) // 2 + 1)
                    for k in range(4 * j, min(4 * j + 4, i + 1)):
                        mm = pe.transpose(PS[:, 3 + c % 3, 128 * (k % 4):128 * (k % 4) + 128], SR[i % 2][:, 128 * k:128 * k + 128], ident)
                    mm.then_inc(sem("t_mm"), 1)

                def weigh(i, j):
                    c = first[i] + j
                    pe.wait_ge(sem(f"t_ev{c % 2}"), b * (CH // 2) + c // 2 + 1)
                    if j == 0 and i >= 2:
                        pe.wait_ge(sem("o_ev"), b * NT + i - 1)
                    for k in range(4 * j, min(4 * j + 4, i + 1)):
                        mm = pe.matmul(PS[:, 6 + i % 2, 0:128], PTB[:, c % 3, 128 * (k % 4):128 * (k % 4) + 128], VV[:, k, :],
                                       start=(k == 0), stop=(k == i))
                    mm.then_inc(sem("w_mm"), 1)

                scores(0)
                for i in range(NT):
                    if i + 1 < NT:
                        scores(i + 1)
                    pe.wait_ge(sem("exp_ready"), b * NT + i + 1)
                    turn(i, 0)
                    for j in range(blocks[i]):
                        if j + 1 < blocks[i]:
                            turn(i, j + 1)
                        weigh(i, j)

            for q in range(2):
                pe.wait_ge(sem("xl2_ready"), q + 1)
                for g in range(16):
                    n = 24 * q + g
                    if n >= 4:
                        pe.wait_ge(sem(f"g_ev{n % 2}"), (n - 4) // 2 + 1)
                    for j in range(4):
                        mm = pe.transpose(PS[:, n % 4, 128 * j:128 * j + 128], XL2[:, 4 * g + j, :], ident)
                    mm.then_inc(sem("g_mm"), 1)
                pe.wait_ge(sem("g_ev0"), 12 * q + 8)
                pe.wait_ge(sem("g_ev1"), 12 * q + 8)
                for g in range(8):
                    if g >= 2:
                        pe.wait_ge(sem("lg_ev"), 8 * q + g - 1)
                    pe.matmul(PS[:, 4 + g % 2, :], GZ[:, 0, :], XT2[:, 512 * g:512 * g + 512], start=True, stop=False)
                    pe.matmul(PS[:, 4 + g % 2, :], GZ[:, 1, :], XT2[:, TOK + 512 * g:TOK + 512 * g + 512],
                              start=False, stop=True).then_inc(sem("lg_mm"), 1)
                pe.wait_ge(sem("gate_ready"), q + 1)
                for g in range(8):
                    n = 24 * q + 16 + g
                    pe.wait_ge(sem(f"g_ev{n % 2}"), (n - 4) // 2 + 1)
                    for j in range(4):
                        mm = pe.transpose(PS[:, n % 4, 128 * j:128 * j + 128], LG[:, 512 * g + 128 * j:512 * g + 128 * j + 128], ident)
                    mm.then_inc(sem("g_mm"), 1)
                pe.wait_ge(sem("g_ev0"), 12 * q + 12)
                pe.wait_ge(sem("g_ev1"), 12 * q + 12)
                for b2 in range(2):
                    for t in range(NT):
                        mm = pe.matmul(PS[:, 6, 128 * q + 64 * b2:128 * q + 64 * b2 + 64], XL2[:, NT * b2 + t, :],
                                       MN[:, t, 64 * b2:64 * b2 + 64], start=(t == 0), stop=(t == NT - 1))
                mm.then_inc(sem("pool_mm"), 1)
                pe.wait_ge(sem("pool_ev"), q + 1)

            def hidden(g):
                pe.wait_ge(sem(f"ew_in{g % 4}"), 32 * (g // 4 + 1))
                if g >= 2:
                    pe.wait_ge(sem("h_ev"), g - 1)
                for e in range(EG):
                    for k in range(4):
                        mm = pe.matmul(PS[:, g % 2, 16 * e + 4 * k:16 * e + 4 * k + 4], W1B[:, g % 4, e, k:HID:4],
                                       poolT[:, :, EG * g + e], start=True, stop=True)
                mm.then_inc(sem("e1_mm"), 1)

            def result(g):
                pe.wait_ge(sem("hg_ready"), g + 1)
                if g >= 2:
                    pe.wait_ge(sem("ot_ev"), g - 1)
                for e in range(EG):
                    for k in range(4):
                        mm = pe.matmul(PS[:, 2 + g % 2, 4 * e:4 * e + 4], W2B[:, g % 4, e, k, :], HG[:, g % 2, 16 * e + 4 * k:16 * e + 4 * k + 4],
                                       start=(k == 0), stop=(k == 3))
                mm.then_inc(sem("e2_mm"), 1)

            hidden(0)
            for g in range(NG):
                if g + 1 < NG:
                    hidden(g + 1)
                result(g)
            pe.wait_ge(sem("ot_ev"), NG)
            for b in range(B):
                mm = pe.transpose(PS[0:EX, 7, 128 * b:128 * b + 128], OT[:, b, :], ident)
            mm.then_inc(sem("oe_mm"), 1)
            pe.wait_ge(sem("oe_ready"), 1)
            for g in range(8 * B):
                b = g // 8
                if g % 8 == 0:
                    pe.wait_ge(sem(f"mt_in{b % 2}"), 16 * (b // 2 + 1))
                if g >= 4:
                    pe.wait_ge(sem("fin_ready"), g - 3)
                for j in range(4):
                    mm = pe.matmul(PS[:, g % 4, 128 * j:128 * j + 128], MTB[:, b % 2, 512 * (g % 8) + 128 * j:512 * (g % 8) + 128 * j + 128],
                                   outE[:, b, :], start=True, stop=True)
                mm.then_inc(sem("fin_mm"), 1)

        def scalar_l1(act):
            def root8():
                act.wait_ge(sem("var_ready"), 8 + root8.n)
                act.activation(WS[:, 3, :], WS[:, 3, :], ACT.Sqrt).then_inc(sem("root_ready"), 1)
                root8.n += 1
            root8.n = 0
            root8()
            with act.Fori(0, B) as b:
                for g in range(1, 32, 2):
                    k = g % 8
                    act.wait_ge(sem("pre_mm"), b * 32 + g + 1)
                    dst = (XT, QT, KT, V[:, 2 * TOK:3 * TOK])[g // 8][:, 512 * k:512 * k + 512]
                    act.activation(dst, PS[:, g % 4, :], ACT.Copy).then_inc(sem("pre_ev1"), 1)
                for i in range(NT):
                    act.wait_ge(sem("nm_ready"), b * NT + i + 1)
                    s = SR[i % 2][:, 0:128 * (i + 1)]
                    act.activation(s, s, ACT.Exp, scale=SCALE, bias=nmax[:, i % 2:i % 2 + 1],
                                   accum_out=rsum[:, i % 2:i % 2 + 1]).then_inc(sem("exp_ready"), 1)
                    for c in range(first[i], first[i] + blocks[i]):
                        if c % 2:
                            w = min(512, 128 * (i + 1) - 512 * (c - first[i]))
                            act.wait_ge(sem("t_mm"), b * CH + c + 1)
                            if c >= 3:
                                act.wait_ge(sem("w_mm"), b * CH + c - 2)
                            act.activation(PTB[:, c % 3, 0:w], PS[:, 3 + c % 3, 0:w], ACT.Copy).then_inc(sem("t_ev1"), 1)
            root8()
            for q in range(2):
                for g in range(1, 16, 2):
                    act.wait_ge(sem("g_mm"), 24 * q + g + 1)
                    act.activation(XT2[:, 512 * g:512 * g + 512], PS[:, g % 4, :], ACT.Copy).then_inc(sem("g_ev1"), 1)
                act.wait_ge(sem("gm_ready"), q + 1)
                act.activation(LG, LG, ACT.Exp, bias=gmx[:, 0:1], accum_out=gmx[:, 1:2]).then_inc(sem("gexp_ready"), 1)
                for g in range(1, 8, 2):
                    act.wait_ge(sem("g_mm"), 24 * q + 16 + g + 1)
                    act.activation(V[:, 2 * TOK + 512 * g:2 * TOK + 512 * g + 512], PS[:, g % 4, :], ACT.Copy).then_inc(sem("g_ev1"), 1)
            for g in range(NG):
                act.wait_ge(sem("h_ev"), g + 1)
                if g >= 2:
                    act.wait_ge(sem("e2_mm"), g - 1)
                act.activation(HG[:, g % 2, :], HB[:, g % 2, :], ACT.Gelu).then_inc(sem("hg_ready"), 1)

        def vector_l1(dve, st, image_stats, row_moments):
            later = st.later

            def token_norm(ready):
                row_moments()
                m, e, v = WS[:, 0, :], WS[:, 1, :], WS[:, 3, :]
                later(dve.tensor_tensor(v, m, m, ALU.mult))
                later(dve.tensor_tensor(v, e, v, ALU.subtract))
                dve.tensor_scalar(v, v, EPS, None, ALU.add).then_inc(sem("var_ready"), 1)
                dve.wait_ge(sem("root_ready"), ready)
                later(dve.reciprocal(tkr, v))
                later(dve.scalar_tensor_tensor(tkn, m, -1.0, tkr, ALU.mult, ALU.mult))

            for k in range(NIM):
                if k % 2 == 0:
                    dve.wait_ge(sem("x1_ready"), k // 2 + 1)
                ins = image_stats(U, k)
            later(ins)
            token_norm(8)
            dve.wait_ge(sem("wt_mm"), 1)
            dve.tensor_copy(WT3.rearrange("p c h -> p (c h)"), PS[:, 0, 0:384])
            later(dve.memset(GZ, 0.0))
            dve.tensor_copy(GZ[:, 0, 0:EX], PS[:, 0, 384:384 + EX])
            dve.tensor_copy(GZ[:, 1, EX:2 * EX], PS[:, 0, 384:384 + EX]).then_inc(sem("wt_ready"), 1)
            tick = lay[:, 0:1]
            later(dve.memset(tick, 0.0))
            dve.memset(tick, 0.0).then_inc(sem("l1_start"), 1)

            base = st.n
            with dve.Fori(0, B) as b:
                tiles = bass.ts(b, NT)
                dve.tensor_tensor(XO, U[:, tiles, :], tkr[:, tiles].unsqueeze(2).broadcast_to([128, NT, D]), ALU.mult).then_inc(sem("tokens_scaled"), 1)
                dve.wait_ge(sem("tokens_scaled"), b + 1)
                dve.memset(tick, 0.0)
                dve.tensor_tensor(XO, XO, tkn[:, tiles].unsqueeze(2).broadcast_to([128, NT, D]), ALU.add).then_inc(sem("tokens_ready"), 1)
                for g in range(0, 32, 2):
                    k = g % 8
                    dve.wait_ge(sem("pre_mm"), b * 32 + g + 1)
                    dst = (XT, QT, KT, V[:, 2 * TOK:3 * TOK])[g // 8][:, 512 * k:512 * k + 512]
                    dve.tensor_copy(dst, PS[:, g % 4, :]).then_inc(sem("pre_ev0"), 1)

                def take_scores(i):
                    for j in range(blocks[i]):
                        c = first[i] + j
                        w = min(512, 128 * (i + 1) - 512 * j)
                        dve.wait_ge(sem("sc_mm"), b * CH + c + 1)
                        if i >= 2 and j == 0:
                            dve.wait_ge(sem("t_mm"), b * CH + first[i - 1])
                        dve.tensor_scalar(SR[i % 2][:, 512 * j:512 * j + w], PS[:, c % 3, 0:w], 1.0, -3e38, ALU.mult, ALU.max,
                                          accum_out=bmax[:, 8 * (i % 2) + j:8 * (i % 2) + j + 1]).then_inc(sem("sc_ev"), 1)
                    dve.wait_ge(sem("sc_ev"), b * CH + first[i] + blocks[i])
                    dve.tensor_reduce(mraw[:, i % 2:i % 2 + 1], bmax[:, 8 * (i % 2):8 * (i % 2) + blocks[i]], AX.X, ALU.max).then_inc(sem("mr_ready"), 1)
                    dve.wait_ge(sem("mr_ready"), b * NT + i + 1)
                    dve.tensor_scalar(nmax[:, i % 2:i % 2 + 1], mraw[:, i % 2:i % 2 + 1], -SCALE, None, ALU.mult).then_inc(sem("nm_ready"), 1)

                def finish(i):
                    dve.reciprocal(rden[:, i % 2:i % 2 + 1], rsum[:, i % 2:i % 2 + 1]).then_inc(sem("rd_ready"), 1)
                    dve.wait_ge(sem("rd_ready"), b * NT + i + 1)
                    dve.wait_ge(sem("w_mm"), b * CH + first[i] + blocks[i])
                    dve.tensor_scalar(XO[:, i, :], PS[:, 6 + i % 2, 0:128], rden[:, i % 2:i % 2 + 1], None, ALU.mult).then_inc(sem("o_ev"), 1)

                take_scores(0)
                for i in range(NT):
                    if i + 1 < NT:
                        take_scores(i + 1)
                    dve.wait_ge(sem("exp_ready"), b * NT + i + 1)
                    for c in range(first[i], first[i] + blocks[i]):
                        if c % 2 == 0:
                            w = min(512, 128 * (i + 1) - 512 * (c - first[i]))
                            dve.wait_ge(sem("t_mm"), b * CH + c + 1)
                            if c >= 3:
                                dve.wait_ge(sem("w_mm"), b * CH + c - 2)
                            dve.tensor_copy(PTB[:, c % 3, 0:w], PS[:, 3 + c % 3, 0:w]).then_inc(sem("t_ev0"), 1)
                    finish(i)
                dve.wait_ge(sem("o_ev"), b * NT + NT)
                dve.memset(tick, 0.0)
                dve.tensor_tensor(U[:, tiles, :], U[:, tiles, :], XO, ALU.add).then_inc(sem("t2_ready"), 1)
                dve.wait_ge(sem("t2_ready"), b + 1)
                dve.memset(tick, 0.0)

            for k in range(NIM):
                ins = image_stats(U, k)
            later(ins)
            token_norm(9)
            for q in range(2):
                tiles = slice(2 * NT * q, 2 * NT * q + 2 * NT)
                later(dve.tensor_tensor(XL2, U[:, tiles, :], tkr[:, tiles].unsqueeze(2).broadcast_to([128, 2 * NT, D]), ALU.mult))
                dve.tensor_tensor(XL2, XL2, tkn[:, tiles].unsqueeze(2).broadcast_to([128, 2 * NT, D]), ALU.add).then_inc(sem("xl2_ready"), 1)
                for g in range(0, 16, 2):
                    dve.wait_ge(sem("g_mm"), 24 * q + g + 1)
                    dve.tensor_copy(XT2[:, 512 * g:512 * g + 512], PS[:, g % 4, :]).then_inc(sem("g_ev0"), 1)
                if q:
                    dve.wait_ge(sem("m_out"), 16)
                for g in range(8):
                    dve.wait_ge(sem("lg_mm"), 8 * q + g + 1)
                    dve.tensor_scalar(LG[:, 512 * g:512 * g + 512], PS[:, 4 + g % 2, :], gb2, -3e38, ALU.add, ALU.max,
                                      accum_out=bmax[:, g:g + 1]).then_inc(sem("lg_ev"), 1)
                dve.wait_ge(sem("lg_ev"), 8 * q + 8)
                later(dve.tensor_reduce(gmx[:, 0:1], bmax[:, 0:8], AX.X, ALU.max))
                dve.tensor_scalar(gmx[:, 0:1], gmx[:, 0:1], -1.0, None, ALU.mult).then_inc(sem("gm_ready"), 1)
                dve.wait_ge(sem("gexp_ready"), q + 1)
                later(dve.reciprocal(gmx[:, 2:3], gmx[:, 1:2]))
                later(dve.tensor_scalar(LG, LG, gmx[:, 2:3], None, ALU.mult))
                later(dve.max(top8, LG))
                later(dve.match_replace(LR, top8, LG, 0.0))
                dve.tensor_tensor(LG, LG, LR, ALU.subtract).then_inc(sem("gate_ready"), 1)
                for g in range(0, 8, 2):
                    dve.wait_ge(sem("g_mm"), 24 * q + 16 + g + 1)
                    dve.tensor_copy(V[:, 2 * TOK + 512 * g:2 * TOK + 512 * g + 512], PS[:, g % 4, :]).then_inc(sem("g_ev0"), 1)
                dve.wait_ge(sem("pool_mm"), q + 1)
                dve.tensor_copy(poolT[:, 2 * q:2 * q + 2, :].rearrange("p b e -> p (b e)"), PS[:, 6, 128 * q:128 * q + 128]).then_inc(sem("pool_ev"), 1)
            dve.wait_ge(sem("b1_in"), 16)

            def take_result(g):
                dve.wait_ge(sem("e2_mm"), g + 1)
                dve.tensor_copy(OT[:, :, EG * g:EG * g + EG], PS[:, 2 + g % 2, 0:16].rearrange("p (e b) -> p b e", b=B)).then_inc(sem("ot_ev"), 1)

            for g in range(NG):
                dve.wait_ge(sem("e1_mm"), g + 1)
                if g >= 2:
                    dve.wait_ge(sem("hg_ready"), g - 1)
                dve.tensor_tensor(HB[:, g % 2, :].rearrange("p (x b) -> p x b", b=B), PS[:, g % 2, 0:64].rearrange("p (x b) -> p x b", b=B),
                                  B1T[:, EG * g:EG * g + EG, :].rearrange("p e k -> p (e k)").unsqueeze(2).broadcast_to([128, 16, B]),
                                  ALU.add).then_inc(sem("h_ev"), 1)
                if g >= 1:
                    take_result(g - 1)
            take_result(NG - 1)
            dve.wait_ge(sem("oe_mm"), 1)
            dve.tensor_tensor(outE, PS[0:EX, 7, :].rearrange("p (b o) -> p b o", b=B), b2n.unsqueeze(1).broadcast_to([EX, B, D]),
                              ALU.add).then_inc(sem("oe_ready"), 1)
            for g in range(8 * B):
                dve.wait_ge(sem("fin_mm"), g + 1)
                u = U[:, 4 * g:4 * g + 4, :]
                dve.tensor_tensor(u, u, PS[:, g % 4, :].rearrange("p (n w) -> p n w", w=W), ALU.add).then_inc(sem("fin_ready"), 1)

        def value_products(eng, k, bs, done):
            r = k // NQ
            nb = bs.stop - bs.start
            eng.wait_ge(sem(f"e_in{k % 3}"), 16 * (k // 3 + 1))
            if k % NQ == 0:
                eng.wait_ge(sem(f"xr_modes{r % 2}"), 64 * (r // 2 + 1))
            if k >= 2:
                eng.wait_ge(sem("v_mm"), k - 1)
            eng.tensor_tensor(YB[:, k % 2, bs].rearrange("p b k m -> p b (k m)"), XR[:, r % 2, bs].rearrange("p b k m -> p b (k m)"),
                              EB[:, k % 3].rearrange("p k m -> p (k m)").unsqueeze(1).broadcast_to([128, nb, 3 * MR]),
                              ALU.mult).then_inc(sem(done), 1)

        def score_products(eng, z):
            h, k = z // (4 * NLC), z // 4 % NLC
            xc, wc = ((0, 0), (1, 1), (1, 0), (0, 2))[z % 4]
            w = min(128, ML - 128 * k)
            if z >= 4:
                eng.wait_ge(sem("s_mm"), z - 3)
            eng.tensor_tensor(ZP[z % 4][0:w], XLT[0:w, xc, k, :].unsqueeze(1).broadcast_to([w, 16, N]),
                              CT[0:w, wc, k, 16 * h:16 * h + 16].unsqueeze(2).broadcast_to([w, 16, N]),
                              ALU.mult).then_inc(sem("zp_pool" if z % 4 == 3 else "zp_dve"), 1)

        def emptied(eng, what, g, rounds=0, groups=0):
            eng.wait_ge(sem(f"{what}{g % 2}"), rounds * ((groups + 1 - g % 2) // 2) + g // 2 + 1)

        def all_emptied(eng, what, rounds, groups):
            eng.wait_ge(sem(f"{what}0"), rounds * ((groups + 1) // 2))
            eng.wait_ge(sem(f"{what}1"), rounds * (groups // 2))

        def forward_evacs(eng, layer, mmsem, scale):
            odd = eng.engine == nc.scalar.engine
            for g in range(int(odd), NF2, 2):
                eng.wait_ge(sem(mmsem), max(layer - 1, 0) * NF2 + g + 1)
                n = 3 if g < NF2 - 1 else 2
                j0 = 1 if g == 0 else 0
                lo = 64 - (3 * g + 2)
                src = PS[:, g % 4, 0:396].rearrange("p (j s c x) -> p s c j x", j=3, s=2, c=2)
                for c in range(2):
                    for o, i in ((Zk[:, c, 3 * g:3 * g + n, :], src[:, 0, c, 0:n, :]),
                                 (Zk[:, c, lo:lo + 3 - j0, :], src[:, 1, c, 2:(0 if j0 else None):-1, :])):
                        if odd:
                            ins = nc.scalar.activation(o, i, ACT.Identity, scale=scale)
                        else:
                            ins = nc.vector.tensor_scalar(o, i, scale, None, ALU.mult)
                ins.then_inc(sem(f"f2_ev{int(odd)}"), 1)

        block = ctx.enter_context(nc.Block())

        @block.sync
        def _(sp):
            sp.dma_start(CST[:], io["consts"]).then_inc(sem("consts_in"), 16)
            for i in range(3):
                sp.dma_start(XN[:, i], x_nat[:, 8 * i:8 * i + 8, :]).then_inc(sem(f"xn_in{i}"), 16)
            sp.dma_start(V[0:NH, 0:2 * M], io["L0_conv_Pcw"].rearrange("n o k x c -> n (o k x c)")).then_inc(sem("w_in"), 16)
            for i, n in enumerate("QKV"):
                sp.dma_start(V[0:NH, 4224 + 1088 * i:4224 + 1088 * (i + 1)],
                             io[f"L0_conv_{n}cw"].rearrange("o n k x c -> n (o k x c)")).then_inc(sem("w_in"), 16)
            for i, n in enumerate("KQPV"):
                col = io[f"L0_conv_{n}sw"].rearrange("a n -> n a") if n == "P" else io[f"L0_conv_{n}sw"]
                row = io[f"L0_conv_{n}sw"] if n == "P" else io[f"L0_conv_{n}sw"].rearrange("n a -> a n")
                sp.dma_start(headc[0:NH, i:i + 1], col).then_inc(sem("w_in"), 16)
                sp.dma_start(headw[:, i, :], row.broadcast_to([128, NH])).then_inc(sem("w_in"), 16)
            for i, n in enumerate(PAR):
                src = io[f"L0_conv_{n}"]
                src = src if n.startswith("m") and n.endswith("sw") else src.unsqueeze(0)
                sp.dma_start(PAR[n], src.broadcast_to([128, 1])).then_inc(sem("w_in"), 16)
            for c in range(3, 16):
                sp.wait_ge(sem("f1_mm"), 2 * (c - 2))
                sp.wait_ge(sem("xsq"), c - 2)
                sp.dma_start(XN[:, c % 3], x_nat[:, 8 * c:8 * c + 8, :]).then_inc(sem(f"xn_in{c % 3}"), 16)
            sp.wait_ge(sem("e_ready"), 1)
            for q in range(3):
                sp.dma_start(e_dram[:, :, q, :].rearrange("r n m -> n r m"), P3[:, q, :].rearrange("p (r m) -> p r m", m=MR)
                             ).then_inc(sem("e_out"), 16)
            sp.wait_ge(sem("e_out"), 48)
            sp.wait_ge(sem("ct_mm"), 1)
            for i in range(4):
                sp.dma_start(V[:, 4096 * i:4096 * (i + 1)], x_img[:, 4096 * i:4096 * (i + 1)]).then_inc(sem(f"xi_in{i}"), 16)
            sp.wait_ge(sem("xs_ready"), 1)
            for q, src in enumerate((XS, Z[:, 0, :], Z[:, 1, :])):
                sp.dma_start(x_dram[:, :, q, :].rearrange("r n m -> n r m"), src.rearrange("p (r m) -> p r m", m=MR)
                             ).then_inc(sem("x_out"), 16)
            sp.wait_ge(sem("x_out"), 48)

            def load_modes(r):
                if r >= 2:
                    sp.wait_ge(sem("y_dve"), NQ * (r - 1))
                    sp.wait_ge(sem("y_pool"), NQ * (r - 1))
                for n in range(4):
                    sp.dma_start(XR[32 * n:32 * n + 32, r % 2].rearrange("p b k m -> p b (k m)"), x_dram[r].rearrange("(b s) k m -> s b (k m)", b=B)
                                 ).then_inc(sem(f"xr_modes{r % 2}"), 16)

            load_modes(0)
            load_modes(1)
            sp.wait_ge(sem("pbar_ready"), 1)
            for k in range(NR * NQ):
                r, g = divmod(k, NQ)
                if k >= 3:
                    sp.wait_ge(sem("y_dve"), k - 2)
                    sp.wait_ge(sem("y_pool"), k - 2)
                sp.dma_start(EB[:, k % 3].rearrange("p k m -> p (k m)"),
                             e_dram[r, 4 * g:4 * g + 4].rearrange("n k m -> n (k m)").unsqueeze(1).broadcast_to([4, 32, 3 * MR])
                             ).then_inc(sem(f"e_in{k % 3}"), 16)
                if g == 2 and 1 <= r < NR - 1:
                    load_modes(r + 1)
            for i, n in enumerate(("m0cw", "m1cw")):
                sp.wait_ge(sem("f2_mm_m"), NF2 * (i + 1))
                sp.dma_start(Af[:, 0:2 * M], io[f"L0_conv_{n}"].rearrange("a b k x c -> (a b) (k x c)")
                             .broadcast_to([128, 2 * M])).then_inc(sem("mw_in"), 16)
            sp.wait_ge(sem("tr_mm"), 3 * NTR)
            for k in range(16):
                if k >= 3:
                    sp.wait_ge(sem("x1_ready"), k - 2)
                sp.dma_start(AF[1][:, 1024 * (k % 3):1024 * (k % 3 + 1)].rearrange("p (i w) -> p i w", w=W),
                             x_nat[:, 8 * k:8 * k + 8, :]).then_inc(sem(f"xr_in{k % 3}"), 16)
            sp.wait_ge(sem("x1_ready"), 16)
            for i, n in enumerate("qkv"):
                sp.dma_start(WN3[:, i, :], io[f"L1_attn_W{n}"]).then_inc(sem("l1w_in"), 16)
            sp.dma_start(gwn, io["L1_ffn_gate_w"]).then_inc(sem("l1w_in"), 16)
            sp.dma_start(b2n, io["L1_ffn_weight2"][:, HID, :]).then_inc(sem("l1w_in"), 16)
            sync_l1(sp)

        @block.gpsimd
        def _(pool):
            pool.wait_ge(sem("rim_ready"), 1)
            rb = rim.unsqueeze(1).broadcast_to([128, 32, 128])
            cb = cim.unsqueeze(1).broadcast_to([128, 32, 128])
            for i in range(4):
                v = V[:, 4096 * i:4096 * (i + 1)].rearrange("p (h w) -> p h w", w=W)
                pool.wait_ge(sem(f"xi_in{i}"), 16)
                pool.tensor_tensor(v, v, rb, ALU.mult).then_inc(sem("xg_scaled"), 1)
                pool.wait_ge(sem("xg_scaled"), i + 1)
                pool.tensor_tensor(v, v, cb, ALU.add).then_inc(sem("xg_ready"), 1)
            pool.wait_ge(sem("xlt_ev"), 1)
            pool.wait_ge(sem("ct_ready"), 1)
            pool.wait_ge(sem("gram_mm"), 1)
            for z in range(3, 8 * NLC, 4):
                score_products(pool, z)
            for k in range(NR * NQ):
                value_products(pool, k, slice(B - 1, B), "y_pool")
            for k in range(16):
                pool.wait_ge(sem(f"xr_in{k % 3}"), 16 * (k // 3 + 1))
                pool.wait_ge(sem("o_ready"), 8 * (k + 1))
                u = U[:, 8 * k:8 * k + 8, :]
                pool.tensor_tensor(u, u, AF[1][:, 1024 * (k % 3):1024 * (k % 3 + 1)].rearrange("p (i w) -> p i w", w=W),
                                   ALU.add).then_inc(sem("x1_ready"), 1)

        @block.tensor
        def _(pe):
            pe.wait_ge(sem("consts_in"), 16)

            def half_forward(layer, k, src, bank_evac):
                if k >= 4:
                    pe.wait_ge(sem(bank_evac), k - 3 + 32 * layer)
                for j in range(4):
                    mm = pe.matmul(PS[:, k % 4, 66 * j:66 * j + 66], src(j), cst["fh"], start=True, stop=True)
                mm.then_inc(sem("f1_mm"), 1)

            def forward(layer, mmsem):
                pe.wait_ge(sem("a_ready"), layer + 1)
                for g in range(NF2):
                    if g >= 4:
                        emptied(pe, "f2_ev", g - 4, layer, NF2)
                    for j in range(3):
                        ky = 3 * g + j
                        o = PS[:, g % 4, 132 * j:132 * j + 132]
                        pe.matmul(o, A[:, :, ky], cst["fwr"], start=True, stop=False)
                        mm = pe.matmul(o, A[:, :, KX + ky], cst["fwi"], start=False, stop=True)
                    mm.then_inc(sem(mmsem), 1)

            def inverse(layer):
                pe.wait_ge(sem("z_ready"), layer + 1)
                for g in range(NTR):
                    if g >= 4:
                        emptied(pe, "tr_ev", g - 4, layer, NTR)
                    for i in range(4 * g, min(4 * g + 4, 2 * KX)):
                        c, kx = divmod(i, KX)
                        mm = pe.matmul(PS[:, g % 4, 128 * (i % 4):128 * (i % 4) + 128], Zk[:, c:c + 2, :, kx], ident,
                                       is_transpose=True, start=True, stop=True)
                    mm.then_inc(sem("tr_mm"), 1)
                all_emptied(pe, "tr_ev", layer + 1, NTR)

                def rows(k):
                    if k >= 2:
                        pe.wait_ge(sem("i1_ev"), 32 * layer + k - 1)
                    for j in range(4):
                        mm = pe.matmul(PS[0:66, 4 + k % 2, 128 * j:128 * j + 128], A_modes[:, :, 4 * k + j], cst["ih"],
                                       start=True, stop=True)
                    mm.then_inc(sem("i1_mm"), 1)

                def columns(k):
                    pe.wait_ge(sem("i1_ev"), 32 * layer + k + 1)
                    if k >= 2:
                        pe.wait_ge(sem("i2_ev"), 32 * layer + k - 1)
                    for j in range(4):
                        mm = pe.matmul(PS[:, 6 + k % 2, 128 * j:128 * j + 128], DB[0:66, k % 3, 128 * j:128 * j + 128],
                                       cst["iw"][0:66, :], start=True, stop=True)
                    mm.then_inc(sem("i2_mm"), 1)

                rows(0)
                for k in range(NIM):
                    if k + 1 < NIM:
                        rows(k + 1)
                    columns(k)

            A_modes = Af.rearrange("p (c n) -> p c n", n=N)

            for c in range(16):
                pe.wait_ge(sem(f"xn_in{c % 3}"), 16 * (c // 3 + 1))
                for q in range(2):
                    half_forward(0, 2 * c + q, lambda j: XN[:, c % 3, 4 * q + j, :], "f1_ev")
                pe.wait_ge(sem("xsq"), c + 1)
                for j in range(8):
                    mm = pe.matmul(PS[:, 4, 8 * c + j:8 * c + j + 1], XQ[:, c % 2, j, :], ones[:, 0:1], start=True, stop=True)
                mm.then_inc(sem("sq_mm"), 1)
            pe.wait_ge(sem("c_ready"), 1)
            for c, src in enumerate((CR, CI)):
                for k in range(NLC):
                    w = min(128, ML - 128 * k)
                    mm = pe.transpose(PS[0:w, 5, 160 * c + 32 * k:160 * c + 32 * k + 32], src[:, 128 * k:128 * k + w], ident[0:NH, 0:NH])
            mm.then_inc(sem("ct_mm"), 1)
            pe.wait_ge(sem("g8_ready"), 1)
            pe.matmul(PS[:, 6, 0:8], cst["group"], G8, start=True, stop=True).then_inc(sem("g8_mm"), 1)
            pe.wait_ge(sem("rc_ready"), 1)
            pe.matmul(PS[:, 6, 16:17], SG[:, 4, :], ones[:, 0:1], start=True, stop=True)
            pe.matmul(PS[:, 6, 17:18], SG[:, 5, :], ones[:, 0:1], start=True, stop=True)
            pe.transpose(PS[:, 7, 0:128], SG[:, 6, :], ident)
            pe.transpose(PS[:, 7, 128:256], SG[:, 7, :], ident).then_inc(sem("is_mm"), 1)
            forward(0, "f2_mm_x")
            pe.wait_ge(sem("xe_ready"), 1)
            for g in range(9):
                if g >= 3:
                    pe.wait_ge(sem("xet_ev"), g - 2)
                for k in range(4 * g, min(4 * g + 4, 33)):
                    mm = pe.transpose(PS[:, g % 3, 128 * (k % 4):128 * (k % 4) + 128], Uf[:, 128 * k:128 * k + 128], ident)
                mm.then_inc(sem("xet_mm"), 1)
            pe.wait_ge(sem("xl_ready"), 1)
            pe.wait_ge(sem("rim_ready"), 1)
            for c in range(2):
                for k in range(NLC):
                    w = min(128, ML - 128 * k)
                    mm = pe.transpose(PS[0:w, (3, 4, 7)[(5 * c + k) // 4], 128 * ((5 * c + k) % 4):128 * ((5 * c + k) % 4) + 128],
                                      XL[:, c, 128 * k:128 * k + w], ident)
            mm.then_inc(sem("xlt_mm"), 1)
            pe.wait_ge(sem("xet_ev"), 9)
            for k in range(33):
                mm = pe.matmul(PS[:, 6, 0:128], XET[:, k, :], XET[:, k, :], start=(k == 0), stop=(k == 32))
            mm.then_inc(sem("gram_mm"), 1)
            pe.wait_ge(sem("xlt_ev"), 1)
            for z in range(8 * NLC):
                h, k, c = z // (4 * NLC), z // 4 % NLC, z % 4
                w = min(128, ML - 128 * k)
                pe.wait_ge(sem("zp_pool" if z % 4 == 3 else "zp_dve"), z // 4 + 1 if z % 4 == 3 else z - z // 4 + 1)
                for b in range(B):
                    s = slice(32 * b, 32 * b + 32)
                    mm = pe.matmul(PS[s, h, :], XLT[0:w, c // 2, k, s], ZP[z % 4][0:w, :, s],
                                   start=(k == 0 and c == 0), stop=(k == NLC - 1 and c == 3))
                mm.then_inc(sem("s_mm"), 1)
            pe.wait_ge(sem("p_ready"), 1)
            for g in range(NQ):
                mm = pe.transpose(PS[:, 2 + g // 4, 128 * (g % 4):128 * (g % 4) + 128],
                                  SE[:, 4 * g:4 * g + 4, :].rearrange("p n s -> p (n s)"), ident)
            mm.then_inc(sem("pt_mm"), 1)
            pe.wait_ge(sem("pb_ready"), 1)
            pe.transpose(PS[:, 6, 0:128], SG2, ident).then_inc(sem("mix_mm"), 1)
            pe.wait_ge(sem("pbt_ready"), 1)
            pe.matmul(PS[:, 7, 0:1], Pbt, beta, start=True, stop=True).then_inc(sem("mix_mm"), 1)
            pe.wait_ge(sem("pt_ev"), 2)
            for k in range(NR * NQ):
                r, g = divmod(k, NQ)
                if g == 0 and r >= 2:
                    pe.wait_ge(sem("zv_ev"), r - 1)
                pe.wait_ge(sem("y_dve"), k + 1)
                pe.wait_ge(sem("y_pool"), k + 1)
                for q in range(3):
                    for b in range(B):
                        s = slice(32 * b, 32 * b + 32)
                        mm = pe.matmul(PS[s, 3 * (r % 2) + q, 0:MR], PT[:, g, s], YB[:, k % 2, b, q, :],
                                       start=(g == 0), stop=(g == NQ - 1))
                mm.then_inc(sem("v_mm"), 1)
            pe.wait_ge(sem("mt_ready"), 1)
            pe.wait_ge(sem("xg_ready"), 4)
            xg = V[:].rearrange("p (h w) -> p h w", w=W)
            for g in range(32):
                if g >= 4:
                    emptied(pe, "mx_ev", g - 4)
                elif g == 0:
                    pe.wait_ge(sem("zv_ev"), NR)
                for j in range(4):
                    mm = pe.matmul(PS[:, g % 4, 128 * j:128 * j + 128], xg[:, :, 4 * g + j], Mt, start=True, stop=True)
                mm.then_inc(sem("mx_mm"), 1)
            all_emptied(pe, "mx_ev", 1, 32)
            inverse(0)
            pe.wait_ge(sem("mv_ready"), 1)
            pe.wait_ge(sem("i2_ev"), 32)
            pe.matmul(PS[:, 7, 0:256], ones, MV, start=True, stop=True).then_inc(sem("mv_mm"), 1)
            for layer in (1, 2):
                for k in range(32):
                    pe.wait_ge(sem("src_ready"), 32 * (layer - 1) + k + 1)
                    half_forward(layer, k, lambda j: Vn[:, 4 * k + j, :], "f1_ev")
                forward(layer, "f2_mm_m")
                inverse(layer)
            pe.wait_ge(sem("mv_ready"), 2)
            pe.matmul(PS[:, 0, 0:256], ones, MV, start=True, stop=True).then_inc(sem("mv_mm"), 1)
            tensor_l1(pe)


        @block.scalar
        def _(act):
            st = Steps(act, sem("act_step"))

            def root():
                root.n += 1
                act.wait_ge(sem("var_ready"), root.n)
                v = root_args[root.n - 1]
                act.activation(v, v, ACT.Sqrt).then_inc(sem("root_ready"), 1)
            root.n = 0

            for c in range(16):
                act.wait_ge(sem(f"xn_in{c % 3}"), 16 * (c // 3 + 1))
                if c >= 2:
                    act.wait_ge(sem("sq_mm"), c - 1)
                act.activation(XQ[:, c % 2], XN[:, c % 3], ACT.Square).then_inc(sem("xsq"), 1)
            root()
            root()

            act.wait_ge(sem("alpha_ready"), 1)
            forward_evacs(act, 0, "f2_mm_x", alpha)
            act.wait_ge(sem("x_beta"), 1)
            act.activation(XE, Z[:, 0:2, :], ACT.Copy, scale=float(np.sqrt(2.0))).then_inc(sem("xe_scaled"), 1)
            for g in range(9):
                act.wait_ge(sem("xet_mm"), g + 1)
                w = 512 if g < 8 else 128
                act.activation(Uf[:, 5376 + 512 * g:5376 + 512 * g + w], PS[:, g % 3, 0:w], ACT.Copy).then_inc(sem("xet_ev"), 1)
            act.wait_ge(sem("sd_ready"), 1)
            act.activation(SE, SD, ACT.Exp).then_inc(sem("se_ready"), 1)
            act.wait_ge(sem("pt_mm"), 1)
            for h in range(2):
                act.activation(PT[:, 4 * h:4 * h + 4, :].rearrange("p n s -> p (n s)"), PS[:, 2 + h, :], ACT.Copy).then_inc(sem("pt_ev"), 1)
            act.wait_ge(sem("x_out"), 48)
            for r in range(NR):
                act.wait_ge(sem("v_mm"), NQ * (r + 1))
                act.activation(Z[:, 2, MR * r:MR * r + MR], PS[:, 3 * (r % 2), 0:MR], ACT.Copy).then_inc(sem("k1_ready"), 1)
            Um = U[:].rearrange("p n w -> p w n")
            for g in range(1, 32, 2):
                act.wait_ge(sem("mx_mm"), g + 1)
                act.activation(Um[:, 4 * g:4 * g + 4, :], PS[:, g % 4, :].rearrange("p (w n) -> p w n", w=4), ACT.Copy).then_inc(sem("mx_ev1"), 1)

            def inverse_evacs(layer):
                for g in range(1, NTR, 2):
                    act.wait_ge(sem("tr_mm"), layer * NTR + g + 1)
                    act.activation(Af[:, 512 * g:512 * (g + 1)], PS[:, g % 4, :], ACT.Copy).then_inc(sem("tr_ev1"), 1)
                for k in range(NIM):
                    act.wait_ge(sem("i1_mm"), 32 * layer + k + 1)
                    if k >= 3:
                        act.wait_ge(sem("i2_mm"), 32 * layer + k - 2)
                    act.activation(DB[0:66, k % 3, :], PS[0:66, 4 + k % 2, :], ACT.Copy).then_inc(sem("i1_ev"), 1)
                    if layer == 1:
                        if k >= 1:
                            gelu(k - 1)
                if layer == 1:
                    gelu(NIM - 1)

            def gelu(k):
                act.wait_ge(sem("y1_ready"), k + 1)
                v = Vn[:, 4 * k:4 * k + 4, :]
                act.activation(v, v, ACT.Gelu).then_inc(sem("src_ready"), 1)

            inverse_evacs(0)
            root()
            root()
            for layer in (1, 2):
                act.wait_ge(sem("a_ready"), layer + 1)
                forward_evacs(act, layer, "f2_mm_m", 1.0)
                act.wait_ge(sem("yr_ready"), layer)
                act.activation(Af[:, 2 * M:3 * M], Z[:, 2, :], ACT.Square, accum_out=lay[:, 0:1]).then_inc(sem("vsum"), 1)
                act.wait_ge(sem("yi_ready"), layer)
                act.activation(Af[:, 3 * M:4 * M], Z[:, 1, :], ACT.Square, accum_out=lay[:, 1:2]).then_inc(sem("vsum"), 1)
                root()
                inverse_evacs(layer)
            root()
            act.wait_ge(sem("fin_coef"), 1)
            for i in range(N):
                act.activation(U[:, i, :], U[:, i, :], ACT.Identity, scale=WS[:, 4, i:i + 1], bias=WS[:, 6, i:i + 1]).then_inc(sem("ua_ready"), 1)
            scalar_l1(act)


        @block.vector
        def _(dve):
            st = Steps(dve, sem("dve_step"))
            later = st.later

            dve.wait_ge(sem("w_in"), 16 * (4 + 8 + 10))
            neg, pos = slice(33, 64), slice(31, 0, -1)
            later(dve.tensor_tensor(WP[:, neg, 0, 0], WP[:, neg, 0, 0], WP[:, pos, 0, 0], ALU.add))
            later(dve.tensor_tensor(WP[:, neg, 0, 1], WP[:, neg, 0, 1], WP[:, pos, 0, 1], ALU.subtract))
            later(dve.memset(WP[:, 1:32, 0, :], 0.0))
            later(dve.memset(WP[:, 0, 0, 1:2], 0.0))
            for w in range(3):
                q = QKV[:, w]
                later(dve.tensor_tensor(q[:, 17:32, 0, 0], q[:, 17:32, 0, 0], q[:, 15:0:-1, 0, 0], ALU.add))
                later(dve.tensor_tensor(q[:, 17:32, 0, 1], q[:, 17:32, 0, 1], q[:, 15:0:-1, 0, 1], ALU.subtract))
                later(dve.tensor_scalar(q[:, 16:32, 0, :], q[:, 16:32, 0, :], 0.5, None, ALU.mult))
                later(dve.memset(q[:, 1:16, 0, :], 0.0))
                later(dve.memset(q[:, 0, 0, 1:2], 0.0))
            ks, qs, psw, vs = (headc[0:NH, i:i + 1] for i in range(4))
            WPf = V[0:NH, 0:2 * M].rearrange("p (m c) -> p m c", c=2)
            P3k = P3.rearrange("p c (k x) -> p c k x", x=KX)
            for c in range(2):
                later(dve.tensor_scalar(P3[:, c, :], WPf[:, :, c], vs, None, ALU.mult))
            for h, (r0, q0) in enumerate(((0, 0), (48, 16))):
                wr, wi = WP[:, r0:r0 + 16, 0:LX, 0], WP[:, r0:r0 + 16, 0:LX, 1]
                vr, vi = QKV[:, 2, q0:q0 + 16, :, 0], QKV[:, 2, q0:q0 + 16, :, 1]
                t1 = T1[:, 0:272].rearrange("p (k x) -> p k x", x=LX)
                er, ei = (P3k[:, c, r0:r0 + 16, 0:LX] for c in range(2))
                later(dve.tensor_scalar(wr, wr, psw, None, ALU.add))
                if h:
                    later(dve.tensor_scalar(wr[:, :, 0:1], wr[:, :, 0:1], psw, None, ALU.add))
                for a, b, e, op in ((wr, vr, er, ALU.add), (wi, vi, er, ALU.subtract), (wr, vi, ei, ALU.add), (wi, vr, ei, ALU.add)):
                    later(dve.tensor_tensor(t1, a, b, ALU.mult))
                    later(dve.tensor_tensor(e, e, t1, op))
            later(dve.tensor_tensor(P3[:, 2, :], P3[:, 0, :], P3[:, 1, :], ALU.add))
            dve.tensor_tensor(P3[:, 1, :], P3[:, 1, :], P3[:, 0, :], ALU.subtract).then_inc(sem("e_ready"), 1)
            flat = V[0:NH, 4224:7488].rearrange("p (w m c) -> p w m c", w=3, c=2)
            ar, ai, br, bi = flat[:, 0, :, 0], flat[:, 0, :, 1], flat[:, 1, :, 0], flat[:, 1, :, 1]
            later(dve.tensor_tensor(CR, ar, br, ALU.mult))
            later(dve.scalar_tensor_tensor(CR, br, qs, CR, ALU.mult, ALU.add))
            later(dve.scalar_tensor_tensor(CR, ar, ks, CR, ALU.mult, ALU.add))
            later(dve.tensor_tensor(T1, ai, bi, ALU.mult))
            later(dve.tensor_tensor(CR, CR, T1, ALU.add))
            later(dve.scalar_tensor_tensor(CI, br, ks, ai, ALU.add, ALU.mult))
            later(dve.scalar_tensor_tensor(T1, ar, qs, bi, ALU.add, ALU.mult))
            later(dve.tensor_tensor(CI, CI, T1, ALU.subtract))
            for c in (CR, CI):
                later(dve.tensor_scalar(c, c, 128.0, None, ALU.mult))
                later(dve.tensor_scalar(c[:, 0:1], c[:, 0:1], 0.5, None, ALU.mult))
                later(dve.memset(c.rearrange("p (k x) -> p k x", x=LX)[:, 1:16, 0:1], 0.0))
            dve.memset(T2[:, 0:1], 0.0).then_inc(sem("c_ready"), 1)
            later(dve.scalar_tensor_tensor(qk, headw[:, 0, :], 64.0, headw[:, 1, :], ALU.mult, ALU.mult))
            later(dve.tensor_tensor(pv, headw[:, 2, :], headw[:, 3, :], ALU.mult))

            def half_evac(layer, k):
                dve.wait_ge(sem("f1_mm"), 32 * layer + k + 1)
                dve.tensor_copy(A[:, 4 * k:4 * k + 4, :].rearrange("p n k -> p (n k)"), PS[:, k % 4, 0:264]).then_inc(sem("f1_ev"), 1)

            for k in range(32):
                half_evac(0, k)
            dve.wait_ge(sem("sq_mm"), 16)
            dve.wait_ge(sem("f1_ev"), 32)
            m1, m2, Rx, Cx, mg, eg, Rf, Cf = (SG[:, i, :] for i in range(8))
            later(dve.tensor_copy(m1, A[:, :, 0]))
            later(dve.tensor_copy(m2, PS[:, 4, 0:128]))
            later(dve.tensor_reduce(G8[:, 0:4], m1.rearrange("p (b t) -> p b t", b=B), AX.X, ALU.add))
            dve.tensor_reduce(G8[:, 4:8], m2.rearrange("p (b t) -> p b t", b=B), AX.X, ALU.add).then_inc(sem("g8_ready"), 1)
            dve.wait_ge(sem("g8_mm"), 1)
            rv, mean, rr, cc = rc[:, 0:4], rc[:, 4:8], rc[:, 8:12], rc[:, 12:16]
            later(dve.tensor_copy(mean, PS[:, 6, 0:4]))
            later(dve.tensor_tensor(rv, mean, mean, ALU.mult))
            later(dve.tensor_tensor(rv, PS[:, 6, 4:8], rv, ALU.subtract))
            dve.tensor_scalar(rv, rv, EPS, None, ALU.add).then_inc(sem("var_ready"), 1)
            dve.wait_ge(sem("root_ready"), 1)
            later(dve.reciprocal(rr, rv))
            later(dve.scalar_tensor_tensor(cc, mean, -1.0, rr, ALU.mult, ALU.mult))
            bt = lambda a: a.rearrange("p (b t) -> p b t", b=B)
            rb, cb = rr.unsqueeze(2).broadcast_to([128, B, T]), cc.unsqueeze(2).broadcast_to([128, B, T])
            later(dve.tensor_copy(bt(Rf), rb))
            later(dve.tensor_copy(bt(Cf), cb))
            later(dve.tensor_tensor(mg, Rf, m1, ALU.mult))
            later(dve.tensor_tensor(mg, mg, Cf, ALU.add))
            later(dve.tensor_tensor(Rx, Rf, m2, ALU.mult))
            later(dve.scalar_tensor_tensor(Cx, Cf, 2.0, m1, ALU.mult, ALU.mult))
            later(dve.tensor_tensor(Rx, Rx, Cx, ALU.add))
            later(dve.tensor_tensor(Rx, Rx, Rf, ALU.mult))
            later(dve.tensor_tensor(Cx, Cf, Cf, ALU.mult))
            dve.tensor_tensor(eg, Rx, Cx, ALU.add).then_inc(sem("rc_ready"), 1)
            for b in range(B):
                a = A[:, T * b:T * b + T, :].rearrange("p n k -> p (n k)")
                later(dve.tensor_scalar(a, a, rr[:, b:b + 1], None, ALU.mult))
            for b in range(B):
                ins = dve.tensor_scalar(A[:, T * b:T * b + T, 0:1], A[:, T * b:T * b + T, 0:1], cc[:, b:b + 1], None, ALU.add)
            ins.then_inc(sem("a_ready"), 1)
            dve.wait_ge(sem("is_mm"), 1)
            later(dve.tensor_copy(rim, PS[:, 7, 0:128]))
            dve.tensor_copy(cim, PS[:, 7, 128:256]).then_inc(sem("rim_ready"), 1)
            later(dve.tensor_copy(istat[:, 0:2], PS[:, 6, 16:18]))
            later(dve.tensor_tensor(istat[:, 2:3], istat[:, 0:1], istat[:, 0:1], ALU.mult))
            later(dve.tensor_tensor(istat[:, 2:3], istat[:, 1:2], istat[:, 2:3], ALU.subtract))
            dve.tensor_scalar(istat[:, 2:3], istat[:, 2:3], EPS, None, ALU.add).then_inc(sem("var_ready"), 1)
            dve.wait_ge(sem("root_ready"), 2)
            later(dve.reciprocal(istat[:, 3:4], istat[:, 2:3]))
            later(dve.tensor_tensor(alpha, istat[:, 3:4], PAR["norm1_w"], ALU.mult))
            later(dve.tensor_tensor(beta, istat[:, 0:1], alpha, ALU.mult))
            dve.tensor_tensor(beta, PAR["norm1_b"], beta, ALU.subtract).then_inc(sem("alpha_ready"), 1)
            dve.wait_ge(sem("alpha_ready"), 1)

            forward_evacs(dve, 0, "f2_mm_x", alpha)
            all_emptied(dve, "f2_ev", 1, NF2)
            dve.tensor_tensor(Z[:, 0, 0:1], Z[:, 0, 0:1], beta, ALU.add).then_inc(sem("x_beta"), 1)
            dve.wait_ge(sem("x_beta"), 1)
            for c in range(2):
                for h in range(2):
                    ins = dve.tensor_copy(XL[:, c, 272 * h:272 * h + 272].rearrange("p (k x) -> p k x", x=LX),
                                          Zk[:, c, 48 * h:48 * h + 16, 0:LX])
            ins.then_inc(sem("xl_ready"), 1)
            dve.tensor_tensor(XS, Z[:, 0, :], Z[:, 1, :], ALU.add).then_inc(sem("xs_ready"), 1)
            dve.wait_ge(sem("xe_scaled"), 1)
            later(dve.tensor_tensor(XEk[:, 0, neg, 32], XEk[:, 0, neg, 32], XEk[:, 0, pos, 32], ALU.add))
            later(dve.tensor_tensor(XEk[:, 1, neg, 32], XEk[:, 1, neg, 32], XEk[:, 1, pos, 32], ALU.subtract))
            for c in range(2):
                later(dve.tensor_scalar(XEk[:, c, neg, 32], XEk[:, c, neg, 32], 0.5, None, ALU.mult))
                later(dve.memset(XEk[:, c, 1:32, 0:33:32], 0.0))
            later(dve.memset(XEk[:, 1, 0:33:32, 0:33:32], 0.0))
            dve.tensor_copy(XEk[:, 0, 0:33:32, 0:33:32], Zk[:, 0, 0:33:32, 0:33:32]).then_inc(sem("xe_ready"), 1)
            dve.wait_ge(sem("ct_mm"), 1)
            for k in range(NLC):
                w = min(128, ML - 128 * k)
                dve.tensor_copy(CT[0:w, 0, k, :], PS[0:w, 5, 32 * k:32 * k + 32])
                dve.tensor_copy(CT[0:w, 1, k, :], PS[0:w, 5, 160 + 32 * k:192 + 32 * k])
                later(dve.tensor_scalar(CT[0:w, 2, k, :], PS[0:w, 5, 160 + 32 * k:192 + 32 * k], -1.0, None, ALU.mult))
            dve.memset(lay[:, 0:1], 0.0).then_inc(sem("ct_ready"), 1)
            dve.wait_ge(sem("xlt_mm"), 1)
            for i in range(2 * NLC):
                w = 128 if i % NLC < NLC - 1 else ML - 128 * (NLC - 1)
                ins = dve.tensor_copy(XLT[0:w, i // NLC, i % NLC, :], PS[0:w, (3, 4, 7)[i // 4], 128 * (i % 4):128 * (i % 4) + 128])
            ins.then_inc(sem("xlt_ev"), 1)
            dve.wait_ge(sem("xlt_ev"), 1)
            dve.wait_ge(sem("gram_mm"), 1)
            for b in range(B):
                later(dve.tensor_copy(Gd[32 * b:32 * b + 32, :], PS[32 * b:32 * b + 32, 6, 32 * b:32 * b + 32]))

            for z in range(8 * NLC):
                if z % 4 < 3:
                    score_products(dve, z)
            qkb = qk.unsqueeze(2).broadcast_to([128, NH, T])
            later(dve.tensor_tensor(SE, qkb, Gd.unsqueeze(1).broadcast_to([128, NH, T]), ALU.mult))
            dve.wait_ge(sem("s_mm"), 8 * NLC)
            later(dve.tensor_tensor(SD, SE, PS[:, 0:2, :].rearrange("p h (n s) -> p (h n) s", s=T), ALU.add))
            later(dve.tensor_reduce(rmx, SD, AX.X, ALU.max))
            dve.tensor_tensor(SD, SD, rmx.unsqueeze(2).broadcast_to([128, NH, T]), ALU.subtract).then_inc(sem("sd_ready"), 1)
            dve.wait_ge(sem("se_ready"), 1)
            later(dve.tensor_reduce(rmx, SE, AX.X, ALU.add))
            later(dve.reciprocal(rmx, rmx))
            dve.tensor_tensor(SE, SE, rmx.unsqueeze(2).broadcast_to([128, NH, T]), ALU.mult).then_inc(sem("p_ready"), 1)
            dve.wait_ge(sem("p_ready"), 1)
            later(dve.tensor_tensor(SD, SE, pv.unsqueeze(2).broadcast_to([128, NH, T]), ALU.mult))
            later(dve.tensor_reduce(Pb, SD.rearrange("p n s -> p s n"), AX.X, ALU.add))
            later(dve.memset(SG2, 0.0))
            for b in range(B):
                s = slice(32 * b, 32 * b + 32)
                ins = dve.tensor_copy(SG2[s, s], Pb[s, :])
            ins.then_inc(sem("pb_ready"), 1)
            dve.wait_ge(sem("mix_mm"), 1)
            dve.tensor_copy(Pbt, PS[:, 6, 0:128]).then_inc(sem("pbt_ready"), 1)
            dve.wait_ge(sem("pbt_ready"), 1)
            dve.scalar_tensor_tensor(Mt, Pbt, alpha, ident, ALU.mult, ALU.add).then_inc(sem("mt_ready"), 1)
            dve.wait_ge(sem("mix_mm"), 2)
            dve.tensor_copy(istat[:, 0:1], PS[:, 7, 0:1]).then_inc(sem("pbar_ready"), 1)
            def value_sums(r):
                m = slice(MR * r, MR * r + MR)
                dve.wait_ge(sem("k1_ready"), r + 1)
                if r == 0:
                    dve.wait_ge(sem("x_out"), 48)
                dve.tensor_tensor(Z[:, 0, m], Z[:, 2, m], PS[:, 3 * (r % 2) + 2, 0:MR], ALU.subtract)
                later(dve.tensor_tensor(Z[:, 1, m], Z[:, 2, m], PS[:, 3 * (r % 2) + 1, 0:MR], ALU.add))
                dve.tensor_scalar(Z[:, 2, m], Z[:, 0, m], -1.0, None, ALU.mult).then_inc(sem("zv_ev"), 1)

            for k in range(NR * NQ):
                value_products(dve, k, slice(0, B - 1), "y_dve")
                if k % NQ == 1 and k > NQ:
                    value_sums(k // NQ - 1)
            value_sums(NR - 1)
            dve.wait_ge(sem("zv_ev"), NR)
            later(dve.tensor_tensor(Z[:, 0, 0:1], Z[:, 0, 0:1], istat[:, 0:1], ALU.add))
            dve.tensor_scalar(Z[:, 2, 0:1], Z[:, 0, 0:1], -1.0, None, ALU.mult).then_inc(sem("z_ready"), 1)
            Um = U[:].rearrange("p n w -> p w n")
            dve.wait_ge(sem("z_ready"), 1)
            for g in range(0, 32, 2):
                dve.wait_ge(sem("mx_mm"), g + 1)
                dve.tensor_copy(Um[:, 4 * g:4 * g + 4, :], PS[:, g % 4, :].rearrange("p (w n) -> p w n", w=4)).then_inc(sem("mx_ev0"), 1)

            def transposed_evacs(layer):
                for g in range(0, NTR, 2):
                    dve.wait_ge(sem("tr_mm"), layer * NTR + g + 1)
                    w = 512 if g < NTR - 1 else 256
                    dve.tensor_copy(Af[:, 512 * g:512 * g + w], PS[:, g % 4, 0:w]).then_inc(sem("tr_ev0"), 1)

            def image_stats(src, k):
                for j in range(4):
                    ins = dve.bn_stats(ST[:, 4 * k + j, :], src[:, 4 * k + j, :])
                return ins

            def row_moments():
                s = ST[:].rearrange("p n k -> p k n")
                t, m, e = WS[:, 2, :], WS[:, 0, :], WS[:, 1, :]
                later(dve.tensor_tensor(m, s[:, 1], s[:, 4], ALU.add))
                later(dve.tensor_scalar(m, m, 0.5, None, ALU.mult))
                later(dve.tensor_tensor(e, s[:, 2], s[:, 5], ALU.add))
                later(dve.tensor_scalar(e, e, 1.0 / 128, None, ALU.mult))
                for i in (1, 4):
                    later(dve.scalar_tensor_tensor(t, s[:, i], 0.5, s[:, i], ALU.mult, ALU.mult))
                    later(dve.tensor_tensor(e, e, t, ALU.add))

            all_emptied(dve, "mx_ev", 1, 32)
            transposed_evacs(0)
            for k in range(NIM):
                dve.wait_ge(sem("i2_mm"), k + 1)
                u = U[:, 4 * k:4 * k + 4, :]
                dve.tensor_tensor(u, u, PS[:, 6 + k % 2, :].rearrange("p (n w) -> p n w", w=W), ALU.add).then_inc(sem("i2_ev"), 1)
                if k >= 1:
                    dve.wait_ge(sem("i2_ev"), k)
                    image_stats(U, k - 1)
            dve.wait_ge(sem("i2_ev"), NIM)
            later(image_stats(U, NIM - 1))
            row_moments()
            dve.memset(lay[:, 0:1], 0.0).then_inc(sem("mv_ready"), 1)
            dve.wait_ge(sem("mv_mm"), 1)
            mu, e2, r, v = WS[:, 2, :], WS[:, 1, :], WS[:, 4, :], WS[:, 3, :]
            later(dve.tensor_copy(mu, PS[:, 7, 0:128]))
            later(dve.tensor_tensor(v, mu, mu, ALU.mult))
            later(dve.tensor_tensor(e2, PS[:, 7, 128:256], v, ALU.subtract))
            dve.tensor_scalar(v, e2, EPS, None, ALU.add).then_inc(sem("var_ready"), 1)
            dve.wait_ge(sem("root_ready"), 3)
            later(dve.reciprocal(r, v))
            later(dve.tensor_scalar(r, r, PAR["attn_w"], None, ALU.mult))
            later(dve.tensor_tensor(v, r, r, ALU.mult))
            v2, r2, b2 = WS[:, 5, :], WS[:, 6, :], WS[:, 7, :]
            later(dve.tensor_tensor(v2, v, e2, ALU.mult))
            dve.tensor_scalar(v2, v2, EPS, None, ALU.add).then_inc(sem("var_ready"), 1)
            dve.wait_ge(sem("root_ready"), 4)
            later(dve.reciprocal(r2, v2))
            later(dve.tensor_scalar(r2, r2, PAR["norm2_w"], None, ALU.mult))
            later(dve.tensor_tensor(r2, r2, r, ALU.mult))
            later(dve.tensor_tensor(b2, mu, r2, ALU.mult))
            later(dve.tensor_scalar(b2, b2, -1.0, PAR["norm2_b"], ALU.mult, ALU.add))
            later(dve.tensor_tensor(v2, mu, r, ALU.mult))
            later(dve.tensor_scalar(v2, v2, -1.0, PAR["attn_b"], ALU.mult, ALU.add))
            for k in range(NIM):
                for i in range(4 * k, 4 * k + 4):
                    ins = dve.tensor_scalar(Vn[:, i, :], U[:, i, :], WS[:, 6, i:i + 1], WS[:, 7, i:i + 1], ALU.mult, ALU.add)
                ins.then_inc(sem("src_ready"), 1)
                if k >= 2:
                    half_evac(1, k - 2)
            half_evac(1, NIM - 2)
            half_evac(1, NIM - 1)
            for layer in (1, 2):
                if layer == 2:
                    for k in range(NIM):
                        half_evac(2, k)
                dve.wait_ge(sem("f1_ev"), 32 * (layer + 1))
                dve.memset(lay[:, 4:5], 0.0).then_inc(sem("a_ready"), 1)
                forward_evacs(dve, layer, "f2_mm_m", 1.0)
                dve.wait_ge(sem("mw_in"), 16 * layer)
                wk = Af[:, 0:2 * M].rearrange("p (k x c) -> p k x c", k=KY, c=2)
                later(dve.tensor_tensor(wk[:, neg, 0, 0], wk[:, neg, 0, 0], wk[:, pos, 0, 0], ALU.add))
                later(dve.tensor_tensor(wk[:, neg, 0, 1], wk[:, neg, 0, 1], wk[:, pos, 0, 1], ALU.subtract))
                later(dve.memset(wk[:, 1:32, 0, :], 0.0))
                later(dve.memset(wk[:, 0, 0, 1:2], 0.0))
                all_emptied(dve, "f2_ev", layer + 1, NF2)
                wr = Af[:, 0:2 * M].rearrange("p (m c) -> p m c", c=2)
                t1, t2 = Af[:, 2 * M:3 * M], Af[:, 3 * M:4 * M]
                yr, yi = Z[:, 2, :], Z[:, 1, :]
                later(dve.tensor_tensor(yr, Z[:, 0, :], wr[:, :, 0], ALU.mult))
                later(dve.tensor_tensor(t1, Z[:, 1, :], wr[:, :, 1], ALU.mult))
                later(dve.tensor_tensor(t2, Z[:, 0, :], wr[:, :, 1], ALU.mult))
                later(dve.tensor_tensor(yr, yr, t1, ALU.subtract))
                later(dve.tensor_tensor(t1, Z[:, 1, :], wr[:, :, 0], ALU.mult))
                later(dve.tensor_tensor(yi, t1, t2, ALU.add))
                later(dve.memset(Z[:, 2, 0:1], 0.0))
                later(dve.memset(Z[:, 1, 0:1], 0.0))
                c0 = Zk[:, 1:3, :, 0]
                later(dve.tensor_tensor(DB[:, 0, 0:128].rearrange("p (c k) -> p c k", c=2), c0, c0, ALU.mult))
                later(dve.tensor_reduce(lay[:, 3:4], DB[:, 0, 0:128], AX.X, ALU.add))
                dve.memset(lay[:, 4:5], 0.0).then_inc(sem("yr_ready"), 1)
                dve.memset(lay[:, 5:6], 0.0).then_inc(sem("yi_ready"), 1)
                dve.wait_ge(sem("vsum"), 2 * layer)
                later(dve.tensor_tensor(lay[:, 2:3], lay[:, 0:1], lay[:, 1:2], ALU.add))
                later(dve.tensor_scalar(lay[:, 2:3], lay[:, 2:3], 2.0, EPS, ALU.mult, ALU.add))
                dve.scalar_tensor_tensor(lay[:, 2:3], lay[:, 3:4], -1.5, lay[:, 2:3], ALU.mult, ALU.add).then_inc(sem("var_ready"), 1)
                dve.wait_ge(sem("root_ready"), 4 + layer)
                later(dve.reciprocal(lay[:, 6:7], lay[:, 2:3]))
                later(dve.tensor_scalar(Z[:, 0, :], Z[:, 2, :], lay[:, 6:7], None, ALU.mult))
                later(dve.tensor_scalar(Z[:, 1, :], Z[:, 1, :], lay[:, 6:7], None, ALU.mult))
                dve.tensor_scalar(Z[:, 2, :], Z[:, 0, :], -1.0, None, ALU.mult).then_inc(sem("z_ready"), 1)
                transposed_evacs(layer)
                sw = PAR["m0sw"] if layer == 1 else PAR["m1sw"]
                for k in range(NIM):
                    dve.wait_ge(sem("i2_mm"), NIM * layer + k + 1)
                    v4 = Vn[:, 4 * k:4 * k + 4, :]
                    y = dve.scalar_tensor_tensor(v4, v4, sw, PS[:, 6 + k % 2, :].rearrange("p (n w) -> p n w", w=W), ALU.mult, ALU.add)
                    y.then_inc(sem("i2_ev"), 1)
                    if layer == 1:
                        dve.wait_ge(sem("i2_ev"), NIM * layer + k + 1)
                        dve.memset(lay[:, 7:8], 0.0).then_inc(sem("y1_ready"), 1)
                    elif k >= 1:
                        dve.wait_ge(sem("i2_ev"), NIM * layer + k)
                        image_stats(Vn, k - 1)
            dve.wait_ge(sem("i2_ev"), 3 * NIM)
            later(image_stats(Vn, NIM - 1))
            row_moments()
            dve.memset(lay[:, 0:1], 0.0).then_inc(sem("mv_ready"), 1)
            dve.wait_ge(sem("mv_mm"), 2)
            later(dve.tensor_copy(mu, PS[:, 0, 0:128]))
            later(dve.tensor_tensor(v, mu, mu, ALU.mult))
            later(dve.tensor_tensor(e2, PS[:, 0, 128:256], v, ALU.subtract))
            dve.tensor_scalar(v, e2, EPS, None, ALU.add).then_inc(sem("var_ready"), 1)
            dve.wait_ge(sem("root_ready"), 7)
            later(dve.reciprocal(v, v))
            later(dve.tensor_scalar(v, v, PAR["mon_w"], None, ALU.mult))
            later(dve.tensor_tensor(b2, mu, v, ALU.mult))
            later(dve.tensor_scalar(b2, b2, -1.0, PAR["mon_b"], ALU.mult, ALU.add))
            dve.tensor_tensor(r2, v2, b2, ALU.add).then_inc(sem("fin_coef"), 1)
            for i in range(N):
                dve.wait_ge(sem("ua_ready"), i + 1)
                dve.scalar_tensor_tensor(U[:, i, :], Vn[:, i, :], WS[:, 3, i:i + 1], U[:, i, :], ALU.mult, ALU.add).then_inc(sem("o_ready"), 1)
            vector_l1(dve, st, image_stats, row_moments)




_INS = ['x', 'L0_conv_norm1_w', 'L0_conv_norm1_b', 'L0_conv_Kcw', 'L0_conv_Ksw', 'L0_conv_Qcw', 'L0_conv_Qsw', 'L0_conv_Vcw',
        'L0_conv_Vsw', 'L0_conv_Pcw', 'L0_conv_Psw', 'L0_conv_attn_w', 'L0_conv_attn_b', 'L0_conv_norm2_w', 'L0_conv_norm2_b',
        'L0_conv_m0cw', 'L0_conv_m0sw', 'L0_conv_m1cw', 'L0_conv_m1sw', 'L0_conv_mon_w', 'L0_conv_mon_b', 'L1_attn_Wq',
        'L1_attn_Wk', 'L1_attn_Wv', 'L1_ffn_gate_w', 'L1_ffn_gate_b', 'L1_ffn_weight1', 'L1_ffn_weight2']


def kernel(**inputs):
    import numpy as _np
    import concourse.bacc as _bacc
    from concourse.bass_utils import run_bass_kernel_spmd as _run

    nc = _bacc.Bacc("TRN2", target_bir_lowering=False, num_devices=1)
    arrays, io = {}, {}
    for name in _INS:
        a = _np.ascontiguousarray(inputs[name])
        arrays[f"in_{name}"] = a
        io[name] = nc.dram_tensor(f"in_{name}", a.shape, mybir.dt.from_np(a.dtype), kind="ExternalInput").ap()
    c = shape_constants()
    arrays["in_consts"] = c
    io["consts"] = nc.dram_tensor("in_consts", c.shape, F32, kind="ExternalInput").ap()
    out = nc.dram_tensor("out_0", (B, T, H, W), F32, kind="ExternalOutput").ap()
    conv_attn_hybrid(nc, io, out)
    r = _run(nc, [arrays], core_ids=[0])
    return r.results[0]["out_0"]
```

```python
import numpy as np
import concourse.bass as bass
from concourse import mybir
from contextlib import ExitStack

F32 = mybir.dt.float32
ALU = mybir.AluOpType
ACT = mybir.ActivationFunctionType
AX = mybir.AxisListType

B, T, H, W = 4, 32, 128, 128
N = B * T
NH = 32
KY, KX = 64, 33
M = KY * KX
LK, LX = 32, 17
ML = LK * LX
NLC = -(-ML // 128)
NR = 6
MR = M // NR
NQ = 8
GW, GE = 4, 16384
EPS = 1e-5
TOK = H * T
NT = T
D = W
EX, HID, TOPK = 64, 512, 8
EG = 4
NEG = -1e30
SCALE = float(D) ** -0.5

CONST_LAYOUT = [("ident", 128), ("ones", 128), ("group", 128), ("mask", 128), ("fh", 66), ("fwr", 132), ("fwi", 132),
                ("ih", 128), ("iw", 128)]


def shape_constants():
    ky = np.concatenate([np.arange(32), np.arange(-32, 0)])
    kx = np.arange(KX)
    p = np.arange(128)
    c = {}
    c["ident"] = np.eye(128)
    c["ones"] = np.full((128, 128), 1.0 / 128)
    c["group"] = (p[:, None] // GW == p[None, :] // GW) / float(GW * T)
    c["mask"] = np.where(p[None, :] > p[:, None], NEG, 0.0)
    a = 2 * np.pi * np.outer(p, kx) / 128
    c["fh"] = np.concatenate([np.cos(a), -np.sin(a)], 1) / 128
    co, si = np.cos(a) / 128, np.sin(a) / 128
    c["fwr"] = np.concatenate([co, -si, co, -si], 1)
    c["fwi"] = np.concatenate([si, co, -si, -co], 1)
    b = 2 * np.pi * np.outer(ky, p) / 128
    c["ih"] = np.concatenate([np.cos(b), -np.sin(b)], 0)
    twice = np.where(kx == 0, 1.0, 2.0)[:, None]
    a = 2 * np.pi * np.outer(kx, p) / 128
    iw = np.zeros((128, 128))
    iw[0:2 * KX] = np.concatenate([twice * np.cos(a), -twice * np.sin(a)], 0)
    c["iw"] = iw
    return np.concatenate([c[n] for n, _ in CONST_LAYOUT], 1).astype(np.float32)


class Steps:

    def __init__(self, eng, sem):
        self.eng, self.sem, self.base, self.n = eng, sem, 0, 0

    def later(self, ins):
        self.n += 1
        ins.then_inc(self.sem, 1)
        self.eng.wait_ge(self.sem, self.base + self.n)


def conv_attn_hybrid(nc, io, out):
    with ExitStack() as ctx:
        def sb(name, shape):
            return ctx.enter_context(nc.sbuf_tensor(name, shape, F32))

        sems = {}

        def sem(name):
            if name not in sems:
                sems[name] = ctx.enter_context(nc.semaphore(name))
            return sems[name]

        CW = sum(w for _, w in CONST_LAYOUT)
        U = sb("U", [128, N, W])
        V = sb("V", [128, 128 * 128])
        A = sb("A", [128, N, 2 * KX])
        Z = sb("Z", [128, 3, M])
        DB = sb("DB", [128, 3, 512])
        CST = sb("CST", [128, CW])
        ST = sb("ST", [128, N, 6])
        MI = sb("MI", [128, 2128])
        PS = ctx.enter_context(nc.psum_tensor("PS", [128, 8, 512], F32))
        e_dram = nc.dram_tensor("e_planes", (NR, NH, 3, MR), F32, kind="Internal").ap()
        x_dram = nc.dram_tensor("x_planes", (NR, N, 3, MR), F32, kind="Internal").ap()

        cst, o = {}, 0
        for name, w in CONST_LAYOUT:
            cst[name] = CST[:, o:o + w]
            o += w
        ident, ones = cst["ident"], cst["ones"]
        Uf = U[:].rearrange("p n w -> p (n w)")
        Af = A[:].rearrange("p n k -> p (n k)")
        Vn = V[:].rearrange("p (n w) -> p n w", w=W)
        Zk = Z[:].rearrange("p c (k x) -> p c k x", x=KX)

        at = [0]

        def mi(width):
            at[0] += width
            assert at[0] <= 2128
            return MI[:, at[0] - width:at[0]]

        CT = mi(3 * NLC * NH).rearrange("p (c k n) -> p c k n", c=3, k=NLC)
        headw = mi(4 * NH).rearrange("p (c n) -> p c n", c=4)
        headc = mi(4)
        par = mi(12)
        PAR = {n: par[:, i:i + 1] for i, n in enumerate(
            ["norm1_w", "norm1_b", "attn_w", "attn_b", "norm2_w", "norm2_b", "mon_w", "mon_b", "m0sw", "m1sw"])}
        rim, cim = mi(128), mi(128)
        alpha, beta, istat = mi(1), mi(1), mi(4)
        Gd = mi(32)
        Pb = mi(32)
        qk = mi(NH)
        pv = mi(NH)
        G8, rc = mi(8), mi(16)
        Pbt, Mt = (ST[:].rearrange("p n k -> p (n k)")[:, 128 * i:128 * i + 128] for i in range(2))
        rmx = mi(NH)
        lay = mi(8)
        WS = mi(8 * 128).rearrange("p (k n) -> p k n", k=8)

        XN = Uf[:, 0:3072].rearrange("p (c i w) -> p c i w", c=3, i=8)
        XQ = Uf[:, 3072:5120].rearrange("p (c i w) -> p c i w", c=2, i=8)
        XE = Uf[:, 0:2 * M].rearrange("p (c m) -> p c m", c=2)
        XEk = Uf[:, 0:2 * M].rearrange("p (c k x) -> p c k x", c=2, x=KX)
        XL = Uf[:, 4224:5312].rearrange("p (c m) -> p c m", c=2)
        XET = Uf[:, 5376:9600].rearrange("p (k n) -> p k n", n=N)
        XLT = Uf[:, 9600:10880].rearrange("p (c k n) -> p c k n", c=2, k=NLC)
        ZP = [Uf[:, o:o + 2048].rearrange("p (n s) -> p n s", n=16) for o in (0, 2048, 5376, 7424)]
        SD = Uf[:, 12928:13952].rearrange("p (n s) -> p n s", n=NH)
        SE = Uf[:, 13952:14976].rearrange("p (n s) -> p n s", n=NH)
        PT = Uf[:, 8448:9472].rearrange("p (g s) -> p g s", g=NQ)
        EB = Uf[:, 9600:12768].rearrange("p (c k m) -> p c k m", c=3, k=3)
        YB = Uf[:, 0:8448].rearrange("p (c b k m) -> p c b k m", c=2, b=B, k=3)
        XR = Af.rearrange("p (c b k m) -> p c b k m", c=2, b=B, k=3)
        SG = Uf[:, 10880:12928].rearrange("p (k n) -> p k n", n=128)
        SG2 = SG[:, 0, :]
        MV = WS[:, 0:2, :].rearrange("p k n -> p (k n)")
        root_args = [rc[:, 0:4], istat[:, 2:3], WS[:, 3, :], WS[:, 5, :], lay[:, 2:3], lay[:, 2:3], WS[:, 3, :]]
        XS = Af[:, 0:M]

        WP = V[0:NH, 0:2 * M].rearrange("p (k x c) -> p k x c", k=KY, c=2)
        QKV = V[0:NH, 4224:7488].rearrange("p (w k x c) -> p w k x c", w=3, k=LK, c=2)
        P3 = V[0:NH, 7488:13824].rearrange("p (k m) -> p k m", k=3)
        CR = V[0:NH, 13824:14368]
        CI = V[0:NH, 14368:14912]
        T1 = V[0:NH, 14912:15456]
        T2 = V[0:NH, 15456:16000]

        x_nat = io["x"].rearrange("b t h w -> h (b t) w")
        x_img = io["x"].rearrange("b t h w -> (b t) (h w)")
        out_nat = out.rearrange("b t h w -> h (b t) w")

        QT = V[:, 0:TOK]
        KT = V[:, TOK:2 * TOK]
        VV = V[:, 2 * TOK:3 * TOK].rearrange("p (t d) -> p t d", d=D)
        XT = V[:, 3 * TOK:4 * TOK]
        AF = [Af, Z[:].rearrange("p c m -> p (c m)")]
        SR = [Af[:, 0:TOK], Af[:, TOK:2 * TOK], XT]
        XB = AF[1][:, 0:TOK].rearrange("p (t d) -> p t d", d=D)
        WT3 = AF[1][:, 4096:4096 + 384].rearrange("p (c h) -> p c h", c=3)
        WN3 = AF[1][:, 4480:4864].rearrange("p (c h) -> p c h", c=3)
        PTB = DB
        bmax = AF[1][:, 4864:4880]
        mraw, rden = AF[1][:, 4880:4882], AF[1][:, 4882:4884]
        nmax, rsum = AF[1][:, 4892:4895], AF[1][:, 5346:5349]
        gmx = AF[1][:, 4884:4892].rearrange("p (q k) -> p q k", q=2)
        tkr = AF[1][:, 4896:5024]
        tkn = AF[1][:, 5024:5152]
        gwT = AF[1][:, 5152:5216]
        gwn = AF[1][0:EX, 5216:5344]
        gbs = AF[1][:, 5344:5345]
        top8 = AF[1][:, 5352:5360]
        poolT = AF[1][:, 5360:5616].rearrange("p (b e) -> p b e", b=B)
        b2n = AF[1][:, 5616:5744]
        outE = AF[1][:, 5744:6000].rearrange("p (q o) -> p q o", q=2)

        NF2, NTR, NIM = 11, 17, 32
        CH = NT * (NT // 4 + 1) // 2

        blocks = [i // 4 + 1 for i in range(NT)]
        first = [sum(blocks[:i]) for i in range(NT)]
        XTS = [DB[:, 0, :], DB[:, 1, :], DB[:, 2, :], ST[:].rearrange("p n k -> p (n k)")[:, 0:512]]
        LG = [Af[:, 0:TOK], Af[:, TOK:2 * TOK]]
        LR = [AF[1][:, 0:TOK], V[:, 3 * TOK:4 * TOK]]
        MN = AF[1][:, 0:TOK].rearrange("p (t e) -> p t e", e=2 * EX)
        VG = V[:].rearrange("p (c k x) -> p c k x", c=4, k=2)
        W1B = VG[:, :, 0, :].rearrange("p c (e h) -> p c e h", e=EG)
        W2B = VG[:, :, 1, :].rearrange("p c (e k o) -> p c e k o", e=EG, k=4)
        B1T = MI[:, 0:EX * 4].rearrange("p (e k) -> p e k", k=4)
        HB = WS[:, 2, :].rearrange("p (c x) -> p c x", c=2)
        HG = WS[:, 3, :].rearrange("p (c x) -> p c x", c=2)
        OT = WS[:, 4:6, :].rearrange("p k n -> p (k n)").rearrange("p (b e) -> p b e", b=B)
        NG = EX // EG

        def sync_l1(sp):
            for b2 in range(2):
                sp.dma_start(gbs[EX * b2:EX * b2 + EX], io["L1_ffn_gate_b"].unsqueeze(1)).then_inc(sem("l1w_in"), 16)
            sp.wait_ge(sem("l1_start"), 1)
            sp.dma_start(B1T, io["L1_ffn_weight1"][:, D, :].rearrange("e (p k) -> p e k", k=4)).then_inc(sem("b1_in"), 16)
            sp.wait_ge(sem("w_mm"), B * CH)
            for g in range(NG):
                if g == 3:
                    sp.wait_ge(sem("gate_ready"), 2)
                if g >= 4:
                    sp.wait_ge(sem("e2_mm"), g - 3)
                e = slice(EG * g, EG * g + EG)
                sp.dma_start(W1B[:, g % 4], io["L1_ffn_weight1"][e, 0:D, :].rearrange("e d h -> d e h")).then_inc(sem(f"ew_in{g % 4}"), 16)
                sp.dma_start(W2B[:, g % 4].rearrange("p e k o -> p e (k o)"),
                             io["L1_ffn_weight2"][e, 0:HID, :].rearrange("e (p k) o -> p e (k o)", k=4)).then_inc(sem(f"ew_in{g % 4}"), 16)
            for b in range(B):
                store(sp, b)
            sp.wait_ge(sem("out_done"), 16 * 2 * B)

        def store(sp, b):
            for h in range(2):
                sp.wait_ge(sem("fin_ready"), 8 * b + 4 * h + 4)
                i = T * b + 16 * h
                sp.dma_start(out_nat[:, i:i + 16, :], U[:, i:i + 16, :]).then_inc(sem("out_done"), 16)

        def tensor_l1(pe):
            pe.wait_ge(sem("l1w_in"), 16 * 8)
            pe.wait_ge(sem("x1_ready"), 16)
            for i in range(3):
                pe.transpose(PS[:, 0, 128 * i:128 * i + 128], WN3[:, i, :], ident)
            pe.transpose(PS[:, 0, 384:384 + EX], gwn, ident[0:EX, 0:EX]).then_inc(sem("wt_mm"), 1)
            pe.wait_ge(sem("wt_ready"), 1)

            with pe.Fori(0, B) as b:
                pe.wait_ge(sem("tokens_ready"), b + 1)
                pe.wait_ge(sem("batch_begun"), b + 1)
                for g in range(32):
                    if g >= 4:
                        pe.wait_ge(sem(f"pre_ev{g % 2}"), b * 16 + (g - 4) // 2 + 1)
                    if g == 8:
                        pe.wait_ge(sem("pre_ev0"), b * 16 + 4)
                        pe.wait_ge(sem("pre_ev1"), b * 16 + 4)
                    o = PS[:, g % 4, :]
                    k = g % 8
                    if g < 8:
                        for j in range(4):
                            mm = pe.transpose(o[:, 128 * j:128 * j + 128], XB[:, 4 * k + j, :], ident)
                    elif g < 24:
                        mm = pe.matmul(o, WT3[:, g // 8 - 1, :], XT[:, 512 * k:512 * k + 512], start=True, stop=True)
                    else:
                        for j in range(4):
                            mm = pe.matmul(o[:, 128 * j:128 * j + 128], XT[:, 512 * k + 128 * j:512 * k + 128 * j + 128],
                                           WT3[:, 2, :], start=True, stop=True)
                    mm.then_inc(sem("pre_mm"), 1)
                pe.wait_ge(sem("pre_ev0"), b * 16 + 16)
                pe.wait_ge(sem("pre_ev1"), b * 16 + 16)

                def scores(i):
                    for j in range(blocks[i]):
                        c = first[i] + j
                        w = min(512, 128 * (i + 1) - 512 * j)
                        if c >= 3:
                            pe.wait_ge(sem("sc_ev"), b * CH + c - 2)
                        last = j == blocks[i] - 1
                        mm = pe.matmul(PS[:, c % 3, 0:w], QT[:, 128 * i:128 * i + 128], KT[:, 512 * j:512 * j + w], start=True, stop=not last)
                        if last:
                            mm = pe.matmul(PS[:, c % 3, w - 128:w], ident, cst["mask"], start=False, stop=True)
                        mm.then_inc(sem("sc_mm"), 1)

                def turn(i, j):
                    c = first[i] + j
                    if c >= 3:
                        pe.wait_ge(sem(f"t_ev{(c - 3) % 2}"), b * (CH // 2) + (c - 3) // 2 + 1)
                    for k in range(4 * j, min(4 * j + 4, i + 1)):
                        mm = pe.transpose(PS[:, 3 + c % 3, 128 * (k % 4):128 * (k % 4) + 128], SR[i % 3][:, 128 * k:128 * k + 128], ident)
                    mm.then_inc(sem("t_mm"), 1)

                def weigh(i, j):
                    c = first[i] + j
                    pe.wait_ge(sem(f"t_ev{c % 2}"), b * (CH // 2) + c // 2 + 1)
                    if j == 0 and i >= 2:
                        pe.wait_ge(sem("o_ev"), b * NT + i - 1)
                    for k in range(4 * j, min(4 * j + 4, i + 1)):
                        mm = pe.matmul(PS[:, 6 + i % 2, 0:128], PTB[:, c % 3, 128 * (k % 4):128 * (k % 4) + 128], VV[:, k, :],
                                       start=(k == 0), stop=(k == i))
                    mm.then_inc(sem("w_mm"), 1)

                scores(0)
                scores(1)
                for i in range(NT):
                    if i + 2 < NT:
                        scores(i + 2)
                    pe.wait_ge(sem("exp_ready"), b * NT + i + 1)
                    turn(i, 0)
                    for j in range(blocks[i]):
                        if j + 1 < blocks[i]:
                            turn(i, j + 1)
                        weigh(i, j)

            def gate_bank(n):
                if n >= 4:
                    pe.wait_ge(sem(f"g_ev{n % 2}"), (n - 4) // 2 + 1)

            def logits(c):
                for h in range(2):
                    pe.wait_ge(sem(f"g_ev{h}"), c + 1)
                if c >= 2:
                    pe.wait_ge(sem("lg_ev"), c - 1)
                for h in range(2):
                    mm = pe.matmul(PS[64 * h:64 * h + 64, 4 + c % 2, :], gwT, XTS[(2 * c + h) % 4], start=True, stop=True)
                mm.then_inc(sem("lg_mm"), 1)

            for c in range(16):
                for h in range(2):
                    gate_bank(2 * c + h)
                    pe.wait_ge(sem(f"xn_ready{h}"), c + 1)
                    i = NT * (2 * (c // 8) + h) + 4 * (c % 8)
                    for j in range(4):
                        mm = pe.transpose(PS[:, (2 * c + h) % 4, 128 * j:128 * j + 128], U[:, i + j, :], ident)
                    mm.then_inc(sem("g_mm"), 1)
                if c >= 1:
                    logits(c - 1)
            logits(15)
            for q in range(2):
                pe.wait_ge(sem("gate_ready"), q + 1)
                for g in range(8):
                    gate_bank(32 + 8 * q + g)
                    for j in range(4):
                        mm = pe.transpose(PS[:, g % 4, 128 * j:128 * j + 128], LG[q][:, 512 * g + 128 * j:512 * g + 128 * j + 128], ident)
                    mm.then_inc(sem("g_mm"), 1)
                for h in range(2):
                    pe.wait_ge(sem(f"g_ev{h}"), 16 + 4 * q + 4)
                for b2 in range(2):
                    for t in range(NT):
                        mm = pe.matmul(PS[:, 6, 128 * q + 64 * b2:128 * q + 64 * b2 + 64], U[:, NT * (2 * q + b2) + t, :],
                                       MN[:, t, 64 * b2:64 * b2 + 64], start=(t == 0), stop=(t == NT - 1))
                mm.then_inc(sem("pool_mm"), 1)
                pe.wait_ge(sem("pool_ev"), q + 1)

            def hidden(g):
                pe.wait_ge(sem(f"ew_in{g % 4}"), 32 * (g // 4 + 1))
                if g >= 2:
                    pe.wait_ge(sem("h_ev"), g - 1)
                for e in range(EG):
                    for k in range(4):
                        mm = pe.matmul(PS[:, g % 2, 16 * e + 4 * k:16 * e + 4 * k + 4], W1B[:, g % 4, e, k:HID:4],
                                       poolT[:, :, EG * g + e], start=True, stop=True)
                mm.then_inc(sem("e1_mm"), 1)

            def result(g):
                pe.wait_ge(sem("hg_ready"), g + 1)
                if g >= 2:
                    pe.wait_ge(sem("ot_ev"), g - 1)
                for e in range(EG):
                    for k in range(4):
                        mm = pe.matmul(PS[:, 2 + g % 2, 4 * e:4 * e + 4], W2B[:, g % 4, e, k, :], HG[:, g % 2, 16 * e + 4 * k:16 * e + 4 * k + 4],
                                       start=(k == 0), stop=(k == 3))
                mm.then_inc(sem("e2_mm"), 1)

            hidden(0)
            for g in range(NG):
                if g + 1 < NG:
                    hidden(g + 1)
                result(g)
            pe.wait_ge(sem("ot_ev"), NG)
            for q in range(2):
                mm = pe.transpose(PS[:, 7, 128 * q:128 * q + 128], OT[:, 2 * q:2 * q + 2, :].rearrange("p b e -> p (b e)"), ident)
            mm.then_inc(sem("oe_mm"), 1)
            pe.wait_ge(sem("oe_ready"), 1)
            for g in range(8 * B):
                b = g // 8
                e = slice(64 * (b % 2), 64 * (b % 2) + 64)
                if g >= 4:
                    pe.wait_ge(sem("fin_ready"), g - 3)
                for j in range(4):
                    mm = pe.matmul(PS[:, g % 4, 128 * j:128 * j + 128], LG[b // 2][e, 512 * (g % 8) + 128 * j:512 * (g % 8) + 128 * j + 128],
                                   outE[e, b // 2, :], start=True, stop=True)
                mm.then_inc(sem("fin_mm"), 1)

        def pool_l1(pool):
            pool.wait_ge(sem("norm_ready"), 1)
            for b in range(B):
                tiles = slice(NT * b, NT * b + NT)
                if b >= 1:
                    pool.wait_ge(sem("pre_mm"), 32 * b - 24)
                pool.tensor_tensor(XB, U[:, tiles, :], tkr[:, tiles].unsqueeze(2).broadcast_to([128, NT, D]), ALU.mult).then_inc(sem("tokens_scaled"), 1)
                pool.wait_ge(sem("tokens_scaled"), b + 1)
                pool.tensor_tensor(XB, XB, tkn[:, tiles].unsqueeze(2).broadcast_to([128, NT, D]), ALU.add).then_inc(sem("tokens_ready"), 1)

        def scalar_l1(act):
            def root8():
                act.wait_ge(sem("var_ready"), 8 + root8.n)
                act.activation(WS[:, 1, :], WS[:, 3, :], ACT.Sqrt).then_inc(sem("root_ready"), 1)
                root8.n += 1
            root8.n = 0
            root8()
            with act.Fori(0, B) as b:
                for g in range(1, 32, 2):
                    k = g % 8
                    act.wait_ge(sem("pre_mm"), b * 32 + g + 1)
                    dst = (XT, QT, KT, V[:, 2 * TOK:3 * TOK])[g // 8][:, 512 * k:512 * k + 512]
                    act.activation(dst, PS[:, g % 4, :], ACT.Copy).then_inc(sem("pre_ev1"), 1)
                for i in range(NT):
                    act.wait_ge(sem("nm_ready"), b * NT + i + 1)
                    s = SR[i % 3][:, 0:128 * (i + 1)]
                    act.activation(s, s, ACT.Exp, scale=SCALE, bias=nmax[:, i % 3:i % 3 + 1],
                                   accum_out=rsum[:, i % 3:i % 3 + 1]).then_inc(sem("exp_ready"), 1)
                    for c in range(first[i], first[i] + blocks[i]):
                        if c % 2:
                            w = min(512, 128 * (i + 1) - 512 * (c - first[i]))
                            act.wait_ge(sem("t_mm"), b * CH + c + 1)
                            if c >= 3:
                                act.wait_ge(sem("w_mm"), b * CH + c - 2)
                            act.activation(PTB[:, c % 3, 0:w], PS[:, 3 + c % 3, 0:w], ACT.Copy).then_inc(sem("t_ev1"), 1)
            root8()
            act.wait_ge(sem("coef_ready"), 1)

            def norm_chunk(c):
                i = NT * (2 * (c // 8) + 1) + 4 * (c % 8)
                for j in range(i, i + 4):
                    ins = act.activation(U[:, j, :], U[:, j, :], ACT.Identity, scale=tkr[:, j:j + 1], bias=tkn[:, j:j + 1])
                ins.then_inc(sem("xn_ready1"), 1)

            def gate_exp(q):
                act.wait_ge(sem("gm_ready"), q + 1)
                act.activation(LG[q], LG[q], ACT.Exp, bias=gmx[:, q, 0:1], accum_out=gmx[:, q, 1:2]).then_inc(sem("gexp_ready"), 1)

            norm_chunk(0)
            for c in range(16):
                if c + 1 < 16:
                    norm_chunk(c + 1)
                act.wait_ge(sem("g_mm"), 2 * c + 2)
                if c >= 2:
                    act.wait_ge(sem("lg_mm"), c - 1)
                act.activation(XTS[(2 * c + 1) % 4], PS[:, (2 * c + 1) % 4, :], ACT.Copy).then_inc(sem("g_ev1"), 1)
                if c == 9:
                    gate_exp(0)
            gate_exp(1)
            for q in range(2):
                for g in range(1, 8, 2):
                    act.wait_ge(sem("g_mm"), 32 + 8 * q + g + 1)
                    if q:
                        act.wait_ge(sem("pool_mm"), 1)
                    act.activation(AF[1][:, 512 * g:512 * g + 512], PS[:, g % 4, :], ACT.Copy).then_inc(sem("g_ev1"), 1)
            for g in range(NG):
                act.wait_ge(sem("h_ev"), g + 1)
                if g >= 2:
                    act.wait_ge(sem("e2_mm"), g - 1)
                act.activation(HG[:, g % 2, :], HB[:, g % 2, :], ACT.Gelu).then_inc(sem("hg_ready"), 1)

        def vector_l1(dve, st, image_stats, row_moments):
            later = st.later

            def token_norm(ready):
                row_moments()
                m, e, v = WS[:, 0, :], WS[:, 1, :], WS[:, 3, :]
                later(dve.tensor_tensor(v, m, m, ALU.mult))
                later(dve.tensor_tensor(v, e, v, ALU.subtract))
                dve.tensor_scalar(v, v, EPS, None, ALU.add).then_inc(sem("var_ready"), 1)
                dve.wait_ge(sem("root_ready"), ready)
                later(dve.reciprocal(tkr, e))
                later(dve.scalar_tensor_tensor(tkn, m, -1.0, tkr, ALU.mult, ALU.mult))

            token_norm(8)
            dve.memset(lay[:, 2:3], 0.0).then_inc(sem("norm_ready"), 1)
            dve.wait_ge(sem("wt_mm"), 1)
            dve.tensor_copy(WT3.rearrange("p c h -> p (c h)"), PS[:, 0, 0:384])
            dve.tensor_copy(gwT, PS[:, 0, 384:384 + EX]).then_inc(sem("wt_ready"), 1)
            tick = lay[:, 0:1]
            later(dve.memset(tick, 0.0))
            dve.memset(tick, 0.0).then_inc(sem("l1_start"), 1)

            base = st.n
            with dve.Fori(0, B) as b:
                dve.memset(lay[:, 1:2], 0.0).then_inc(sem("batch_begun"), 1)
                for g in range(0, 32, 2):
                    k = g % 8
                    dve.wait_ge(sem("pre_mm"), b * 32 + g + 1)
                    dst = (XT, QT, KT, V[:, 2 * TOK:3 * TOK])[g // 8][:, 512 * k:512 * k + 512]
                    dve.tensor_copy(dst, PS[:, g % 4, :]).then_inc(sem("pre_ev0"), 1)

                def take_scores(i):
                    for j in range(blocks[i]):
                        c = first[i] + j
                        w = min(512, 128 * (i + 1) - 512 * j)
                        dve.wait_ge(sem("sc_mm"), b * CH + c + 1)
                        if i >= 3 and j == 0:
                            dve.wait_ge(sem("t_mm"), b * CH + first[i - 2])
                        dve.tensor_scalar(SR[i % 3][:, 512 * j:512 * j + w], PS[:, c % 3, 0:w], 1.0, -3e38, ALU.mult, ALU.max,
                                          accum_out=bmax[:, 8 * (i % 2) + j:8 * (i % 2) + j + 1]).then_inc(sem("sc_ev"), 1)
                    dve.wait_ge(sem("sc_ev"), b * CH + first[i] + blocks[i])
                    dve.tensor_reduce(mraw[:, i % 2:i % 2 + 1], bmax[:, 8 * (i % 2):8 * (i % 2) + blocks[i]], AX.X, ALU.max).then_inc(sem("mr_ready"), 1)
                    dve.wait_ge(sem("mr_ready"), b * NT + i + 1)
                    dve.tensor_scalar(nmax[:, i % 3:i % 3 + 1], mraw[:, i % 2:i % 2 + 1], -SCALE, None, ALU.mult).then_inc(sem("nm_ready"), 1)

                def finish(i):
                    dve.reciprocal(rden[:, i % 2:i % 2 + 1], rsum[:, i % 3:i % 3 + 1]).then_inc(sem("rd_ready"), 1)
                    dve.wait_ge(sem("rd_ready"), b * NT + i + 1)
                    dve.wait_ge(sem("w_mm"), b * CH + first[i] + blocks[i])
                    if i > 0:
                        dve.wait_ge(sem("o_ev"), b * NT + i)
                    dve.memset(tick, 0.0)
                    u = U[:, bass.ds(b * NT + i, 1), :]
                    dve.scalar_tensor_tensor(u, PS[:, 6 + i % 2, 0:128].unsqueeze(1), rden[:, i % 2:i % 2 + 1], u, ALU.mult, ALU.add).then_inc(sem("o_ev"), 1)
                    if i > 0:
                        dve.bn_stats(ST[:, bass.ds(b * NT + i - 1, 1), :], U[:, bass.ds(b * NT + i - 1, 1), :])

                take_scores(0)
                take_scores(1)
                for i in range(NT):
                    if i + 2 < NT:
                        take_scores(i + 2)
                    dve.wait_ge(sem("exp_ready"), b * NT + i + 1)
                    for c in range(first[i], first[i] + blocks[i]):
                        if c % 2 == 0:
                            w = min(512, 128 * (i + 1) - 512 * (c - first[i]))
                            dve.wait_ge(sem("t_mm"), b * CH + c + 1)
                            if c >= 3:
                                dve.wait_ge(sem("w_mm"), b * CH + c - 2)
                            dve.tensor_copy(PTB[:, c % 3, 0:w], PS[:, 3 + c % 3, 0:w]).then_inc(sem("t_ev0"), 1)
                    finish(i)
                dve.wait_ge(sem("o_ev"), b * NT + NT)
                dve.memset(tick, 0.0)
                dve.bn_stats(ST[:, bass.ds(b * NT + NT - 1, 1), :], U[:, bass.ds(b * NT + NT - 1, 1), :]).then_inc(sem("stats_done"), 1)

            dve.wait_ge(sem("stats_done"), B)
            token_norm(9)
            dve.memset(lay[:, 2:3], 0.0).then_inc(sem("coef_ready"), 1)

            def norm_chunk(c):
                i = NT * 2 * (c // 8) + 4 * (c % 8)
                for j in range(i, i + 4):
                    ins = dve.tensor_scalar(U[:, j, :], U[:, j, :], tkr[:, j:j + 1], tkn[:, j:j + 1], ALU.mult, ALU.add)
                ins.then_inc(sem("xn_ready0"), 1)

            def take_logits(c):
                dve.wait_ge(sem("lg_mm"), c + 1)
                dve.tensor_scalar(LG[c // 8][:, 512 * (c % 8):512 * (c % 8) + 512], PS[:, 4 + c % 2, :], gbs, -3e38, ALU.add, ALU.max,
                                  accum_out=bmax[:, c:c + 1]).then_inc(sem("lg_ev"), 1)
                if c % 8 == 7:
                    q = c // 8
                    dve.wait_ge(sem("lg_ev"), c + 1)
                    later(dve.tensor_reduce(gmx[:, q, 0:1], bmax[:, 8 * q:8 * q + 8], AX.X, ALU.max))
                    dve.tensor_scalar(gmx[:, q, 0:1], gmx[:, q, 0:1], -1.0, None, ALU.mult).then_inc(sem("gm_ready"), 1)

            norm_chunk(0)
            for c in range(16):
                if c + 1 < 16:
                    norm_chunk(c + 1)
                dve.wait_ge(sem("g_mm"), 2 * c + 1)
                if c >= 2:
                    dve.wait_ge(sem("lg_mm"), c - 1)
                dve.tensor_copy(XTS[2 * c % 4], PS[:, 2 * c % 4, :]).then_inc(sem("g_ev0"), 1)
                if c >= 1:
                    take_logits(c - 1)
            take_logits(15)
            for q in range(2):
                dve.wait_ge(sem("gexp_ready"), q + 1)
                later(dve.reciprocal(gmx[:, q, 2:3], gmx[:, q, 1:2]))
                later(dve.tensor_scalar(LG[q], LG[q], gmx[:, q, 2:3], None, ALU.mult))
                later(dve.max(top8, LG[q]))
                later(dve.match_replace(LR[q], top8, LG[q], 0.0))
                dve.tensor_tensor(LG[q], LG[q], LR[q], ALU.subtract).then_inc(sem("gate_ready"), 1)
                if q:
                    dve.wait_ge(sem("pool_mm"), 1)
                    dve.tensor_copy(poolT[:, 0:2, :].rearrange("p b e -> p (b e)"), PS[:, 6, 0:128]).then_inc(sem("pool_ev"), 1)
                for g in range(0, 8, 2):
                    dve.wait_ge(sem("g_mm"), 32 + 8 * q + g + 1)
                    dve.tensor_copy(AF[1][:, 512 * g:512 * g + 512], PS[:, g % 4, :]).then_inc(sem("g_ev0"), 1)
            dve.wait_ge(sem("pool_mm"), 2)
            dve.tensor_copy(poolT[:, 2:4, :].rearrange("p b e -> p (b e)"), PS[:, 6, 128:256]).then_inc(sem("pool_ev"), 1)
            dve.wait_ge(sem("b1_in"), 16)

            def take_result(g):
                dve.wait_ge(sem("e2_mm"), g + 1)
                dve.tensor_copy(OT[:, :, EG * g:EG * g + EG], PS[:, 2 + g % 2, 0:16].rearrange("p (e b) -> p b e", b=B)).then_inc(sem("ot_ev"), 1)

            for g in range(NG):
                dve.wait_ge(sem("e1_mm"), g + 1)
                if g >= 2:
                    dve.wait_ge(sem("hg_ready"), g - 1)
                dve.tensor_tensor(HB[:, g % 2, :].rearrange("p (x b) -> p x b", b=B), PS[:, g % 2, 0:64].rearrange("p (x b) -> p x b", b=B),
                                  B1T[:, EG * g:EG * g + EG, :].rearrange("p e k -> p (e k)").unsqueeze(2).broadcast_to([128, 16, B]),
                                  ALU.add).then_inc(sem("h_ev"), 1)
                if g >= 1:
                    take_result(g - 1)
                for j in range(8 * g, 8 * g + 8):
                    ins = dve.tensor_scalar(U[:, j, :], U[:, j, :], WS[:, 1, j:j + 1], WS[:, 0, j:j + 1], ALU.mult, ALU.add)
            ins.then_inc(sem("restored"), 1)
            take_result(NG - 1)
            dve.wait_ge(sem("oe_mm"), 1)
            dve.tensor_tensor(outE, PS[:, 7, 0:256].rearrange("p (q o) -> p q o", q=2), b2n.unsqueeze(1).broadcast_to([128, 2, D]),
                              ALU.add).then_inc(sem("oe_ready"), 1)
            dve.wait_ge(sem("restored"), 1)
            for g in range(8 * B):
                dve.wait_ge(sem("fin_mm"), g + 1)
                u = U[:, 4 * g:4 * g + 4, :]
                dve.tensor_tensor(u, u, PS[:, g % 4, :].rearrange("p (n w) -> p n w", w=W), ALU.add).then_inc(sem("fin_ready"), 1)

        def value_products(eng, k, bs, done):
            r = k // NQ
            nb = bs.stop - bs.start
            eng.wait_ge(sem(f"e_in{k % 3}"), 16 * (k // 3 + 1))
            if k % NQ == 0:
                eng.wait_ge(sem(f"xr_modes{r % 2}"), 64 * (r // 2 + 1))
            if k >= 2:
                eng.wait_ge(sem("v_mm"), k - 1)
            eng.tensor_tensor(YB[:, k % 2, bs].rearrange("p b k m -> p b (k m)"), XR[:, r % 2, bs].rearrange("p b k m -> p b (k m)"),
                              EB[:, k % 3].rearrange("p k m -> p (k m)").unsqueeze(1).broadcast_to([128, nb, 3 * MR]),
                              ALU.mult).then_inc(sem(done), 1)

        def score_products(eng, z):
            h, k = z // (4 * NLC), z // 4 % NLC
            xc, wc = ((0, 0), (1, 1), (1, 0), (0, 2))[z % 4]
            w = min(128, ML - 128 * k)
            if z >= 4:
                eng.wait_ge(sem("s_mm"), z - 3)
            eng.tensor_tensor(ZP[z % 4][0:w], XLT[0:w, xc, k, :].unsqueeze(1).broadcast_to([w, 16, N]),
                              CT[0:w, wc, k, 16 * h:16 * h + 16].unsqueeze(2).broadcast_to([w, 16, N]),
                              ALU.mult).then_inc(sem("zp_pool" if z % 4 == 3 else "zp_dve"), 1)

        def emptied(eng, what, g, rounds=0, groups=0):
            eng.wait_ge(sem(f"{what}{g % 2}"), rounds * ((groups + 1 - g % 2) // 2) + g // 2 + 1)

        def all_emptied(eng, what, rounds, groups):
            eng.wait_ge(sem(f"{what}0"), rounds * ((groups + 1) // 2))
            eng.wait_ge(sem(f"{what}1"), rounds * (groups // 2))

        def forward_evacs(eng, layer, mmsem, scale):
            odd = eng.engine == nc.scalar.engine
            for g in range(int(odd), NF2, 2):
                eng.wait_ge(sem(mmsem), max(layer - 1, 0) * NF2 + g + 1)
                n = 3 if g < NF2 - 1 else 2
                j0 = 1 if g == 0 else 0
                lo = 64 - (3 * g + 2)
                src = PS[:, g % 4, 0:396].rearrange("p (j s c x) -> p s c j x", j=3, s=2, c=2)
                for c in range(2):
                    for o, i in ((Zk[:, c, 3 * g:3 * g + n, :], src[:, 0, c, 0:n, :]),
                                 (Zk[:, c, lo:lo + 3 - j0, :], src[:, 1, c, 2:(0 if j0 else None):-1, :])):
                        if odd:
                            ins = nc.scalar.activation(o, i, ACT.Identity, scale=scale)
                        else:
                            ins = nc.vector.tensor_scalar(o, i, scale, None, ALU.mult)
                ins.then_inc(sem(f"f2_ev{int(odd)}"), 1)

        block = ctx.enter_context(nc.Block())

        @block.sync
        def _(sp):
            sp.dma_start(CST[:], io["consts"]).then_inc(sem("consts_in"), 16)
            for i in range(3):
                sp.dma_start(XN[:, i], x_nat[:, 8 * i:8 * i + 8, :]).then_inc(sem(f"xn_in{i}"), 16)
            sp.dma_start(V[0:NH, 0:2 * M], io["L0_conv_Pcw"].rearrange("n o k x c -> n (o k x c)")).then_inc(sem("w_in"), 16)
            for i, n in enumerate("QKV"):
                sp.dma_start(V[0:NH, 4224 + 1088 * i:4224 + 1088 * (i + 1)],
                             io[f"L0_conv_{n}cw"].rearrange("o n k x c -> n (o k x c)")).then_inc(sem("w_in"), 16)
            for i, n in enumerate("KQPV"):
                col = io[f"L0_conv_{n}sw"].rearrange("a n -> n a") if n == "P" else io[f"L0_conv_{n}sw"]
                row = io[f"L0_conv_{n}sw"] if n == "P" else io[f"L0_conv_{n}sw"].rearrange("n a -> a n")
                sp.dma_start(headc[0:NH, i:i + 1], col).then_inc(sem("w_in"), 16)
                sp.dma_start(headw[:, i, :], row.broadcast_to([128, NH])).then_inc(sem("w_in"), 16)
            for i, n in enumerate(PAR):
                src = io[f"L0_conv_{n}"]
                src = src if n.startswith("m") and n.endswith("sw") else src.unsqueeze(0)
                sp.dma_start(PAR[n], src.broadcast_to([128, 1])).then_inc(sem("w_in"), 16)
            for c in range(3, 16):
                sp.wait_ge(sem("f1_mm"), 2 * (c - 2))
                sp.wait_ge(sem("xsq"), c - 2)
                sp.dma_start(XN[:, c % 3], x_nat[:, 8 * c:8 * c + 8, :]).then_inc(sem(f"xn_in{c % 3}"), 16)
            sp.wait_ge(sem("e_ready"), 1)
            for q in range(3):
                sp.dma_start(e_dram[:, :, q, :].rearrange("r n m -> n r m"), P3[:, q, :].rearrange("p (r m) -> p r m", m=MR)
                             ).then_inc(sem("e_out"), 16)
            sp.wait_ge(sem("e_out"), 48)
            sp.wait_ge(sem("ct_mm"), 1)
            for i in range(4):
                sp.dma_start(V[:, 4096 * i:4096 * (i + 1)], x_img[:, 4096 * i:4096 * (i + 1)]).then_inc(sem(f"xi_in{i}"), 16)
            sp.wait_ge(sem("xs_ready"), 1)
            for q, src in enumerate((XS, Z[:, 0, :], Z[:, 1, :])):
                sp.dma_start(x_dram[:, :, q, :].rearrange("r n m -> n r m"), src.rearrange("p (r m) -> p r m", m=MR)
                             ).then_inc(sem("x_out"), 16)
            sp.wait_ge(sem("x_out"), 48)

            def load_modes(r):
                if r >= 2:
                    sp.wait_ge(sem("y_dve"), NQ * (r - 1))
                    sp.wait_ge(sem("y_pool"), NQ * (r - 1))
                for n in range(4):
                    sp.dma_start(XR[32 * n:32 * n + 32, r % 2].rearrange("p b k m -> p b (k m)"), x_dram[r].rearrange("(b s) k m -> s b (k m)", b=B)
                                 ).then_inc(sem(f"xr_modes{r % 2}"), 16)

            load_modes(0)
            load_modes(1)
            sp.wait_ge(sem("pbar_ready"), 1)
            for k in range(NR * NQ):
                r, g = divmod(k, NQ)
                if k >= 3:
                    sp.wait_ge(sem("y_dve"), k - 2)
                    sp.wait_ge(sem("y_pool"), k - 2)
                sp.dma_start(EB[:, k % 3].rearrange("p k m -> p (k m)"),
                             e_dram[r, 4 * g:4 * g + 4].rearrange("n k m -> n (k m)").unsqueeze(1).broadcast_to([4, 32, 3 * MR])
                             ).then_inc(sem(f"e_in{k % 3}"), 16)
                if g == 2 and 1 <= r < NR - 1:
                    load_modes(r + 1)
            for i, n in enumerate(("m0cw", "m1cw")):
                sp.wait_ge(sem("f2_mm_m"), NF2 * (i + 1))
                sp.dma_start(Af[:, 0:2 * M], io[f"L0_conv_{n}"].rearrange("a b k x c -> (a b) (k x c)")
                             .broadcast_to([128, 2 * M])).then_inc(sem("mw_in"), 16)
            sp.wait_ge(sem("tr_mm"), 3 * NTR)
            for k in range(16):
                if k >= 3:
                    sp.wait_ge(sem("x1_ready"), k - 2)
                sp.dma_start(AF[1][:, 1024 * (k % 3):1024 * (k % 3 + 1)].rearrange("p (i w) -> p i w", w=W),
                             x_nat[:, 8 * k:8 * k + 8, :]).then_inc(sem(f"xr_in{k % 3}"), 16)
            sp.wait_ge(sem("x1_ready"), 16)
            for i, n in enumerate("qkv"):
                sp.dma_start(WN3[:, i, :], io[f"L1_attn_W{n}"]).then_inc(sem("l1w_in"), 16)
            sp.dma_start(gwn, io["L1_ffn_gate_w"]).then_inc(sem("l1w_in"), 16)
            for h in range(2):
                sp.dma_start(b2n[EX * h:EX * h + EX], io["L1_ffn_weight2"][:, HID, :]).then_inc(sem("l1w_in"), 16)
            sync_l1(sp)

        @block.gpsimd
        def _(pool):
            pool.wait_ge(sem("rim_ready"), 1)
            rb = rim.unsqueeze(1).broadcast_to([128, 32, 128])
            cb = cim.unsqueeze(1).broadcast_to([128, 32, 128])
            for i in range(4):
                v = V[:, 4096 * i:4096 * (i + 1)].rearrange("p (h w) -> p h w", w=W)
                pool.wait_ge(sem(f"xi_in{i}"), 16)
                pool.tensor_tensor(v, v, rb, ALU.mult).then_inc(sem("xg_scaled"), 1)
                pool.wait_ge(sem("xg_scaled"), i + 1)
                pool.tensor_tensor(v, v, cb, ALU.add).then_inc(sem("xg_ready"), 1)
            pool.wait_ge(sem("xlt_ev"), 1)
            pool.wait_ge(sem("ct_ready"), 1)
            pool.wait_ge(sem("gram_mm"), 1)
            for z in range(3, 8 * NLC, 4):
                score_products(pool, z)
            for k in range(NR * NQ):
                value_products(pool, k, slice(B - 1, B), "y_pool")
            for k in range(16):
                pool.wait_ge(sem(f"xr_in{k % 3}"), 16 * (k // 3 + 1))
                pool.wait_ge(sem("o_ready"), 8 * (k + 1))
                u = U[:, 8 * k:8 * k + 8, :]
                pool.tensor_tensor(u, u, AF[1][:, 1024 * (k % 3):1024 * (k % 3 + 1)].rearrange("p (i w) -> p i w", w=W),
                                   ALU.add).then_inc(sem("x1_ready"), 1)
            pool_l1(pool)

        @block.tensor
        def _(pe):
            pe.wait_ge(sem("consts_in"), 16)

            def half_forward(layer, k, src, bank_evac):
                if k >= 4:
                    pe.wait_ge(sem(bank_evac), k - 3 + 32 * layer)
                for j in range(4):
                    mm = pe.matmul(PS[:, k % 4, 66 * j:66 * j + 66], src(j), cst["fh"], start=True, stop=True)
                mm.then_inc(sem("f1_mm"), 1)

            def forward(layer, mmsem):
                pe.wait_ge(sem("a_ready"), layer + 1)
                for g in range(NF2):
                    if g >= 4:
                        emptied(pe, "f2_ev", g - 4, layer, NF2)
                    for j in range(3):
                        ky = 3 * g + j
                        o = PS[:, g % 4, 132 * j:132 * j + 132]
                        pe.matmul(o, A[:, :, ky], cst["fwr"], start=True, stop=False)
                        mm = pe.matmul(o, A[:, :, KX + ky], cst["fwi"], start=False, stop=True)
                    mm.then_inc(sem(mmsem), 1)

            def inverse(layer):
                pe.wait_ge(sem("z_ready"), layer + 1)
                for g in range(NTR):
                    if g >= 4:
                        emptied(pe, "tr_ev", g - 4, layer, NTR)
                    for i in range(4 * g, min(4 * g + 4, 2 * KX)):
                        c, kx = divmod(i, KX)
                        mm = pe.matmul(PS[:, g % 4, 128 * (i % 4):128 * (i % 4) + 128], Zk[:, c:c + 2, :, kx], ident,
                                       is_transpose=True, start=True, stop=True)
                    mm.then_inc(sem("tr_mm"), 1)
                all_emptied(pe, "tr_ev", layer + 1, NTR)

                def rows(k):
                    if k >= 2:
                        pe.wait_ge(sem("i1_ev"), 32 * layer + k - 1)
                    for j in range(4):
                        mm = pe.matmul(PS[0:66, 4 + k % 2, 128 * j:128 * j + 128], A_modes[:, :, 4 * k + j], cst["ih"],
                                       start=True, stop=True)
                    mm.then_inc(sem("i1_mm"), 1)

                def columns(k):
                    pe.wait_ge(sem("i1_ev"), 32 * layer + k + 1)
                    if k >= 2:
                        pe.wait_ge(sem("i2_ev"), 32 * layer + k - 1)
                    for j in range(4):
                        mm = pe.matmul(PS[:, 6 + k % 2, 128 * j:128 * j + 128], DB[0:66, k % 3, 128 * j:128 * j + 128],
                                       cst["iw"][0:66, :], start=True, stop=True)
                    mm.then_inc(sem("i2_mm"), 1)

                rows(0)
                for k in range(NIM):
                    if k + 1 < NIM:
                        rows(k + 1)
                    columns(k)

            A_modes = Af.rearrange("p (c n) -> p c n", n=N)

            for c in range(16):
                pe.wait_ge(sem(f"xn_in{c % 3}"), 16 * (c // 3 + 1))
                for q in range(2):
                    half_forward(0, 2 * c + q, lambda j: XN[:, c % 3, 4 * q + j, :], "f1_ev")
                pe.wait_ge(sem("xsq"), c + 1)
                for j in range(8):
                    mm = pe.matmul(PS[:, 4, 8 * c + j:8 * c + j + 1], XQ[:, c % 2, j, :], ones[:, 0:1], start=True, stop=True)
                mm.then_inc(sem("sq_mm"), 1)
            pe.wait_ge(sem("c_ready"), 1)
            for c, src in enumerate((CR, CI)):
                for k in range(NLC):
                    w = min(128, ML - 128 * k)
                    mm = pe.transpose(PS[0:w, 5, 160 * c + 32 * k:160 * c + 32 * k + 32], src[:, 128 * k:128 * k + w], ident[0:NH, 0:NH])
            mm.then_inc(sem("ct_mm"), 1)
            pe.wait_ge(sem("g8_ready"), 1)
            pe.matmul(PS[:, 6, 0:8], cst["group"], G8, start=True, stop=True).then_inc(sem("g8_mm"), 1)
            pe.wait_ge(sem("rc_ready"), 1)
            pe.matmul(PS[:, 6, 16:17], SG[:, 4, :], ones[:, 0:1], start=True, stop=True)
            pe.matmul(PS[:, 6, 17:18], SG[:, 5, :], ones[:, 0:1], start=True, stop=True)
            pe.transpose(PS[:, 7, 0:128], SG[:, 6, :], ident)
            pe.transpose(PS[:, 7, 128:256], SG[:, 7, :], ident).then_inc(sem("is_mm"), 1)
            forward(0, "f2_mm_x")
            pe.wait_ge(sem("xe_ready"), 1)
            for g in range(9):
                if g >= 3:
                    pe.wait_ge(sem("xet_ev"), g - 2)
                for k in range(4 * g, min(4 * g + 4, 33)):
                    mm = pe.transpose(PS[:, g % 3, 128 * (k % 4):128 * (k % 4) + 128], Uf[:, 128 * k:128 * k + 128], ident)
                mm.then_inc(sem("xet_mm"), 1)
            pe.wait_ge(sem("xl_ready"), 1)
            pe.wait_ge(sem("rim_ready"), 1)
            for c in range(2):
                for k in range(NLC):
                    w = min(128, ML - 128 * k)
                    mm = pe.transpose(PS[0:w, (3, 4, 7)[(5 * c + k) // 4], 128 * ((5 * c + k) % 4):128 * ((5 * c + k) % 4) + 128],
                                      XL[:, c, 128 * k:128 * k + w], ident)
            mm.then_inc(sem("xlt_mm"), 1)
            pe.wait_ge(sem("xet_ev"), 9)
            for k in range(33):
                mm = pe.matmul(PS[:, 6, 0:128], XET[:, k, :], XET[:, k, :], start=(k == 0), stop=(k == 32))
            mm.then_inc(sem("gram_mm"), 1)
            pe.wait_ge(sem("xlt_ev"), 1)
            for z in range(8 * NLC):
                h, k, c = z // (4 * NLC), z // 4 % NLC, z % 4
                w = min(128, ML - 128 * k)
                pe.wait_ge(sem("zp_pool" if z % 4 == 3 else "zp_dve"), z // 4 + 1 if z % 4 == 3 else z - z // 4 + 1)
                for b in range(B):
                    s = slice(32 * b, 32 * b + 32)
                    mm = pe.matmul(PS[s, h, :], XLT[0:w, c // 2, k, s], ZP[z % 4][0:w, :, s],
                                   start=(k == 0 and c == 0), stop=(k == NLC - 1 and c == 3))
                mm.then_inc(sem("s_mm"), 1)
            pe.wait_ge(sem("p_ready"), 1)
            for g in range(NQ):
                mm = pe.transpose(PS[:, 2 + g // 4, 128 * (g % 4):128 * (g % 4) + 128],
                                  SE[:, 4 * g:4 * g + 4, :].rearrange("p n s -> p (n s)"), ident)
            mm.then_inc(sem("pt_mm"), 1)
            pe.wait_ge(sem("pb_ready"), 1)
            pe.transpose(PS[:, 6, 0:128], SG2, ident).then_inc(sem("mix_mm"), 1)
            pe.wait_ge(sem("pbt_ready"), 1)
            pe.matmul(PS[:, 7, 0:1], Pbt, beta, start=True, stop=True).then_inc(sem("mix_mm"), 1)
            pe.wait_ge(sem("pt_ev"), 2)
            for k in range(NR * NQ):
                r, g = divmod(k, NQ)
                if g == 0 and r >= 2:
                    pe.wait_ge(sem("zv_ev"), r - 1)
                pe.wait_ge(sem("y_dve"), k + 1)
                pe.wait_ge(sem("y_pool"), k + 1)
                for q in range(3):
                    for b in range(B):
                        s = slice(32 * b, 32 * b + 32)
                        mm = pe.matmul(PS[s, 3 * (r % 2) + q, 0:MR], PT[:, g, s], YB[:, k % 2, b, q, :],
                                       start=(g == 0), stop=(g == NQ - 1))
                mm.then_inc(sem("v_mm"), 1)
            pe.wait_ge(sem("mt_ready"), 1)
            pe.wait_ge(sem("xg_ready"), 4)
            xg = V[:].rearrange("p (h w) -> p h w", w=W)
            for g in range(32):
                if g >= 4:
                    emptied(pe, "mx_ev", g - 4)
                elif g == 0:
                    pe.wait_ge(sem("zv_ev"), NR)
                for j in range(4):
                    mm = pe.matmul(PS[:, g % 4, 128 * j:128 * j + 128], xg[:, :, 4 * g + j], Mt, start=True, stop=True)
                mm.then_inc(sem("mx_mm"), 1)
            all_emptied(pe, "mx_ev", 1, 32)
            inverse(0)
            pe.wait_ge(sem("mv_ready"), 1)
            pe.wait_ge(sem("i2_ev"), 32)
            pe.matmul(PS[:, 7, 0:256], ones, MV, start=True, stop=True).then_inc(sem("mv_mm"), 1)
            for layer in (1, 2):
                for k in range(32):
                    pe.wait_ge(sem("src_ready"), 32 * (layer - 1) + k + 1)
                    half_forward(layer, k, lambda j: Vn[:, 4 * k + j, :], "f1_ev")
                forward(layer, "f2_mm_m")
                inverse(layer)
            pe.wait_ge(sem("mv_ready"), 2)
            pe.matmul(PS[:, 0, 0:256], ones, MV, start=True, stop=True).then_inc(sem("mv_mm"), 1)
            tensor_l1(pe)


        @block.scalar
        def _(act):
            st = Steps(act, sem("act_step"))

            def root():
                root.n += 1
                act.wait_ge(sem("var_ready"), root.n)
                v = root_args[root.n - 1]
                act.activation(v, v, ACT.Sqrt).then_inc(sem("root_ready"), 1)
            root.n = 0

            for c in range(16):
                act.wait_ge(sem(f"xn_in{c % 3}"), 16 * (c // 3 + 1))
                if c >= 2:
                    act.wait_ge(sem("sq_mm"), c - 1)
                act.activation(XQ[:, c % 2], XN[:, c % 3], ACT.Square).then_inc(sem("xsq"), 1)
            root()
            root()

            act.wait_ge(sem("alpha_ready"), 1)
            forward_evacs(act, 0, "f2_mm_x", alpha)
            act.wait_ge(sem("x_beta"), 1)
            act.activation(XE, Z[:, 0:2, :], ACT.Copy, scale=float(np.sqrt(2.0))).then_inc(sem("xe_scaled"), 1)
            for g in range(9):
                act.wait_ge(sem("xet_mm"), g + 1)
                w = 512 if g < 8 else 128
                act.activation(Uf[:, 5376 + 512 * g:5376 + 512 * g + w], PS[:, g % 3, 0:w], ACT.Copy).then_inc(sem("xet_ev"), 1)
            act.wait_ge(sem("sd_ready"), 1)
            act.activation(SE, SD, ACT.Exp).then_inc(sem("se_ready"), 1)
            act.wait_ge(sem("pt_mm"), 1)
            for h in range(2):
                act.activation(PT[:, 4 * h:4 * h + 4, :].rearrange("p n s -> p (n s)"), PS[:, 2 + h, :], ACT.Copy).then_inc(sem("pt_ev"), 1)
            act.wait_ge(sem("x_out"), 48)
            for r in range(NR):
                act.wait_ge(sem("v_mm"), NQ * (r + 1))
                act.activation(Z[:, 2, MR * r:MR * r + MR], PS[:, 3 * (r % 2), 0:MR], ACT.Copy).then_inc(sem("k1_ready"), 1)
            Um = U[:].rearrange("p n w -> p w n")
            for g in range(1, 32, 2):
                act.wait_ge(sem("mx_mm"), g + 1)
                act.activation(Um[:, 4 * g:4 * g + 4, :], PS[:, g % 4, :].rearrange("p (w n) -> p w n", w=4), ACT.Copy).then_inc(sem("mx_ev1"), 1)

            def inverse_evacs(layer):
                for g in range(1, NTR, 2):
                    act.wait_ge(sem("tr_mm"), layer * NTR + g + 1)
                    act.activation(Af[:, 512 * g:512 * (g + 1)], PS[:, g % 4, :], ACT.Copy).then_inc(sem("tr_ev1"), 1)
                for k in range(NIM):
                    act.wait_ge(sem("i1_mm"), 32 * layer + k + 1)
                    if k >= 3:
                        act.wait_ge(sem("i2_mm"), 32 * layer + k - 2)
                    act.activation(DB[0:66, k % 3, :], PS[0:66, 4 + k % 2, :], ACT.Copy).then_inc(sem("i1_ev"), 1)
                    if layer == 1:
                        if k >= 1:
                            gelu(k - 1)
                if layer == 1:
                    gelu(NIM - 1)

            def gelu(k):
                act.wait_ge(sem("y1_ready"), k + 1)
                v = Vn[:, 4 * k:4 * k + 4, :]
                act.activation(v, v, ACT.Gelu).then_inc(sem("src_ready"), 1)

            inverse_evacs(0)
            root()
            root()
            for layer in (1, 2):
                act.wait_ge(sem("a_ready"), layer + 1)
                forward_evacs(act, layer, "f2_mm_m", 1.0)
                act.wait_ge(sem("yr_ready"), layer)
                act.activation(Af[:, 2 * M:3 * M], Z[:, 2, :], ACT.Square, accum_out=lay[:, 0:1]).then_inc(sem("vsum"), 1)
                act.wait_ge(sem("yi_ready"), layer)
                act.activation(Af[:, 3 * M:4 * M], Z[:, 1, :], ACT.Square, accum_out=lay[:, 1:2]).then_inc(sem("vsum"), 1)
                root()
                inverse_evacs(layer)
            root()
            act.wait_ge(sem("fin_coef"), 1)
            for i in range(N):
                act.activation(U[:, i, :], U[:, i, :], ACT.Identity, scale=WS[:, 4, i:i + 1], bias=WS[:, 6, i:i + 1]).then_inc(sem("ua_ready"), 1)
            scalar_l1(act)


        @block.vector
        def _(dve):
            st = Steps(dve, sem("dve_step"))
            later = st.later

            dve.wait_ge(sem("w_in"), 16 * (4 + 8 + 10))
            neg, pos = slice(33, 64), slice(31, 0, -1)
            later(dve.tensor_tensor(WP[:, neg, 0, 0], WP[:, neg, 0, 0], WP[:, pos, 0, 0], ALU.add))
            later(dve.tensor_tensor(WP[:, neg, 0, 1], WP[:, neg, 0, 1], WP[:, pos, 0, 1], ALU.subtract))
            later(dve.memset(WP[:, 1:32, 0, :], 0.0))
            later(dve.memset(WP[:, 0, 0, 1:2], 0.0))
            for w in range(3):
                q = QKV[:, w]
                later(dve.tensor_tensor(q[:, 17:32, 0, 0], q[:, 17:32, 0, 0], q[:, 15:0:-1, 0, 0], ALU.add))
                later(dve.tensor_tensor(q[:, 17:32, 0, 1], q[:, 17:32, 0, 1], q[:, 15:0:-1, 0, 1], ALU.subtract))
                later(dve.tensor_scalar(q[:, 16:32, 0, :], q[:, 16:32, 0, :], 0.5, None, ALU.mult))
                later(dve.memset(q[:, 1:16, 0, :], 0.0))
                later(dve.memset(q[:, 0, 0, 1:2], 0.0))
            ks, qs, psw, vs = (headc[0:NH, i:i + 1] for i in range(4))
            WPf = V[0:NH, 0:2 * M].rearrange("p (m c) -> p m c", c=2)
            P3k = P3.rearrange("p c (k x) -> p c k x", x=KX)
            for c in range(2):
                later(dve.tensor_scalar(P3[:, c, :], WPf[:, :, c], vs, None, ALU.mult))
            for h, (r0, q0) in enumerate(((0, 0), (48, 16))):
                wr, wi = WP[:, r0:r0 + 16, 0:LX, 0], WP[:, r0:r0 + 16, 0:LX, 1]
                vr, vi = QKV[:, 2, q0:q0 + 16, :, 0], QKV[:, 2, q0:q0 + 16, :, 1]
                t1 = T1[:, 0:272].rearrange("p (k x) -> p k x", x=LX)
                er, ei = (P3k[:, c, r0:r0 + 16, 0:LX] for c in range(2))
                later(dve.tensor_scalar(wr, wr, psw, None, ALU.add))
                if h:
                    later(dve.tensor_scalar(wr[:, :, 0:1], wr[:, :, 0:1], psw, None, ALU.add))
                for a, b, e, op in ((wr, vr, er, ALU.add), (wi, vi, er, ALU.subtract), (wr, vi, ei, ALU.add), (wi, vr, ei, ALU.add)):
                    later(dve.tensor_tensor(t1, a, b, ALU.mult))
                    later(dve.tensor_tensor(e, e, t1, op))
            later(dve.tensor_tensor(P3[:, 2, :], P3[:, 0, :], P3[:, 1, :], ALU.add))
            dve.tensor_tensor(P3[:, 1, :], P3[:, 1, :], P3[:, 0, :], ALU.subtract).then_inc(sem("e_ready"), 1)
            flat = V[0:NH, 4224:7488].rearrange("p (w m c) -> p w m c", w=3, c=2)
            ar, ai, br, bi = flat[:, 0, :, 0], flat[:, 0, :, 1], flat[:, 1, :, 0], flat[:, 1, :, 1]
            later(dve.tensor_tensor(CR, ar, br, ALU.mult))
            later(dve.scalar_tensor_tensor(CR, br, qs, CR, ALU.mult, ALU.add))
            later(dve.scalar_tensor_tensor(CR, ar, ks, CR, ALU.mult, ALU.add))
            later(dve.tensor_tensor(T1, ai, bi, ALU.mult))
            later(dve.tensor_tensor(CR, CR, T1, ALU.add))
            later(dve.scalar_tensor_tensor(CI, br, ks, ai, ALU.add, ALU.mult))
            later(dve.scalar_tensor_tensor(T1, ar, qs, bi, ALU.add, ALU.mult))
            later(dve.tensor_tensor(CI, CI, T1, ALU.subtract))
            for c in (CR, CI):
                later(dve.tensor_scalar(c, c, 128.0, None, ALU.mult))
                later(dve.tensor_scalar(c[:, 0:1], c[:, 0:1], 0.5, None, ALU.mult))
                later(dve.memset(c.rearrange("p (k x) -> p k x", x=LX)[:, 1:16, 0:1], 0.0))
            dve.memset(T2[:, 0:1], 0.0).then_inc(sem("c_ready"), 1)
            later(dve.scalar_tensor_tensor(qk, headw[:, 0, :], 64.0, headw[:, 1, :], ALU.mult, ALU.mult))
            later(dve.tensor_tensor(pv, headw[:, 2, :], headw[:, 3, :], ALU.mult))

            def half_evac(layer, k):
                dve.wait_ge(sem("f1_mm"), 32 * layer + k + 1)
                dve.tensor_copy(A[:, 4 * k:4 * k + 4, :].rearrange("p n k -> p (n k)"), PS[:, k % 4, 0:264]).then_inc(sem("f1_ev"), 1)

            for k in range(32):
                half_evac(0, k)
            dve.wait_ge(sem("sq_mm"), 16)
            dve.wait_ge(sem("f1_ev"), 32)
            m1, m2, Rx, Cx, mg, eg, Rf, Cf = (SG[:, i, :] for i in range(8))
            later(dve.tensor_copy(m1, A[:, :, 0]))
            later(dve.tensor_copy(m2, PS[:, 4, 0:128]))
            later(dve.tensor_reduce(G8[:, 0:4], m1.rearrange("p (b t) -> p b t", b=B), AX.X, ALU.add))
            dve.tensor_reduce(G8[:, 4:8], m2.rearrange("p (b t) -> p b t", b=B), AX.X, ALU.add).then_inc(sem("g8_ready"), 1)
            dve.wait_ge(sem("g8_mm"), 1)
            rv, mean, rr, cc = rc[:, 0:4], rc[:, 4:8], rc[:, 8:12], rc[:, 12:16]
            later(dve.tensor_copy(mean, PS[:, 6, 0:4]))
            later(dve.tensor_tensor(rv, mean, mean, ALU.mult))
            later(dve.tensor_tensor(rv, PS[:, 6, 4:8], rv, ALU.subtract))
            dve.tensor_scalar(rv, rv, EPS, None, ALU.add).then_inc(sem("var_ready"), 1)
            dve.wait_ge(sem("root_ready"), 1)
            later(dve.reciprocal(rr, rv))
            later(dve.scalar_tensor_tensor(cc, mean, -1.0, rr, ALU.mult, ALU.mult))
            bt = lambda a: a.rearrange("p (b t) -> p b t", b=B)
            rb, cb = rr.unsqueeze(2).broadcast_to([128, B, T]), cc.unsqueeze(2).broadcast_to([128, B, T])
            later(dve.tensor_copy(bt(Rf), rb))
            later(dve.tensor_copy(bt(Cf), cb))
            later(dve.tensor_tensor(mg, Rf, m1, ALU.mult))
            later(dve.tensor_tensor(mg, mg, Cf, ALU.add))
            later(dve.tensor_tensor(Rx, Rf, m2, ALU.mult))
            later(dve.scalar_tensor_tensor(Cx, Cf, 2.0, m1, ALU.mult, ALU.mult))
            later(dve.tensor_tensor(Rx, Rx, Cx, ALU.add))
            later(dve.tensor_tensor(Rx, Rx, Rf, ALU.mult))
            later(dve.tensor_tensor(Cx, Cf, Cf, ALU.mult))
            dve.tensor_tensor(eg, Rx, Cx, ALU.add).then_inc(sem("rc_ready"), 1)
            for b in range(B):
                a = A[:, T * b:T * b + T, :].rearrange("p n k -> p (n k)")
                later(dve.tensor_scalar(a, a, rr[:, b:b + 1], None, ALU.mult))
            for b in range(B):
                ins = dve.tensor_scalar(A[:, T * b:T * b + T, 0:1], A[:, T * b:T * b + T, 0:1], cc[:, b:b + 1], None, ALU.add)
            ins.then_inc(sem("a_ready"), 1)
            dve.wait_ge(sem("is_mm"), 1)
            later(dve.tensor_copy(rim, PS[:, 7, 0:128]))
            dve.tensor_copy(cim, PS[:, 7, 128:256]).then_inc(sem("rim_ready"), 1)
            later(dve.tensor_copy(istat[:, 0:2], PS[:, 6, 16:18]))
            later(dve.tensor_tensor(istat[:, 2:3], istat[:, 0:1], istat[:, 0:1], ALU.mult))
            later(dve.tensor_tensor(istat[:, 2:3], istat[:, 1:2], istat[:, 2:3], ALU.subtract))
            dve.tensor_scalar(istat[:, 2:3], istat[:, 2:3], EPS, None, ALU.add).then_inc(sem("var_ready"), 1)
            dve.wait_ge(sem("root_ready"), 2)
            later(dve.reciprocal(istat[:, 3:4], istat[:, 2:3]))
            later(dve.tensor_tensor(alpha, istat[:, 3:4], PAR["norm1_w"], ALU.mult))
            later(dve.tensor_tensor(beta, istat[:, 0:1], alpha, ALU.mult))
            dve.tensor_tensor(beta, PAR["norm1_b"], beta, ALU.subtract).then_inc(sem("alpha_ready"), 1)
            dve.wait_ge(sem("alpha_ready"), 1)

            forward_evacs(dve, 0, "f2_mm_x", alpha)
            all_emptied(dve, "f2_ev", 1, NF2)
            dve.tensor_tensor(Z[:, 0, 0:1], Z[:, 0, 0:1], beta, ALU.add).then_inc(sem("x_beta"), 1)
            dve.wait_ge(sem("x_beta"), 1)
            for c in range(2):
                for h in range(2):
                    ins = dve.tensor_copy(XL[:, c, 272 * h:272 * h + 272].rearrange("p (k x) -> p k x", x=LX),
                                          Zk[:, c, 48 * h:48 * h + 16, 0:LX])
            ins.then_inc(sem("xl_ready"), 1)
            dve.tensor_tensor(XS, Z[:, 0, :], Z[:, 1, :], ALU.add).then_inc(sem("xs_ready"), 1)
            dve.wait_ge(sem("xe_scaled"), 1)
            later(dve.tensor_tensor(XEk[:, 0, neg, 32], XEk[:, 0, neg, 32], XEk[:, 0, pos, 32], ALU.add))
            later(dve.tensor_tensor(XEk[:, 1, neg, 32], XEk[:, 1, neg, 32], XEk[:, 1, pos, 32], ALU.subtract))
            for c in range(2):
                later(dve.tensor_scalar(XEk[:, c, neg, 32], XEk[:, c, neg, 32], 0.5, None, ALU.mult))
                later(dve.memset(XEk[:, c, 1:32, 0:33:32], 0.0))
            later(dve.memset(XEk[:, 1, 0:33:32, 0:33:32], 0.0))
            dve.tensor_copy(XEk[:, 0, 0:33:32, 0:33:32], Zk[:, 0, 0:33:32, 0:33:32]).then_inc(sem("xe_ready"), 1)
            dve.wait_ge(sem("ct_mm"), 1)
            for k in range(NLC):
                w = min(128, ML - 128 * k)
                dve.tensor_copy(CT[0:w, 0, k, :], PS[0:w, 5, 32 * k:32 * k + 32])
                dve.tensor_copy(CT[0:w, 1, k, :], PS[0:w, 5, 160 + 32 * k:192 + 32 * k])
                later(dve.tensor_scalar(CT[0:w, 2, k, :], PS[0:w, 5, 160 + 32 * k:192 + 32 * k], -1.0, None, ALU.mult))
            dve.memset(lay[:, 0:1], 0.0).then_inc(sem("ct_ready"), 1)
            dve.wait_ge(sem("xlt_mm"), 1)
            for i in range(2 * NLC):
                w = 128 if i % NLC < NLC - 1 else ML - 128 * (NLC - 1)
                ins = dve.tensor_copy(XLT[0:w, i // NLC, i % NLC, :], PS[0:w, (3, 4, 7)[i // 4], 128 * (i % 4):128 * (i % 4) + 128])
            ins.then_inc(sem("xlt_ev"), 1)
            dve.wait_ge(sem("xlt_ev"), 1)
            dve.wait_ge(sem("gram_mm"), 1)
            for b in range(B):
                later(dve.tensor_copy(Gd[32 * b:32 * b + 32, :], PS[32 * b:32 * b + 32, 6, 32 * b:32 * b + 32]))

            for z in range(8 * NLC):
                if z % 4 < 3:
                    score_products(dve, z)
            qkb = qk.unsqueeze(2).broadcast_to([128, NH, T])
            later(dve.tensor_tensor(SE, qkb, Gd.unsqueeze(1).broadcast_to([128, NH, T]), ALU.mult))
            dve.wait_ge(sem("s_mm"), 8 * NLC)
            later(dve.tensor_tensor(SD, SE, PS[:, 0:2, :].rearrange("p h (n s) -> p (h n) s", s=T), ALU.add))
            later(dve.tensor_reduce(rmx, SD, AX.X, ALU.max))
            dve.tensor_tensor(SD, SD, rmx.unsqueeze(2).broadcast_to([128, NH, T]), ALU.subtract).then_inc(sem("sd_ready"), 1)
            dve.wait_ge(sem("se_ready"), 1)
            later(dve.tensor_reduce(rmx, SE, AX.X, ALU.add))
            later(dve.reciprocal(rmx, rmx))
            dve.tensor_tensor(SE, SE, rmx.unsqueeze(2).broadcast_to([128, NH, T]), ALU.mult).then_inc(sem("p_ready"), 1)
            dve.wait_ge(sem("p_ready"), 1)
            later(dve.tensor_tensor(SD, SE, pv.unsqueeze(2).broadcast_to([128, NH, T]), ALU.mult))
            later(dve.tensor_reduce(Pb, SD.rearrange("p n s -> p s n"), AX.X, ALU.add))
            later(dve.memset(SG2, 0.0))
            for b in range(B):
                s = slice(32 * b, 32 * b + 32)
                ins = dve.tensor_copy(SG2[s, s], Pb[s, :])
            ins.then_inc(sem("pb_ready"), 1)
            dve.wait_ge(sem("mix_mm"), 1)
            dve.tensor_copy(Pbt, PS[:, 6, 0:128]).then_inc(sem("pbt_ready"), 1)
            dve.wait_ge(sem("pbt_ready"), 1)
            dve.scalar_tensor_tensor(Mt, Pbt, alpha, ident, ALU.mult, ALU.add).then_inc(sem("mt_ready"), 1)
            dve.wait_ge(sem("mix_mm"), 2)
            dve.tensor_copy(istat[:, 0:1], PS[:, 7, 0:1]).then_inc(sem("pbar_ready"), 1)
            def value_sums(r):
                m = slice(MR * r, MR * r + MR)
                dve.wait_ge(sem("k1_ready"), r + 1)
                if r == 0:
                    dve.wait_ge(sem("x_out"), 48)
                dve.tensor_tensor(Z[:, 0, m], Z[:, 2, m], PS[:, 3 * (r % 2) + 2, 0:MR], ALU.subtract)
                later(dve.tensor_tensor(Z[:, 1, m], Z[:, 2, m], PS[:, 3 * (r % 2) + 1, 0:MR], ALU.add))
                dve.tensor_scalar(Z[:, 2, m], Z[:, 0, m], -1.0, None, ALU.mult).then_inc(sem("zv_ev"), 1)

            for k in range(NR * NQ):
                value_products(dve, k, slice(0, B - 1), "y_dve")
                if k % NQ == 1 and k > NQ:
                    value_sums(k // NQ - 1)
            value_sums(NR - 1)
            dve.wait_ge(sem("zv_ev"), NR)
            later(dve.tensor_tensor(Z[:, 0, 0:1], Z[:, 0, 0:1], istat[:, 0:1], ALU.add))
            dve.tensor_scalar(Z[:, 2, 0:1], Z[:, 0, 0:1], -1.0, None, ALU.mult).then_inc(sem("z_ready"), 1)
            Um = U[:].rearrange("p n w -> p w n")
            dve.wait_ge(sem("z_ready"), 1)
            for g in range(0, 32, 2):
                dve.wait_ge(sem("mx_mm"), g + 1)
                dve.tensor_copy(Um[:, 4 * g:4 * g + 4, :], PS[:, g % 4, :].rearrange("p (w n) -> p w n", w=4)).then_inc(sem("mx_ev0"), 1)

            def transposed_evacs(layer):
                for g in range(0, NTR, 2):
                    dve.wait_ge(sem("tr_mm"), layer * NTR + g + 1)
                    w = 512 if g < NTR - 1 else 256
                    dve.tensor_copy(Af[:, 512 * g:512 * g + w], PS[:, g % 4, 0:w]).then_inc(sem("tr_ev0"), 1)

            def image_stats(src, k):
                for j in range(4):
                    ins = dve.bn_stats(ST[:, 4 * k + j, :], src[:, 4 * k + j, :])
                return ins

            def row_moments():
                s = ST[:].rearrange("p n k -> p k n")
                t, m, e = WS[:, 2, :], WS[:, 0, :], WS[:, 1, :]
                later(dve.tensor_tensor(m, s[:, 1], s[:, 4], ALU.add))
                later(dve.tensor_scalar(m, m, 0.5, None, ALU.mult))
                later(dve.tensor_tensor(e, s[:, 2], s[:, 5], ALU.add))
                later(dve.tensor_scalar(e, e, 1.0 / 128, None, ALU.mult))
                for i in (1, 4):
                    later(dve.scalar_tensor_tensor(t, s[:, i], 0.5, s[:, i], ALU.mult, ALU.mult))
                    later(dve.tensor_tensor(e, e, t, ALU.add))

            all_emptied(dve, "mx_ev", 1, 32)
            transposed_evacs(0)
            for k in range(NIM):
                dve.wait_ge(sem("i2_mm"), k + 1)
                u = U[:, 4 * k:4 * k + 4, :]
                dve.tensor_tensor(u, u, PS[:, 6 + k % 2, :].rearrange("p (n w) -> p n w", w=W), ALU.add).then_inc(sem("i2_ev"), 1)
                if k >= 1:
                    dve.wait_ge(sem("i2_ev"), k)
                    image_stats(U, k - 1)
            dve.wait_ge(sem("i2_ev"), NIM)
            later(image_stats(U, NIM - 1))
            row_moments()
            dve.memset(lay[:, 0:1], 0.0).then_inc(sem("mv_ready"), 1)
            dve.wait_ge(sem("mv_mm"), 1)
            mu, e2, r, v = WS[:, 2, :], WS[:, 1, :], WS[:, 4, :], WS[:, 3, :]
            later(dve.tensor_copy(mu, PS[:, 7, 0:128]))
            later(dve.tensor_tensor(v, mu, mu, ALU.mult))
            later(dve.tensor_tensor(e2, PS[:, 7, 128:256], v, ALU.subtract))
            dve.tensor_scalar(v, e2, EPS, None, ALU.add).then_inc(sem("var_ready"), 1)
            dve.wait_ge(sem("root_ready"), 3)
            later(dve.reciprocal(r, v))
            later(dve.tensor_scalar(r, r, PAR["attn_w"], None, ALU.mult))
            later(dve.tensor_tensor(v, r, r, ALU.mult))
            v2, r2, b2 = WS[:, 5, :], WS[:, 6, :], WS[:, 7, :]
            later(dve.tensor_tensor(v2, v, e2, ALU.mult))
            dve.tensor_scalar(v2, v2, EPS, None, ALU.add).then_inc(sem("var_ready"), 1)
            dve.wait_ge(sem("root_ready"), 4)
            later(dve.reciprocal(r2, v2))
            later(dve.tensor_scalar(r2, r2, PAR["norm2_w"], None, ALU.mult))
            later(dve.tensor_tensor(r2, r2, r, ALU.mult))
            later(dve.tensor_tensor(b2, mu, r2, ALU.mult))
            later(dve.tensor_scalar(b2, b2, -1.0, PAR["norm2_b"], ALU.mult, ALU.add))
            later(dve.tensor_tensor(v2, mu, r, ALU.mult))
            later(dve.tensor_scalar(v2, v2, -1.0, PAR["attn_b"], ALU.mult, ALU.add))
            for k in range(NIM):
                for i in range(4 * k, 4 * k + 4):
                    ins = dve.tensor_scalar(Vn[:, i, :], U[:, i, :], WS[:, 6, i:i + 1], WS[:, 7, i:i + 1], ALU.mult, ALU.add)
                ins.then_inc(sem("src_ready"), 1)
                if k >= 2:
                    half_evac(1, k - 2)
            half_evac(1, NIM - 2)
            half_evac(1, NIM - 1)
            for layer in (1, 2):
                if layer == 2:
                    for k in range(NIM):
                        half_evac(2, k)
                dve.wait_ge(sem("f1_ev"), 32 * (layer + 1))
                dve.memset(lay[:, 4:5], 0.0).then_inc(sem("a_ready"), 1)
                forward_evacs(dve, layer, "f2_mm_m", 1.0)
                dve.wait_ge(sem("mw_in"), 16 * layer)
                wk = Af[:, 0:2 * M].rearrange("p (k x c) -> p k x c", k=KY, c=2)
                later(dve.tensor_tensor(wk[:, neg, 0, 0], wk[:, neg, 0, 0], wk[:, pos, 0, 0], ALU.add))
                later(dve.tensor_tensor(wk[:, neg, 0, 1], wk[:, neg, 0, 1], wk[:, pos, 0, 1], ALU.subtract))
                later(dve.memset(wk[:, 1:32, 0, :], 0.0))
                later(dve.memset(wk[:, 0, 0, 1:2], 0.0))
                all_emptied(dve, "f2_ev", layer + 1, NF2)
                wr = Af[:, 0:2 * M].rearrange("p (m c) -> p m c", c=2)
                t1, t2 = Af[:, 2 * M:3 * M], Af[:, 3 * M:4 * M]
                yr, yi = Z[:, 2, :], Z[:, 1, :]
                later(dve.tensor_tensor(yr, Z[:, 0, :], wr[:, :, 0], ALU.mult))
                later(dve.tensor_tensor(t1, Z[:, 1, :], wr[:, :, 1], ALU.mult))
                later(dve.tensor_tensor(t2, Z[:, 0, :], wr[:, :, 1], ALU.mult))
                later(dve.tensor_tensor(yr, yr, t1, ALU.subtract))
                later(dve.tensor_tensor(t1, Z[:, 1, :], wr[:, :, 0], ALU.mult))
                later(dve.tensor_tensor(yi, t1, t2, ALU.add))
                later(dve.memset(Z[:, 2, 0:1], 0.0))
                later(dve.memset(Z[:, 1, 0:1], 0.0))
                c0 = Zk[:, 1:3, :, 0]
                later(dve.tensor_tensor(DB[:, 0, 0:128].rearrange("p (c k) -> p c k", c=2), c0, c0, ALU.mult))
                later(dve.tensor_reduce(lay[:, 3:4], DB[:, 0, 0:128], AX.X, ALU.add))
                dve.memset(lay[:, 4:5], 0.0).then_inc(sem("yr_ready"), 1)
                dve.memset(lay[:, 5:6], 0.0).then_inc(sem("yi_ready"), 1)
                dve.wait_ge(sem("vsum"), 2 * layer)
                later(dve.tensor_tensor(lay[:, 2:3], lay[:, 0:1], lay[:, 1:2], ALU.add))
                later(dve.tensor_scalar(lay[:, 2:3], lay[:, 2:3], 2.0, EPS, ALU.mult, ALU.add))
                dve.scalar_tensor_tensor(lay[:, 2:3], lay[:, 3:4], -1.5, lay[:, 2:3], ALU.mult, ALU.add).then_inc(sem("var_ready"), 1)
                dve.wait_ge(sem("root_ready"), 4 + layer)
                later(dve.reciprocal(lay[:, 6:7], lay[:, 2:3]))
                later(dve.tensor_scalar(Z[:, 0, :], Z[:, 2, :], lay[:, 6:7], None, ALU.mult))
                later(dve.tensor_scalar(Z[:, 1, :], Z[:, 1, :], lay[:, 6:7], None, ALU.mult))
                dve.tensor_scalar(Z[:, 2, :], Z[:, 0, :], -1.0, None, ALU.mult).then_inc(sem("z_ready"), 1)
                transposed_evacs(layer)
                sw = PAR["m0sw"] if layer == 1 else PAR["m1sw"]
                for k in range(NIM):
                    dve.wait_ge(sem("i2_mm"), NIM * layer + k + 1)
                    v4 = Vn[:, 4 * k:4 * k + 4, :]
                    y = dve.scalar_tensor_tensor(v4, v4, sw, PS[:, 6 + k % 2, :].rearrange("p (n w) -> p n w", w=W), ALU.mult, ALU.add)
                    y.then_inc(sem("i2_ev"), 1)
                    if layer == 1:
                        dve.wait_ge(sem("i2_ev"), NIM * layer + k + 1)
                        dve.memset(lay[:, 7:8], 0.0).then_inc(sem("y1_ready"), 1)
                    elif k >= 1:
                        dve.wait_ge(sem("i2_ev"), NIM * layer + k)
                        image_stats(Vn, k - 1)
            dve.wait_ge(sem("i2_ev"), 3 * NIM)
            later(image_stats(Vn, NIM - 1))
            row_moments()
            dve.memset(lay[:, 0:1], 0.0).then_inc(sem("mv_ready"), 1)
            dve.wait_ge(sem("mv_mm"), 2)
            later(dve.tensor_copy(mu, PS[:, 0, 0:128]))
            later(dve.tensor_tensor(v, mu, mu, ALU.mult))
            later(dve.tensor_tensor(e2, PS[:, 0, 128:256], v, ALU.subtract))
            dve.tensor_scalar(v, e2, EPS, None, ALU.add).then_inc(sem("var_ready"), 1)
            dve.wait_ge(sem("root_ready"), 7)
            later(dve.reciprocal(v, v))
            later(dve.tensor_scalar(v, v, PAR["mon_w"], None, ALU.mult))
            later(dve.tensor_tensor(b2, mu, v, ALU.mult))
            later(dve.tensor_scalar(b2, b2, -1.0, PAR["mon_b"], ALU.mult, ALU.add))
            dve.tensor_tensor(r2, v2, b2, ALU.add).then_inc(sem("fin_coef"), 1)
            for i in range(N + 24):
                if i < N:
                    dve.wait_ge(sem("ua_ready"), i + 1)
                    dve.scalar_tensor_tensor(U[:, i, :], Vn[:, i, :], WS[:, 3, i:i + 1], U[:, i, :], ALU.mult, ALU.add).then_inc(sem("o_ready"), 1)
                if i >= 24 and i % 4 == 3:
                    k = (i - 24) // 4
                    dve.wait_ge(sem("x1_ready"), k // 2 + 1)
                    ins = image_stats(U, k)
            later(ins)
            vector_l1(dve, st, image_stats, row_moments)




_INS = ['x', 'L0_conv_norm1_w', 'L0_conv_norm1_b', 'L0_conv_Kcw', 'L0_conv_Ksw', 'L0_conv_Qcw', 'L0_conv_Qsw', 'L0_conv_Vcw',
        'L0_conv_Vsw', 'L0_conv_Pcw', 'L0_conv_Psw', 'L0_conv_attn_w', 'L0_conv_attn_b', 'L0_conv_norm2_w', 'L0_conv_norm2_b',
        'L0_conv_m0cw', 'L0_conv_m0sw', 'L0_conv_m1cw', 'L0_conv_m1sw', 'L0_conv_mon_w', 'L0_conv_mon_b', 'L1_attn_Wq',
        'L1_attn_Wk', 'L1_attn_Wv', 'L1_ffn_gate_w', 'L1_ffn_gate_b', 'L1_ffn_weight1', 'L1_ffn_weight2']


def kernel(**inputs):
    import numpy as _np
    import concourse.bacc as _bacc
    from concourse.bass_utils import run_bass_kernel_spmd as _run

    nc = _bacc.Bacc("TRN2", target_bir_lowering=False, num_devices=1)
    arrays, io = {}, {}
    for name in _INS:
        a = _np.ascontiguousarray(inputs[name])
        arrays[f"in_{name}"] = a
        io[name] = nc.dram_tensor(f"in_{name}", a.shape, mybir.dt.from_np(a.dtype), kind="ExternalInput").ap()
    c = shape_constants()
    arrays["in_consts"] = c
    io["consts"] = nc.dram_tensor("in_consts", c.shape, F32, kind="ExternalInput").ap()
    out = nc.dram_tensor("out_0", (B, T, H, W), F32, kind="ExternalOutput").ap()
    conv_attn_hybrid(nc, io, out)
    r = _run(nc, [arrays], core_ids=[0])
    return r.results[0]["out_0"]
```

```python
import numpy as np
import concourse.bass as bass
from concourse import mybir
from contextlib import ExitStack

F32 = mybir.dt.float32
F16 = mybir.dt.float16
BF16 = mybir.dt.bfloat16
ALU = mybir.AluOpType
ACT = mybir.ActivationFunctionType
AX = mybir.AxisListType

B, T, H, W = 4, 32, 128, 128
N = B * T
NH = 32
KY, KX = 64, 33
M = KY * KX
LK, LX = 32, 17
ML = LK * LX
NLC = -(-ML // 128)
NR = 6
MR = M // NR
NQ = 8
GW, GE = 4, 16384
EPS = 1e-5
TOK = H * T
NT = T
D = W
EX, HID, TOPK = 64, 512, 8
EG = 4
NEG = -1e30
SCALE = float(D) ** -0.5
QUP, KUP = 16.0, 1024.0

CONST_LAYOUT = [("ident", 128), ("ones", 128), ("group", 128), ("mask", 128), ("fh", 66), ("fwr", 132), ("fwi", 132),
                ("ih", 128), ("iw", 128)]


def shape_constants():
    ky = np.concatenate([np.arange(32), np.arange(-32, 0)])
    kx = np.arange(KX)
    p = np.arange(128)
    c = {}
    c["ident"] = np.eye(128)
    c["ones"] = np.full((128, 128), 1.0 / 128)
    c["group"] = (p[:, None] // GW == p[None, :] // GW) / float(GW * T)
    c["mask"] = np.where(p[None, :] > p[:, None], NEG, 0.0)
    a = 2 * np.pi * np.outer(p, kx) / 128
    c["fh"] = np.concatenate([np.cos(a), -np.sin(a)], 1) / 128
    co, si = np.cos(a) / 128, np.sin(a) / 128
    c["fwr"] = np.concatenate([co, -si, co, -si], 1)
    c["fwi"] = np.concatenate([si, co, -si, -co], 1)
    b = 2 * np.pi * np.outer(ky, p) / 128
    c["ih"] = np.concatenate([np.cos(b), -np.sin(b)], 0)
    twice = np.where(kx == 0, 1.0, 2.0)[:, None]
    a = 2 * np.pi * np.outer(kx, p) / 128
    iw = np.zeros((128, 128))
    iw[0:2 * KX] = np.concatenate([twice * np.cos(a), -twice * np.sin(a)], 0)
    c["iw"] = iw
    return np.concatenate([c[n] for n, _ in CONST_LAYOUT], 1).astype(np.float32)


class Steps:

    def __init__(self, eng, sem):
        self.eng, self.sem, self.base, self.n = eng, sem, 0, 0

    def later(self, ins):
        self.n += 1
        ins.then_inc(self.sem, 1)
        self.eng.wait_ge(self.sem, self.base + self.n)


def conv_attn_hybrid(nc, io, out):
    with ExitStack() as ctx:
        def sb(name, shape):
            return ctx.enter_context(nc.sbuf_tensor(name, shape, F32))

        sems = {}

        def sem(name):
            if name not in sems:
                sems[name] = ctx.enter_context(nc.semaphore(name))
            return sems[name]

        CW = sum(w for _, w in CONST_LAYOUT)
        U = sb("U", [128, N, W])
        V = sb("V", [128, 128 * 128])
        A = sb("A", [128, N, 2 * KX])
        Z = sb("Z", [128, 3, M])
        DB = sb("DB", [128, 3, 512])
        CST = sb("CST", [128, CW])
        ST = sb("ST", [128, N, 6])
        MI = sb("MI", [128, 2128])
        PS = ctx.enter_context(nc.psum_tensor("PS", [128, 8, 512], F32))
        e_dram = nc.dram_tensor("e_planes", (NR, NH, 3, MR), F32, kind="Internal").ap()
        x_dram = nc.dram_tensor("x_planes", (NR, N, 3, MR), F32, kind="Internal").ap()

        cst, o = {}, 0
        for name, w in CONST_LAYOUT:
            cst[name] = CST[:, o:o + w]
            o += w
        ident, ones = cst["ident"], cst["ones"]
        fh_at = sum(w for n, w in CONST_LAYOUT[:[n for n, _ in CONST_LAYOUT].index("fh")])
        fh_wide = CST[:, fh_at:fh_at + 128]
        Uf = U[:].rearrange("p n w -> p (n w)")
        Af = A[:].rearrange("p n k -> p (n k)")
        Vn = V[:].rearrange("p (n w) -> p n w", w=W)
        Zk = Z[:].rearrange("p c (k x) -> p c k x", x=KX)

        at = [0]

        def mi(width):
            at[0] += width
            assert at[0] <= 2128
            return MI[:, at[0] - width:at[0]]

        CT = mi(3 * NLC * NH).rearrange("p (c k n) -> p c k n", c=3, k=NLC)
        headw = mi(4 * NH).rearrange("p (c n) -> p c n", c=4)
        headc = mi(4)
        par = mi(12)
        PAR = {n: par[:, i:i + 1] for i, n in enumerate(
            ["norm1_w", "norm1_b", "attn_w", "attn_b", "norm2_w", "norm2_b", "mon_w", "mon_b", "m0sw", "m1sw"])}
        rim, cim = mi(128), mi(128)
        alpha, beta, istat = mi(1), mi(1), mi(4)
        Gd = mi(32)
        Pb = mi(32)
        qk = mi(NH)
        pv = mi(NH)
        G8, rc = mi(8), mi(16)
        Pbt, Mt = (ST[:].rearrange("p n k -> p (n k)")[:, 128 * i:128 * i + 128] for i in range(2))
        rmx = mi(NH)
        lay = mi(8)
        WS = mi(8 * 128).rearrange("p (k n) -> p k n", k=8)

        XN = Uf[:, 0:3072].rearrange("p (c i w) -> p c i w", c=3, i=8)
        XQ = Uf[:, 3072:5120].rearrange("p (c i w) -> p c i w", c=2, i=8)
        XE = Uf[:, 0:2 * M].rearrange("p (c m) -> p c m", c=2)
        XEk = Uf[:, 0:2 * M].rearrange("p (c k x) -> p c k x", c=2, x=KX)
        XL = Uf[:, 4224:5312].rearrange("p (c m) -> p c m", c=2)
        XET = Uf[:, 5376:9600].rearrange("p (k n) -> p k n", n=N)
        XLT = Uf[:, 9600:10880].rearrange("p (c k n) -> p c k n", c=2, k=NLC)
        ZP = [Uf[:, o:o + 2048].rearrange("p (n s) -> p n s", n=16) for o in (0, 2048, 5376, 7424)]
        SD = Uf[:, 12928:13952].rearrange("p (n s) -> p n s", n=NH)
        SE = Uf[:, 13952:14976].rearrange("p (n s) -> p n s", n=NH)
        PT = Uf[:, 8448:9472].rearrange("p (g s) -> p g s", g=NQ)
        EB = Uf[:, 9600:12768].rearrange("p (c k m) -> p c k m", c=3, k=3)
        YB = Uf[:, 0:8448].rearrange("p (c b k m) -> p c b k m", c=2, b=B, k=3)
        XR = Af.rearrange("p (c b k m) -> p c b k m", c=2, b=B, k=3)
        SG = Uf[:, 10880:12928].rearrange("p (k n) -> p k n", n=128)
        SG2 = SG[:, 0, :]
        MV = WS[:, 0:2, :].rearrange("p k n -> p (k n)")
        root_args = [rc[:, 0:4], istat[:, 2:3], WS[:, 3, :], WS[:, 5, :], lay[:, 2:3], lay[:, 2:3], WS[:, 3, :]]
        XS = Af[:, 0:M]

        WP = V[0:NH, 0:2 * M].rearrange("p (k x c) -> p k x c", k=KY, c=2)
        QKV = V[0:NH, 4224:7488].rearrange("p (w k x c) -> p w k x c", w=3, k=LK, c=2)
        P3 = V[0:NH, 7488:13824].rearrange("p (k m) -> p k m", k=3)
        CR = V[0:NH, 13824:14368]
        CI = V[0:NH, 14368:14912]
        T1 = V[0:NH, 14912:15456]
        T2 = V[0:NH, 15456:16000]

        x_nat = io["x"].rearrange("b t h w -> h (b t) w")
        x_img = io["x"].rearrange("b t h w -> (b t) (h w)")
        out_nat = out.rearrange("b t h w -> h (b t) w")

        QH, QL = (V[:, 0:TOK].bitcast(F16)[:, TOK * i:TOK * i + TOK] for i in range(2))
        KH, KL = (V[:, TOK:2 * TOK].bitcast(F16)[:, TOK * i:TOK * i + TOK] for i in range(2))
        ident16, mask16 = (WS[:, 4, 64 * i:64 * i + 64].bitcast(BF16) for i in range(2))
        VV = V[:, 2 * TOK:3 * TOK].rearrange("p (t d) -> p t d", d=D)
        XT = V[:, 3 * TOK:4 * TOK]
        AF = [Af, Z[:].rearrange("p c m -> p (c m)")]
        SR = [Af[:, 0:TOK], Af[:, TOK:2 * TOK], XT]
        XB = AF[1][:, 0:TOK].rearrange("p (t d) -> p t d", d=D)
        WT2 = AF[1][:, 4096:4096 + 256].rearrange("p (c h) -> p c h", c=2)
        WN3 = AF[1][:, 4480:4864].rearrange("p (c h) -> p c h", c=3)
        PTB = DB
        bmax = AF[1][:, 4864:4880]
        mraw, rden = AF[1][:, 4880:4882], AF[1][:, 4882:4884]
        nmax, rsum = AF[1][:, 4892:4895], AF[1][:, 5346:5350]
        gmx = AF[1][:, 4884:4892].rearrange("p (q k) -> p q k", q=2)
        tkr = AF[1][:, 4896:5024]
        tkn = AF[1][:, 5024:5152]
        gwT = AF[1][:, 5152:5216]
        gwn = AF[1][0:EX, 5216:5344]
        gbs = AF[1][:, 5344:5345]
        top8 = AF[1][:, 5352:5360]
        stf = ST[:].rearrange("p n k -> p (n k)")
        poolT = stf[:, 0:EX * B + 28]
        b2n = AF[1][:, 5616:5744]
        outE = AF[1][:, 5744:6256].rearrange("p (q b o) -> p q b o", q=2, b=2)

        NF2, NTR, NIM = 11, 17, 32
        CH = NT * (NT // 4 + 1) // 2

        blocks = [i // 4 + 1 for i in range(NT)]
        first = [sum(blocks[:i]) for i in range(NT)]
        XTS = [DB[:, 0, :], DB[:, 1, :], DB[:, 2, :], stf[:, 0:512]]
        LG = [Af[:, 0:TOK], Af[:, TOK:2 * TOK]]
        LR = [AF[1][:, 0:TOK], V[:, 3 * TOK:4 * TOK]]
        MN = AF[1][:, 0:TOK].rearrange("p (t e) -> p t e", e=2 * EX)
        VG = V[:].rearrange("p (c k x) -> p c k x", c=4, k=2)
        W1B = VG[:, :, 0, :].rearrange("p c (e h) -> p c e h", e=EG)
        W2B = VG[:, :, 1, :].rearrange("p c (e k o) -> p c e k o", e=EG, k=4)
        B1T = MI[:, 0:EX * 4].rearrange("p (e k) -> p e k", k=4)
        HB = WS[:, 2, :].rearrange("p (c x) -> p c x", c=2)
        HG = [WS[:, 3, 0:96], WS[:, 6, 0:96]]
        OT = WS[:, 4:6, :].rearrange("p k n -> p (k n)").rearrange("p (b e) -> p b e", b=B)
        HP = [DB[:, 0, :], DB[:, 1, :]]
        RB = [DB[:, 2, 0:D], DB[:, 2, D:2 * D]]
        NG = EX // EG

        def sync_l1(sp):
            for b2 in range(2):
                sp.dma_start(gbs[EX * b2:EX * b2 + EX], io["L1_ffn_gate_b"].unsqueeze(1)).then_inc(sem("l1w_in"), 16)
            sp.wait_ge(sem("l1_start"), 1)
            sp.dma_start(B1T, io["L1_ffn_weight1"][:, D, :].rearrange("e (p k) -> p e k", k=4)).then_inc(sem("b1_in"), 16)
            sp.wait_ge(sem("w_mm"), B * CH)
            for g in range(NG):
                if g == 3:
                    sp.wait_ge(sem("gate_ready"), 2)
                if g >= 4:
                    sp.wait_ge(sem("e2_mm"), g - 3)
                e = slice(EG * g, EG * g + EG)
                sp.dma_start(W1B[:, g % 4], io["L1_ffn_weight1"][e, 0:D, :].rearrange("e d h -> d e h")).then_inc(sem(f"ew_in{g % 4}"), 16)
                sp.dma_start(W2B[:, g % 4].rearrange("p e k o -> p e (k o)"),
                             io["L1_ffn_weight2"][e, 0:HID, :].rearrange("e (p k) o -> p e (k o)", k=4)).then_inc(sem(f"ew_in{g % 4}"), 16)
            for s in range(8):
                sp.wait_ge(sem("fin_ready"), 4 * s + 4)
                for b in range(2 * (s // 4), 2 * (s // 4) + 2):
                    i = T * b + 8 * (s % 4)
                    sp.dma_start(out_nat[:, i:i + 8, :], U[:, i:i + 8, :]).then_inc(sem("out_done"), 16)
            sp.wait_ge(sem("out_done"), 16 * 4 * B)

        def tensor_l1(pe):
            pe.wait_ge(sem("l1w_in"), 16 * 8)
            pe.wait_ge(sem("x1_ready"), NIM)
            pe.matmul(PS[:, 0, 0:128], WN3[:, 0, :], WN3[:, 1, :], start=True, stop=True)
            pe.transpose(PS[:, 0, 128:256], WN3[:, 2, :], ident)
            pe.transpose(PS[:, 0, 384:384 + EX], gwn, ident[0:EX, 0:EX]).then_inc(sem("wt_mm"), 1)
            pe.wait_ge(sem("wt_ready"), 1)

            with pe.Fori(0, B) as b:
                pe.wait_ge(sem("tokens_ready"), b + 1)
                pe.wait_ge(sem("batch_begun"), b + 1)
                for g in range(24):
                    f = g - 4
                    if 8 <= f < 16:
                        pe.wait_ge(sem("lo_ready"), b * 16 + f - 7)
                    elif f >= 0:
                        pe.wait_ge(sem(f"pre_ev{f % 2}"), b * 8 + (f // 2 + 1 if f < 8 else (f - 16) // 2 + 5))
                    if g == 8:
                        pe.wait_ge(sem("pre_ev0"), b * 8 + 4)
                        pe.wait_ge(sem("pre_ev1"), b * 8 + 4)
                    o = PS[:, g % 4, :]
                    k = g % 8
                    if g < 8:
                        for j in range(4):
                            mm = pe.transpose(o[:, 128 * j:128 * j + 128], XB[:, 4 * k + j, :], ident)
                    elif g < 16:
                        mm = pe.matmul(o, WT2[:, 0, :], XT[:, 512 * k:512 * k + 512], start=True, stop=True)
                    else:
                        for j in range(4):
                            mm = pe.matmul(o[:, 128 * j:128 * j + 128], XT[:, 512 * k + 128 * j:512 * k + 128 * j + 128],
                                           WT2[:, 1, :], start=True, stop=True)
                    mm.then_inc(sem("pre_mm"), 1)
                pe.wait_ge(sem("pre_ev0"), b * 8 + 8)
                pe.wait_ge(sem("pre_ev1"), b * 8 + 8)
                pe.wait_ge(sem("lo_ready"), b * 16 + 16)

                def scores(i):
                    for j in range(blocks[i]):
                        c = first[i] + j
                        w = min(512, 128 * (i + 1) - 512 * j)
                        if c >= 3:
                            pe.wait_ge(sem("sc_ev"), b * CH + c - 2)
                        last = j == blocks[i] - 1
                        for q, k in ((QH, KH), (QH, KL), (QL, KH)):
                            mm = pe.matmul(PS[:, c % 3, 0:w], q[:, 128 * i:128 * i + 128], k[:, 512 * j:512 * j + w],
                                           start=q is QH and k is KH, stop=q is QL and not last)
                        if last:
                            mm = pe.matmul(PS[:, c % 3, w - 128:w], ident16, mask16, start=False, stop=True)
                        mm.then_inc(sem("sc_mm"), 1)

                def turn(i, j):
                    c = first[i] + j
                    if c >= 3:
                        pe.wait_ge(sem(f"t_ev{(c - 3) % 2}"), b * (CH // 2) + (c - 3) // 2 + 1)
                    for k in range(4 * j, min(4 * j + 4, i + 1)):
                        mm = pe.transpose(PS[:, 3 + c % 3, 128 * (k % 4):128 * (k % 4) + 128], SR[i % 3][:, 128 * k:128 * k + 128], ident)
                    mm.then_inc(sem("t_mm"), 1)

                def weigh(i, j):
                    c = first[i] + j
                    pe.wait_ge(sem(f"t_ev{c % 2}"), b * (CH // 2) + c // 2 + 1)
                    if j == 0 and i >= 2:
                        pe.wait_ge(sem("o_ev"), b * NT + i - 1)
                    for k in range(4 * j, min(4 * j + 4, i + 1)):
                        mm = pe.matmul(PS[:, 6 + i % 2, 0:128], PTB[:, c % 3, 128 * (k % 4):128 * (k % 4) + 128], VV[:, k, :],
                                       start=(k == 0), stop=(k == i))
                    mm.then_inc(sem("w_mm"), 1)

                scores(0)
                scores(1)
                for i in range(NT):
                    pe.wait_ge(sem("exp_ready"), b * NT + i + 1)
                    turn(i, 0)
                    if i + 2 < NT:
                        scores(i + 2)
                    if i > 0:
                        weigh(i - 1, blocks[i - 1] - 1)
                    for j in range(1, blocks[i]):
                        turn(i, j)
                        weigh(i, j - 1)
                weigh(NT - 1, blocks[NT - 1] - 1)

            def gate_bank(n):
                if n >= 4:
                    pe.wait_ge(sem(f"g_ev{n % 2}"), (n - 4) // 2 + 1)

            def logits(c):
                for h in range(2):
                    pe.wait_ge(sem(f"g_ev{h}"), c + 1)
                if c >= 2:
                    pe.wait_ge(sem("lg_ev"), c - 1)
                for h in range(2):
                    mm = pe.matmul(PS[64 * h:64 * h + 64, 4 + c % 2, :], gwT, XTS[(2 * c + h) % 4], start=True, stop=True)
                mm.then_inc(sem("lg_mm"), 1)

            for c in range(16):
                for h in range(2):
                    gate_bank(2 * c + h)
                    pe.wait_ge(sem(f"xn_ready{h}"), c + 1)
                    i = NT * (2 * (c // 8) + h) + 4 * (c % 8)
                    for j in range(4):
                        mm = pe.transpose(PS[:, (2 * c + h) % 4, 128 * j:128 * j + 128], U[:, i + j, :], ident)
                    mm.then_inc(sem("g_mm"), 1)
                if c >= 1:
                    logits(c - 1)
            logits(15)
            for q in range(2):
                pe.wait_ge(sem("gate_ready"), q + 1)
                for g in range(8):
                    gate_bank(32 + 8 * q + g)
                    for j in range(4):
                        mm = pe.transpose(PS[:, g % 4, 128 * j:128 * j + 128], LG[q][:, 512 * g + 128 * j:512 * g + 128 * j + 128], ident)
                    mm.then_inc(sem("g_mm"), 1)
                for h in range(2):
                    pe.wait_ge(sem(f"g_ev{h}"), 16 + 4 * q + 4)
                for b2 in range(2):
                    for t in range(NT):
                        mm = pe.matmul(PS[:, 6, 128 * q + 64 * b2:128 * q + 64 * b2 + 64], U[:, NT * (2 * q + b2) + t, :],
                                       MN[:, t, 64 * b2:64 * b2 + 64], start=(t == 0), stop=(t == NT - 1))
                mm.then_inc(sem("pool_mm"), 1)
                pe.wait_ge(sem("pool_ev"), q + 1)

            def hidden(g):
                pe.wait_ge(sem(f"ew_in{g % 4}"), 32 * (g // 4 + 1))
                if g >= 2:
                    pe.wait_ge(sem("hp_ready"), g - 1)
                for e in range(EG):
                    mm = pe.matmul(PS[32 * e:32 * e + 32, g % 2, :], poolT[:, B * (EG * g + e):B * (EG * g + e) + 32], W1B[:, g % 4, e, :], start=True, stop=True)
                mm.then_inc(sem("e1_mm"), 1)

            def turn_hidden(g):
                pe.wait_ge(sem("hp_ready"), g + 1)
                if g >= 2:
                    pe.wait_ge(sem("h_ev"), g - 1)
                for k in range(4):
                    mm = pe.transpose(PS[:, 2 + g % 2, 128 * k:128 * k + 128], HP[g % 2][:, k:HID:4], ident)
                mm.then_inc(sem("ht_mm"), 1)

            def result(g):
                pe.wait_ge(sem("hg_ready"), g + 1)
                if g >= 2:
                    pe.wait_ge(sem("rb_ready"), g - 1)
                for k in range(4):
                    for e in range(EG):
                        mm = pe.matmul(PS[32 * e:32 * e + 32, 4 + g % 2, 0:D], HG[g % 2][:, 16 * e + 4 * k:16 * e + 4 * k + 32],
                                       W2B[:, g % 4, e, k, :], start=(k == 0), stop=(k == 3))
                mm.then_inc(sem("e2_mm"), 1)

            def turn_result(g):
                pe.wait_ge(sem("rb_ready"), g + 1)
                if g >= 2:
                    pe.wait_ge(sem("ot_ev"), g - 1)
                pe.transpose(PS[:, 6 + g % 2, 0:128], RB[g % 2], ident).then_inc(sem("rt_mm"), 1)

            for s in range(NG + 3):
                if s < NG:
                    hidden(s)
                if 0 <= s - 1 < NG:
                    turn_hidden(s - 1)
                if 0 <= s - 2 < NG:
                    result(s - 2)
                if 0 <= s - 3:
                    turn_result(s - 3)
            pe.wait_ge(sem("ot_ev"), NG)
            for q in range(2):
                mm = pe.transpose(PS[:, 4, 128 * q:128 * q + 128], OT[:, 2 * q:2 * q + 2, :].rearrange("p b e -> p (b e)"), ident)
            mm.then_inc(sem("oe_mm"), 1)
            pe.wait_ge(sem("oe_ready"), 1)
            for g in range(8 * B):
                q, t = g // 16, 2 * (g % 16)
                if g >= 4:
                    pe.wait_ge(sem("fin_ready"), g - 3)
                for j in range(2):
                    mm = pe.matmul(PS[:, g % 4, 256 * j:256 * j + 256], LG[q][:, 128 * (t + j):128 * (t + j) + 128],
                                   outE[:, q].rearrange("p b o -> p (b o)"), start=True, stop=True)
                mm.then_inc(sem("fin_mm"), 1)

        def pool_l1(pool, pool_steps):
            pool.wait_ge(sem("norm_ready"), 1)
            for b in range(B):
                tiles = slice(NT * b, NT * b + NT)
                if b >= 1:
                    pool.wait_ge(sem("pre_mm"), 24 * b - 16)
                pool_steps.later(pool.tensor_tensor(XB, U[:, tiles, :], tkr[:, tiles].unsqueeze(2).broadcast_to([128, NT, D]), ALU.mult))
                pool.tensor_tensor(XB, XB, tkn[:, tiles].unsqueeze(2).broadcast_to([128, NT, D]), ALU.add).then_inc(sem("tokens_ready"), 1)

        def scalar_l1(act):
            def root8():
                act.wait_ge(sem("var_ready"), 8 + root8.n)
                act.activation(WS[:, 1, :], WS[:, 3, :], ACT.Sqrt).then_inc(sem("root_ready"), 1)
                root8.n += 1
            root8.n = 0
            root8()
            with act.Fori(0, B) as b:
                for g in (1, 3, 5, 7, *range(8, 24)):
                    k = g % 8
                    t = slice(512 * k, 512 * k + 512)
                    if g < 16 or g % 2:
                        act.wait_ge(sem("pre_mm"), b * 24 + g + 1)
                    if g < 8:
                        act.activation(XT[:, t], PS[:, g % 4, :], ACT.Copy).then_inc(sem("pre_ev1"), 1)
                    elif g < 16:
                        act.activation(QH[:, t], PS[:, g % 4, :], ACT.Copy).then_inc(sem("hi_ready"), 1)
                    else:
                        if g % 2:
                            act.activation(V[:, 2 * TOK + 512 * k:2 * TOK + 512 * k + 512], PS[:, g % 4, :], ACT.Copy).then_inc(sem("pre_ev1"), 1)
                        act.activation(KH[:, t], XT[:, t], ACT.Copy, scale=KUP).then_inc(sem("hi_ready"), 1)

                def exponentials(i):
                    act.wait_ge(sem("nm_ready"), b * NT + i + 1)
                    s = SR[i % 3][:, 0:128 * (i + 1)]
                    act.activation(s, s, ACT.Exp, scale=SCALE / (QUP * KUP), bias=nmax[:, i % 3:i % 3 + 1],
                                   accum_out=rsum[:, i % 4:i % 4 + 1]).then_inc(sem("exp_ready"), 1)

                def take_turned(i, c):
                    w = min(512, 128 * (i + 1) - 512 * (c - first[i]))
                    act.wait_ge(sem("t_mm"), b * CH + c + 1)
                    if c >= 3:
                        act.wait_ge(sem("w_mm"), b * CH + c - 2)
                    act.activation(PTB[:, c % 3, 0:w], PS[:, 3 + c % 3, 0:w], ACT.Copy).then_inc(sem("t_ev1"), 1)

                exponentials(0)
                for i in range(NT):
                    if first[i] % 2:
                        take_turned(i, first[i])
                    if i + 1 < NT:
                        exponentials(i + 1)
                    for c in range(first[i] + 1, first[i] + blocks[i]):
                        if c % 2:
                            take_turned(i, c)
            root8()
            act.wait_ge(sem("coef_ready"), 1)

            def norm_chunk(c):
                i = NT * (2 * (c // 8) + 1) + 4 * (c % 8)
                for j in range(i, i + 4):
                    ins = act.activation(U[:, j, :], U[:, j, :], ACT.Identity, scale=tkr[:, j:j + 1], bias=tkn[:, j:j + 1])
                ins.then_inc(sem("xn_ready1"), 1)

            def gate_exp(q):
                act.wait_ge(sem("gm_ready"), q + 1)
                act.activation(LG[q], LG[q], ACT.Exp, bias=gmx[:, q, 0:1], accum_out=gmx[:, q, 1:2]).then_inc(sem("gexp_ready"), 1)

            norm_chunk(0)
            for c in range(16):
                if c + 1 < 16:
                    norm_chunk(c + 1)
                act.wait_ge(sem("g_mm"), 2 * c + 2)
                if c >= 2:
                    act.wait_ge(sem("lg_mm"), c - 1)
                act.activation(XTS[(2 * c + 1) % 4], PS[:, (2 * c + 1) % 4, :], ACT.Copy).then_inc(sem("g_ev1"), 1)
                if c == 9:
                    gate_exp(0)
            gate_exp(1)
            for q in range(2):
                for g in range(1, 8, 2):
                    act.wait_ge(sem("g_mm"), 32 + 8 * q + g + 1)
                    if q:
                        act.wait_ge(sem("pool_mm"), 1)
                    act.activation(AF[1][:, 512 * g:512 * g + 512], PS[:, g % 4, :], ACT.Copy).then_inc(sem("g_ev1"), 1)
            for s in range(NG + 1):
                if s < NG:
                    act.wait_ge(sem("e1_mm"), s + 1)
                    if s >= 2:
                        act.wait_ge(sem("ht_mm"), s - 1)
                    act.activation(HP[s % 2], PS[:, s % 2, :], ACT.Copy).then_inc(sem("hp_ready"), 1)
                if s >= 1:
                    g = s - 1
                    act.wait_ge(sem("h_ev"), g + 1)
                    if g >= 2:
                        act.wait_ge(sem("e2_mm"), g - 1)
                    act.activation(HG[g % 2][:, 0:64], HB[:, g % 2, :], ACT.Gelu).then_inc(sem("hg_ready"), 1)

        def vector_l1(dve, st, image_stats, row_moments):
            later = st.later

            def token_norm(ready):
                row_moments()
                m, e, v = WS[:, 0, :], WS[:, 1, :], WS[:, 3, :]
                later(dve.tensor_tensor(v, m, m, ALU.mult))
                later(dve.tensor_tensor(v, e, v, ALU.subtract))
                dve.tensor_scalar(v, v, EPS, None, ALU.add).then_inc(sem("var_ready"), 1)
                dve.wait_ge(sem("root_ready"), ready)
                later(dve.reciprocal(tkr, e))
                later(dve.scalar_tensor_tensor(tkn, m, -1.0, tkr, ALU.mult, ALU.mult))

            token_norm(8)
            dve.memset(lay[:, 2:3], 0.0).then_inc(sem("norm_ready"), 1)
            dve.wait_ge(sem("wt_mm"), 1)
            dve.tensor_scalar(WT2[:, 0, :], PS[:, 0, 0:128], QUP, None, ALU.mult)
            dve.tensor_copy(WT2[:, 1, :], PS[:, 0, 128:256])
            dve.tensor_copy(gwT, PS[:, 0, 384:384 + EX])
            dve.tensor_copy(ident16, ident)
            dve.tensor_copy(mask16, cst["mask"]).then_inc(sem("wt_ready"), 1)
            tick = lay[:, 0:1]
            later(dve.memset(tick, 0.0))
            dve.memset(tick, 0.0).then_inc(sem("l1_start"), 1)

            base = st.n
            with dve.Fori(0, B) as b:
                dve.memset(lay[:, 1:2], 0.0).then_inc(sem("batch_begun"), 1)
                for g in (0, 2, 4, 6, *range(8, 24)):
                    k = g % 8
                    t = slice(512 * k, 512 * k + 512)
                    if g < 8 or g >= 16 and g % 2 == 0:
                        dve.wait_ge(sem("pre_mm"), b * 24 + g + 1)
                        dst = XT[:, t] if g < 8 else V[:, 2 * TOK + 512 * k:2 * TOK + 512 * k + 512]
                        dve.tensor_copy(dst, PS[:, g % 4, :]).then_inc(sem("pre_ev0"), 1)
                    if g >= 8:
                        dve.wait_ge(sem("hi_ready"), b * 16 + g - 7)
                        hi, lo, of, up = (QH, QL, PS[:, g % 4, :], 1.0) if g < 16 else (KH, KL, XT[:, t], KUP)
                        dve.scalar_tensor_tensor(lo[:, t], of, up, hi[:, t], ALU.mult, ALU.subtract).then_inc(sem("lo_ready"), 1)

                def take_scores(i):
                    for j in range(blocks[i]):
                        c = first[i] + j
                        w = min(512, 128 * (i + 1) - 512 * j)
                        dve.wait_ge(sem("sc_mm"), b * CH + c + 1)
                        if i >= 3 and j == 0:
                            dve.wait_ge(sem("t_mm"), b * CH + first[i - 2])
                        dve.tensor_scalar(SR[i % 3][:, 512 * j:512 * j + w], PS[:, c % 3, 0:w], 1.0, -3e38, ALU.mult, ALU.max,
                                          accum_out=bmax[:, 8 * (i % 2) + j:8 * (i % 2) + j + 1]).then_inc(sem("sc_ev"), 1)
                    dve.wait_ge(sem("sc_ev"), b * CH + first[i] + blocks[i])
                    dve.tensor_reduce(mraw[:, i % 2:i % 2 + 1], bmax[:, 8 * (i % 2):8 * (i % 2) + blocks[i]], AX.X, ALU.max).then_inc(sem("mr_ready"), 1)
                    dve.wait_ge(sem("mr_ready"), b * NT + i + 1)
                    dve.tensor_scalar(nmax[:, i % 3:i % 3 + 1], mraw[:, i % 2:i % 2 + 1], -SCALE / (QUP * KUP), None, ALU.mult).then_inc(sem("nm_ready"), 1)

                def finish(i):
                    dve.wait_ge(sem("exp_ready"), b * NT + i + 1)
                    dve.reciprocal(rden[:, i % 2:i % 2 + 1], rsum[:, i % 4:i % 4 + 1]).then_inc(sem("rd_ready"), 1)
                    dve.wait_ge(sem("rd_ready"), b * NT + i + 1)
                    dve.wait_ge(sem("w_mm"), b * CH + first[i] + blocks[i])
                    if i > 0:
                        dve.wait_ge(sem("o_ev"), b * NT + i)
                    dve.memset(tick, 0.0)
                    u = U[:, bass.ds(b * NT + i, 1), :]
                    dve.scalar_tensor_tensor(u, PS[:, 6 + i % 2, 0:128].unsqueeze(1), rden[:, i % 2:i % 2 + 1], u, ALU.mult, ALU.add).then_inc(sem("o_ev"), 1)
                    if i > 0:
                        dve.bn_stats(ST[:, bass.ds(b * NT + i - 1, 1), :], U[:, bass.ds(b * NT + i - 1, 1), :])

                def take_turned(i, c):
                    w = min(512, 128 * (i + 1) - 512 * (c - first[i]))
                    dve.wait_ge(sem("t_mm"), b * CH + c + 1)
                    if c >= 3:
                        dve.wait_ge(sem("w_mm"), b * CH + c - 2)
                    dve.tensor_copy(PTB[:, c % 3, 0:w], PS[:, 3 + c % 3, 0:w]).then_inc(sem("t_ev0"), 1)

                take_scores(0)
                take_scores(1)
                for i in range(NT):
                    if first[i] % 2 == 0:
                        take_turned(i, first[i])
                    if i + 2 < NT:
                        take_scores(i + 2)
                    if i > 0:
                        finish(i - 1)
                    for c in range(first[i] + 1, first[i] + blocks[i]):
                        if c % 2 == 0:
                            take_turned(i, c)
                finish(NT - 1)
                dve.wait_ge(sem("o_ev"), b * NT + NT)
                dve.memset(tick, 0.0)
                dve.bn_stats(ST[:, bass.ds(b * NT + NT - 1, 1), :], U[:, bass.ds(b * NT + NT - 1, 1), :]).then_inc(sem("stats_done"), 1)

            dve.wait_ge(sem("stats_done"), B)
            token_norm(9)
            dve.memset(lay[:, 2:3], 0.0).then_inc(sem("coef_ready"), 1)

            def norm_chunk(c):
                i = NT * 2 * (c // 8) + 4 * (c % 8)
                for j in range(i, i + 4):
                    ins = dve.tensor_scalar(U[:, j, :], U[:, j, :], tkr[:, j:j + 1], tkn[:, j:j + 1], ALU.mult, ALU.add)
                ins.then_inc(sem("xn_ready0"), 1)

            def take_logits(c):
                dve.wait_ge(sem("lg_mm"), c + 1)
                dve.tensor_scalar(LG[c // 8][:, 512 * (c % 8):512 * (c % 8) + 512], PS[:, 4 + c % 2, :], gbs, -3e38, ALU.add, ALU.max,
                                  accum_out=bmax[:, c:c + 1]).then_inc(sem("lg_ev"), 1)
                if c % 8 == 7:
                    q = c // 8
                    dve.wait_ge(sem("lg_ev"), c + 1)
                    later(dve.tensor_reduce(gmx[:, q, 0:1], bmax[:, 8 * q:8 * q + 8], AX.X, ALU.max))
                    dve.tensor_scalar(gmx[:, q, 0:1], gmx[:, q, 0:1], -1.0, None, ALU.mult).then_inc(sem("gm_ready"), 1)

            def pooled(q):
                return dve.tensor_copy(poolT[:, 0:EX * B].rearrange("p (e b) -> p e b", b=B)[:, :, 2 * q:2 * q + 2],
                                       PS[:, 6, 128 * q:128 * q + 128].rearrange("p (b e) -> p e b", b=2))

            norm_chunk(0)
            for c in range(16):
                if c + 1 < 16:
                    norm_chunk(c + 1)
                dve.wait_ge(sem("g_mm"), 2 * c + 1)
                if c >= 2:
                    dve.wait_ge(sem("lg_mm"), c - 1)
                dve.tensor_copy(XTS[2 * c % 4], PS[:, 2 * c % 4, :]).then_inc(sem("g_ev0"), 1)
                if c >= 1:
                    take_logits(c - 1)
            take_logits(15)
            dve.memset(HG[0], 0.0)
            dve.memset(HG[1], 0.0)
            dve.memset(poolT[:, EX * B:], 0.0)
            for q in range(2):
                dve.wait_ge(sem("gexp_ready"), q + 1)
                later(dve.reciprocal(gmx[:, q, 2:3], gmx[:, q, 1:2]))
                later(dve.tensor_scalar(LG[q], LG[q], gmx[:, q, 2:3], None, ALU.mult))
                later(dve.max(top8, LG[q]))
                later(dve.match_replace(LR[q], top8, LG[q], 0.0))
                dve.tensor_tensor(LG[q], LG[q], LR[q], ALU.subtract).then_inc(sem("gate_ready"), 1)
                if q:
                    dve.wait_ge(sem("pool_mm"), 1)
                    pooled(0).then_inc(sem("pool_ev"), 1)
                for g in range(0, 8, 2):
                    dve.wait_ge(sem("g_mm"), 32 + 8 * q + g + 1)
                    dve.tensor_copy(AF[1][:, 512 * g:512 * g + 512], PS[:, g % 4, :]).then_inc(sem("g_ev0"), 1)
            dve.wait_ge(sem("pool_mm"), 2)
            pooled(1).then_inc(sem("pool_ev"), 1)
            dve.wait_ge(sem("b1_in"), 16)

            later(dve.memset(outE, 0.0))

            def take_hidden(g):
                dve.wait_ge(sem("ht_mm"), g + 1)
                if g >= 2:
                    dve.wait_ge(sem("hg_ready"), g - 1)
                dve.tensor_tensor(HB[:, g % 2, :].rearrange("p (e k b) -> p e k b", e=EG, k=4),
                                  PS[:, 2 + g % 2, :].rearrange("p (k e r b) -> p r e k b", k=4, e=EG, b=B)[:, 0],
                                  B1T[:, EG * g:EG * g + EG, :].unsqueeze(3).broadcast_to([128, EG, 4, B]), ALU.add).then_inc(sem("h_ev"), 1)

            def take_result(g):
                dve.wait_ge(sem("e2_mm"), g + 1)
                if g >= 2:
                    dve.wait_ge(sem("rt_mm"), g - 1)
                dve.tensor_copy(RB[g % 2], PS[:, 4 + g % 2, 0:D]).then_inc(sem("rb_ready"), 1)

            def place_result(g):
                dve.wait_ge(sem("rt_mm"), g + 1)
                dve.tensor_copy(OT[:, :, EG * g:EG * g + EG], PS[:, 6 + g % 2, 0:128].rearrange("p (e r b) -> p r b e", e=EG, b=B)[:, 0]).then_inc(sem("ot_ev"), 1)

            for s in range(NG + 3):
                if 0 <= s - 1 < NG:
                    take_hidden(s - 1)
                if 0 <= s - 2 < NG:
                    take_result(s - 2)
                if 0 <= s - 3:
                    place_result(s - 3)
                if s < NG:
                    for j in range(8 * s, 8 * s + 8):
                        ins = dve.tensor_scalar(U[:, j, :], U[:, j, :], WS[:, 1, j:j + 1], WS[:, 0, j:j + 1], ALU.mult, ALU.add)
                    if s == NG - 1:
                        later(ins)
            dve.wait_ge(sem("oe_mm"), 1)
            for b2 in range(2):
                e = slice(EX * b2, EX * b2 + EX)
                ins = dve.tensor_tensor(outE[e, :, b2], PS[e, 4, 0:256].rearrange("p (q o) -> p q o", q=2),
                                        b2n[e].unsqueeze(1).broadcast_to([EX, 2, D]), ALU.add)
            ins.then_inc(sem("oe_ready"), 1)
            for g in range(8 * B):
                q, t = g // 16, 2 * (g % 16)
                dve.wait_ge(sem("fin_mm"), g + 1)
                u = U[:, 2 * NT * q:2 * NT * q + 2 * NT, :].rearrange("p (b t) w -> p b t w", b=2)[:, :, t:t + 2]
                dve.tensor_tensor(u, u, PS[:, g % 4, :].rearrange("p (t b w) -> p b t w", t=2, b=2), ALU.add).then_inc(sem("fin_ready"), 1)

        def value_products(eng, k, parts, done):
            r = k // NQ
            eng.wait_ge(sem(f"e_in{k % 3}"), 16 * (k // 3 + 1))
            if k % NQ == 0:
                eng.wait_ge(sem(f"xr_modes{r % 2}"), 64 * (r // 2 + 1))
            if k >= 2:
                eng.wait_ge(sem("v_mm"), k - 1)
            for bs, ps in parts:
                shape = [128, bs.stop - bs.start, MR * (ps.stop - ps.start)]
                ins = eng.tensor_tensor(YB[:, k % 2, bs, ps].rearrange("p b k m -> p b (k m)"), XR[:, r % 2, bs, ps].rearrange("p b k m -> p b (k m)"),
                                        EB[:, k % 3, ps].rearrange("p k m -> p (k m)").unsqueeze(1).broadcast_to(shape), ALU.mult)
            ins.then_inc(sem(done), 1)

        MD = M * 2 // 3

        def mode_products(eng, later, m):
            wr = Af[:, 0:2 * M].rearrange("p (m c) -> p m c", c=2)[:, m]
            t1, t2 = Af[:, 2 * M:3 * M][:, m], Af[:, 3 * M:4 * M][:, m]
            zr, zi, yr = Z[:, 0, m], Z[:, 1, m], Z[:, 2, m]

            def real():
                later(eng.tensor_tensor(yr, zr, wr[:, :, 0], ALU.mult))
                later(eng.tensor_tensor(t1, zi, wr[:, :, 1], ALU.mult))
                later(eng.tensor_tensor(t2, zr, wr[:, :, 1], ALU.mult))
                later(eng.tensor_tensor(yr, yr, t1, ALU.subtract))

            def imag():
                later(eng.tensor_tensor(t1, zi, wr[:, :, 0], ALU.mult))
                later(eng.tensor_tensor(zi, t1, t2, ALU.add))

            return real, imag

        def score_products(eng, z):
            h, k = z // (4 * NLC), z // 4 % NLC
            xc, wc = ((0, 0), (1, 1), (1, 0), (0, 2))[z % 4]
            w = min(128, ML - 128 * k)
            if z >= 4:
                eng.wait_ge(sem("s_mm"), z - 3)
            eng.tensor_tensor(ZP[z % 4][0:w], XLT[0:w, xc, k, :].unsqueeze(1).broadcast_to([w, 16, N]),
                              CT[0:w, wc, k, 16 * h:16 * h + 16].unsqueeze(2).broadcast_to([w, 16, N]),
                              ALU.mult).then_inc(sem("zp_pool" if z % 4 == 3 else "zp_dve"), 1)

        def emptied(eng, what, g, rounds=0, groups=0):
            eng.wait_ge(sem(f"{what}{g % 2}"), rounds * ((groups + 1 - g % 2) // 2) + g // 2 + 1)

        def all_emptied(eng, what, rounds, groups):
            eng.wait_ge(sem(f"{what}0"), rounds * ((groups + 1) // 2))
            eng.wait_ge(sem(f"{what}1"), rounds * (groups // 2))

        def forward_evacs(eng, layer, mmsem, scale):
            odd = eng.engine == nc.scalar.engine
            for g in range(int(odd), NF2, 2):
                eng.wait_ge(sem(mmsem), max(layer - 1, 0) * NF2 + g + 1)
                n = 3 if g < NF2 - 1 else 2
                j0 = 1 if g == 0 else 0
                lo = 64 - (3 * g + 2)
                src = PS[:, g % 4, 0:396].rearrange("p (j s c x) -> p s c j x", j=3, s=2, c=2)
                for c in range(2):
                    for o, i in ((Zk[:, c, 3 * g:3 * g + n, :], src[:, 0, c, 0:n, :]),
                                 (Zk[:, c, lo:lo + 3 - j0, :], src[:, 1, c, 2:(0 if j0 else None):-1, :])):
                        if odd:
                            ins = nc.scalar.activation(o, i, ACT.Identity, scale=scale)
                        else:
                            ins = nc.vector.tensor_scalar(o, i, scale, None, ALU.mult)
                ins.then_inc(sem(f"f2_ev{int(odd)}"), 1)

        block = ctx.enter_context(nc.Block())

        @block.sync
        def _(sp):
            sp.dma_start(CST[:], io["consts"]).then_inc(sem("consts_in"), 16)
            for i in range(3):
                sp.dma_start(XN[:, i], x_nat[:, 8 * i:8 * i + 8, :]).then_inc(sem(f"xn_in{i}"), 16)
            sp.dma_start(V[0:NH, 0:2 * M], io["L0_conv_Pcw"].rearrange("n o k x c -> n (o k x c)")).then_inc(sem("w_in"), 16)
            for i, n in enumerate("QKV"):
                sp.dma_start(V[0:NH, 4224 + 1088 * i:4224 + 1088 * (i + 1)],
                             io[f"L0_conv_{n}cw"].rearrange("o n k x c -> n (o k x c)")).then_inc(sem("w_in"), 16)
            for i, n in enumerate("KQPV"):
                col = io[f"L0_conv_{n}sw"].rearrange("a n -> n a") if n == "P" else io[f"L0_conv_{n}sw"]
                row = io[f"L0_conv_{n}sw"] if n == "P" else io[f"L0_conv_{n}sw"].rearrange("n a -> a n")
                sp.dma_start(headc[0:NH, i:i + 1], col).then_inc(sem("w_in"), 16)
                sp.dma_start(headw[:, i, :], row.broadcast_to([128, NH])).then_inc(sem("w_in"), 16)
            for i, n in enumerate(PAR):
                src = io[f"L0_conv_{n}"]
                src = src if n.startswith("m") and n.endswith("sw") else src.unsqueeze(0)
                sp.dma_start(PAR[n], src.broadcast_to([128, 1])).then_inc(sem("w_in"), 16)
            for c in range(3, 16):
                sp.wait_ge(sem("f1_mm"), 2 * (c - 2))
                sp.wait_ge(sem("xsq"), c - 2)
                sp.dma_start(XN[:, c % 3], x_nat[:, 8 * c:8 * c + 8, :]).then_inc(sem(f"xn_in{c % 3}"), 16)
            sp.wait_ge(sem("e_ready"), 1)
            for q in range(3):
                sp.dma_start(e_dram[:, :, q, :].rearrange("r n m -> n r m"), P3[:, q, :].rearrange("p (r m) -> p r m", m=MR)
                             ).then_inc(sem("e_out"), 16)
            sp.wait_ge(sem("e_out"), 48)
            sp.wait_ge(sem("ct_mm"), 1)
            for i in range(4):
                sp.dma_start(V[:, 4096 * i:4096 * (i + 1)], x_img[:, 4096 * i:4096 * (i + 1)]).then_inc(sem(f"xi_in{i}"), 16)
            sp.wait_ge(sem("xs_ready"), 1)
            for q, src in enumerate((XS, Z[:, 0, :], Z[:, 1, :])):
                sp.dma_start(x_dram[:, :, q, :].rearrange("r n m -> n r m"), src.rearrange("p (r m) -> p r m", m=MR)
                             ).then_inc(sem("x_out"), 16)
            sp.wait_ge(sem("x_out"), 48)

            def load_modes(r):
                if r >= 2:
                    sp.wait_ge(sem("y_dve"), NQ * (r - 1))
                    sp.wait_ge(sem("y_pool"), NQ * (r - 1))
                for n in range(4):
                    sp.dma_start(XR[32 * n:32 * n + 32, r % 2].rearrange("p b k m -> p b (k m)"), x_dram[r].rearrange("(b s) k m -> s b (k m)", b=B)
                                 ).then_inc(sem(f"xr_modes{r % 2}"), 16)

            load_modes(0)
            load_modes(1)
            sp.wait_ge(sem("pbar_ready"), 1)
            for k in range(NR * NQ):
                r, g = divmod(k, NQ)
                if k >= 3:
                    sp.wait_ge(sem("y_dve"), k - 2)
                    sp.wait_ge(sem("y_pool"), k - 2)
                sp.dma_start(EB[:, k % 3].rearrange("p k m -> p (k m)"),
                             e_dram[r, 4 * g:4 * g + 4].rearrange("n k m -> n (k m)").unsqueeze(1).broadcast_to([4, 32, 3 * MR])
                             ).then_inc(sem(f"e_in{k % 3}"), 16)
                if g == 2 and 1 <= r < NR - 1:
                    load_modes(r + 1)
            for i, n in enumerate(("m0cw", "m1cw")):
                sp.wait_ge(sem("f2_mm_m"), NF2 * (i + 1))
                sp.dma_start(Af[:, 0:2 * M], io[f"L0_conv_{n}"].rearrange("a b k x c -> (a b) (k x c)")
                             .broadcast_to([128, 2 * M])).then_inc(sem("mw_in"), 16)
            sp.wait_ge(sem("tr_mm"), 3 * NTR)
            for k in range(16):
                if k >= 3:
                    sp.wait_ge(sem("ax_ready"), k - 2)
                sp.dma_start(AF[1][:, 1024 * (k % 3):1024 * (k % 3 + 1)].rearrange("p (i w) -> p i w", w=W),
                             x_nat[:, 8 * k:8 * k + 8, :]).then_inc(sem(f"xr_in{k % 3}"), 16)
            sp.wait_ge(sem("x1_ready"), NIM)
            for i, n in enumerate("qkv"):
                sp.dma_start(WN3[:, i, :], io[f"L1_attn_W{n}"]).then_inc(sem("l1w_in"), 16)
            sp.dma_start(gwn, io["L1_ffn_gate_w"]).then_inc(sem("l1w_in"), 16)
            for h in range(2):
                sp.dma_start(b2n[EX * h:EX * h + EX], io["L1_ffn_weight2"][:, HID, :]).then_inc(sem("l1w_in"), 16)
            sync_l1(sp)

        @block.gpsimd
        def _(pool):
            pool.wait_ge(sem("xlt_ev"), 1)
            pool.wait_ge(sem("ct_ready"), 1)
            pool.wait_ge(sem("gram_mm"), 1)
            for z in range(3, 8 * NLC, 4):
                score_products(pool, z)
            for k in range(NR * NQ):
                value_products(pool, k, ((slice(3, 4), slice(0, 3)), (slice(2, 3), slice(2, 3))), "y_pool")
            pool_steps = Steps(pool, sem("pool_step"))
            for layer in (1, 2):
                pool.wait_ge(sem("weights_folded"), layer)
                real, imag = mode_products(pool, pool_steps.later, slice(MD, M))
                real()
                imag()
            pool.wait_ge(sem("a_kept"), 3)
            for k in range(16):
                pool.wait_ge(sem(f"xr_in{k % 3}"), 16 * (k // 3 + 1))
                u = U[:, 8 * k:8 * k + 8, :]
                pool.tensor_tensor(u, u, AF[1][:, 1024 * (k % 3):1024 * (k % 3 + 1)].rearrange("p (i w) -> p i w", w=W),
                                   ALU.add).then_inc(sem("ax_ready"), 1)
            pool.wait_ge(sem("ax_ready"), 16)
            for g in range(NIM):
                if g % 4 == 3:
                    pool.wait_ge(sem("mn_dve"), g // 4 + 1)
                else:
                    pool.wait_ge(sem("mn_act"), 3 * (g // 4) + g % 4 + 1)
                u = U[:, 4 * g:4 * g + 4, :]
                pool.tensor_tensor(u, u, Vn[:, 4 * g:4 * g + 4, :], ALU.add).then_inc(sem("x1_ready"), 1)
            pool_l1(pool, pool_steps)

        @block.tensor
        def _(pe):
            pe.wait_ge(sem("consts_in"), 16)

            def half_forward(layer, k, src, bank_evac):
                if k >= 4:
                    pe.wait_ge(sem(bank_evac), k - 3 + 32 * layer)
                for j in range(4):
                    mm = pe.matmul(PS[:, k % 4, 66 * j:66 * j + 128], src(j), fh_wide, start=True, stop=True)
                mm.then_inc(sem("f1_mm"), 1)

            def forward(layer, mmsem):
                pe.wait_ge(sem("a_ready"), layer + 1)
                for g in range(NF2):
                    if g >= 4:
                        emptied(pe, "f2_ev", g - 4, layer, NF2)
                    for j in range(3):
                        ky = 3 * g + j
                        o = PS[:, g % 4, 132 * j:132 * j + 132]
                        pe.matmul(o, A[:, :, ky], cst["fwr"], start=True, stop=False)
                        mm = pe.matmul(o, A[:, :, KX + ky], cst["fwi"], start=False, stop=True)
                    mm.then_inc(sem(mmsem), 1)

            def inverse(layer):
                pe.wait_ge(sem("z_ready"), layer + 1)
                for g in range(NTR):
                    if g >= 4:
                        emptied(pe, "tr_ev", g - 4, layer, NTR)
                    for i in range(4 * g, min(4 * g + 4, 2 * KX)):
                        c, kx = divmod(i, KX)
                        mm = pe.matmul(PS[:, g % 4, 128 * (i % 4):128 * (i % 4) + 128], Zk[:, c:c + 2, :, kx], ident,
                                       is_transpose=True, start=True, stop=True)
                    mm.then_inc(sem("tr_mm"), 1)
                all_emptied(pe, "tr_ev", layer + 1, NTR)

                def rows(k):
                    if k >= 2:
                        pe.wait_ge(sem("i1_ev"), 32 * layer + k - 1)
                    for j in range(4):
                        mm = pe.matmul(PS[0:66, 4 + k % 2, 128 * j:128 * j + 128], A_modes[:, :, 4 * k + j], cst["ih"],
                                       start=True, stop=True)
                    mm.then_inc(sem("i1_mm"), 1)

                def columns(k):
                    pe.wait_ge(sem("i1_ev"), 32 * layer + k + 1)
                    if k >= 2:
                        pe.wait_ge(sem("i2_ev"), 32 * layer + k - 1)
                    for j in range(4):
                        mm = pe.matmul(PS[:, 6 + k % 2, 128 * j:128 * j + 128], DB[0:66, k % 3, 128 * j:128 * j + 128],
                                       cst["iw"][0:66, :], start=True, stop=True)
                    mm.then_inc(sem("i2_mm"), 1)

                rows(0)
                for k in range(NIM):
                    if k + 1 < NIM:
                        rows(k + 1)
                    columns(k)

            A_modes = Af.rearrange("p (c n) -> p c n", n=N)

            for c in range(16):
                pe.wait_ge(sem(f"xn_in{c % 3}"), 16 * (c // 3 + 1))
                for q in range(2):
                    half_forward(0, 2 * c + q, lambda j: XN[:, c % 3, 4 * q + j, :], "f1_ev")
                pe.wait_ge(sem("xsq"), c + 1)
                for j in range(8):
                    mm = pe.matmul(PS[:, 4, 8 * c + j:8 * c + j + 128], XQ[:, c % 2, j, :], ones, start=True, stop=True)
                mm.then_inc(sem("sq_mm"), 1)
            pe.wait_ge(sem("c_ready"), 1)
            for c, src in enumerate((CR, CI)):
                for k in range(NLC):
                    w = min(128, ML - 128 * k)
                    mm = pe.transpose(PS[0:w, 5, 160 * c + 32 * k:160 * c + 32 * k + 32], src[:, 128 * k:128 * k + w], ident[0:NH, 0:NH])
            mm.then_inc(sem("ct_mm"), 1)
            pe.wait_ge(sem("g8_ready"), 1)
            pe.matmul(PS[:, 6, 0:8], cst["group"], G8, start=True, stop=True).then_inc(sem("g8_mm"), 1)
            pe.wait_ge(sem("rc_ready"), 1)
            pe.matmul(PS[:, 6, 16:17], SG[:, 4, :], ones[:, 0:1], start=True, stop=True)
            pe.matmul(PS[:, 6, 17:18], SG[:, 5, :], ones[:, 0:1], start=True, stop=True)
            pe.transpose(PS[:, 7, 0:128], SG[:, 6, :], ident)
            pe.transpose(PS[:, 7, 128:256], SG[:, 7, :], ident).then_inc(sem("is_mm"), 1)
            forward(0, "f2_mm_x")
            pe.wait_ge(sem("xe_ready"), 1)
            for g in range(9):
                if g >= 3:
                    pe.wait_ge(sem("xet_ev"), g - 2)
                for k in range(4 * g, min(4 * g + 4, 33)):
                    mm = pe.transpose(PS[:, g % 3, 128 * (k % 4):128 * (k % 4) + 128], Uf[:, 128 * k:128 * k + 128], ident)
                mm.then_inc(sem("xet_mm"), 1)
            pe.wait_ge(sem("xl_ready"), 1)
            pe.wait_ge(sem("rim_ready"), 1)
            for c in range(2):
                for k in range(NLC):
                    w = min(128, ML - 128 * k)
                    mm = pe.transpose(PS[0:w, (3, 4, 7)[(5 * c + k) // 4], 128 * ((5 * c + k) % 4):128 * ((5 * c + k) % 4) + 128],
                                      XL[:, c, 128 * k:128 * k + w], ident)
            mm.then_inc(sem("xlt_mm"), 1)
            pe.wait_ge(sem("xet_ev"), 9)
            for k in range(33):
                mm = pe.matmul(PS[:, 6, 0:128], XET[:, k, :], XET[:, k, :], start=(k == 0), stop=(k == 32))
            mm.then_inc(sem("gram_mm"), 1)
            pe.wait_ge(sem("xlt_ev"), 1)
            for z in range(8 * NLC):
                h, k, c = z // (4 * NLC), z // 4 % NLC, z % 4
                w = min(128, ML - 128 * k)
                pe.wait_ge(sem("zp_pool" if z % 4 == 3 else "zp_dve"), z // 4 + 1 if z % 4 == 3 else z - z // 4 + 1)
                for b in range(B):
                    s = slice(32 * b, 32 * b + 32)
                    mm = pe.matmul(PS[s, h, :], XLT[0:w, c // 2, k, s], ZP[z % 4][0:w, :, s],
                                   start=(k == 0 and c == 0), stop=(k == NLC - 1 and c == 3))
                mm.then_inc(sem("s_mm"), 1)
            pe.wait_ge(sem("p_ready"), 1)
            for g in range(NQ):
                mm = pe.transpose(PS[:, 2 + g // 4, 128 * (g % 4):128 * (g % 4) + 128],
                                  SE[:, 4 * g:4 * g + 4, :].rearrange("p n s -> p (n s)"), ident)
            mm.then_inc(sem("pt_mm"), 1)
            pe.wait_ge(sem("pb_ready"), 1)
            pe.transpose(PS[:, 6, 0:128], SG2, ident).then_inc(sem("mix_mm"), 1)
            pe.wait_ge(sem("pbt_ready"), 1)
            pe.matmul(PS[:, 7, 0:1], Pbt, beta, start=True, stop=True).then_inc(sem("mix_mm"), 1)
            pe.wait_ge(sem("pt_ev"), 2)
            for k in range(NR * NQ):
                r, g = divmod(k, NQ)
                if g == 0 and r >= 2:
                    pe.wait_ge(sem("zv_ev"), r - 1)
                pe.wait_ge(sem("y_dve"), k + 1)
                pe.wait_ge(sem("y_pool"), k + 1)
                for q in range(3):
                    for b in range(B):
                        s = slice(32 * b, 32 * b + 32)
                        mm = pe.matmul(PS[s, 3 * (r % 2) + q, 0:MR], PT[:, g, s], YB[:, k % 2, b, q, :],
                                       start=(g == 0), stop=(g == NQ - 1))
                mm.then_inc(sem("v_mm"), 1)
            pe.wait_ge(sem("mt_ready"), 1)
            pe.wait_ge(sem("xg_ready"), 1)
            xg = V[:].rearrange("p (h w) -> p h w", w=W)
            for g in range(32):
                if g >= 4:
                    emptied(pe, "mx_ev", g - 4)
                elif g == 0:
                    pe.wait_ge(sem("zv_ev"), NR)
                for j in range(4):
                    mm = pe.matmul(PS[:, g % 4, 128 * j:128 * j + 128], xg[:, :, 4 * g + j], Mt, start=True, stop=True)
                mm.then_inc(sem("mx_mm"), 1)
            all_emptied(pe, "mx_ev", 1, 32)
            inverse(0)
            pe.wait_ge(sem("mv_ready"), 1)
            pe.wait_ge(sem("i2_ev"), 32)
            pe.matmul(PS[:, 7, 0:256], ones, MV, start=True, stop=True).then_inc(sem("mv_mm"), 1)
            for layer in (1, 2):
                for k in range(32):
                    if layer == 1 and k % 2:
                        pe.wait_ge(sem("src_odd"), k // 2 + 1)
                    else:
                        pe.wait_ge(sem("src_ready"), k // 2 + 1 if layer == 1 else NIM // 2 + k + 1)
                    half_forward(layer, k, lambda j: Vn[:, 4 * k + j, :], "f1_ev")
                forward(layer, "f2_mm_m")
                inverse(layer)
            pe.wait_ge(sem("mv_ready"), 2)
            pe.matmul(PS[:, 0, 0:256], ones, MV, start=True, stop=True).then_inc(sem("mv_mm"), 1)
            tensor_l1(pe)


        @block.scalar
        def _(act):
            st = Steps(act, sem("act_step"))

            def root():
                root.n += 1
                act.wait_ge(sem("var_ready"), root.n)
                v = root_args[root.n - 1]
                act.activation(v, v, ACT.Sqrt).then_inc(sem("root_ready"), 1)
            root.n = 0

            for c in range(16):
                act.wait_ge(sem(f"xn_in{c % 3}"), 16 * (c // 3 + 1))
                if c >= 2:
                    act.wait_ge(sem("sq_mm"), c - 1)
                act.activation(XQ[:, c % 2], XN[:, c % 3], ACT.Square).then_inc(sem("xsq"), 1)
                for k in range(2 * c, 2 * c + 2):
                    act.wait_ge(sem("f1_mm"), k + 1)
                    act.activation(A[:, 4 * k:4 * k + 4, :].rearrange("p n k -> p (n k)"), PS[:, k % 4, 0:264], ACT.Copy).then_inc(sem("f1_ev"), 1)
            root()
            root()

            act.wait_ge(sem("alpha_ready"), 1)
            forward_evacs(act, 0, "f2_mm_x", alpha)
            act.wait_ge(sem("x_beta"), 1)
            act.activation(XE, Z[:, 0:2, :], ACT.Copy, scale=float(np.sqrt(2.0))).then_inc(sem("xe_scaled"), 1)
            for g in range(9):
                act.wait_ge(sem("xet_mm"), g + 1)
                w = 512 if g < 8 else 128
                act.activation(Uf[:, 5376 + 512 * g:5376 + 512 * g + w], PS[:, g % 3, 0:w], ACT.Copy).then_inc(sem("xet_ev"), 1)
            act.wait_ge(sem("rim_ready"), 1)
            for i in range(4):
                act.wait_ge(sem(f"xi_in{i}"), 16)
            Vc = V[:].rearrange("p (h w) -> p w h", w=W)
            for w in range(W):
                ins = act.activation(Vc[:, w, :], Vc[:, w, :], ACT.Identity, scale=rim[:, w:w + 1], bias=cim[:, w:w + 1])
            ins.then_inc(sem("xg_ready"), 1)
            act.wait_ge(sem("sd_ready"), 1)
            act.activation(SE, SD, ACT.Exp).then_inc(sem("se_ready"), 1)
            act.wait_ge(sem("pt_mm"), 1)
            for h in range(2):
                act.activation(PT[:, 4 * h:4 * h + 4, :].rearrange("p n s -> p (n s)"), PS[:, 2 + h, :], ACT.Copy).then_inc(sem("pt_ev"), 1)
            act.wait_ge(sem("x_out"), 48)
            for r in range(NR):
                act.wait_ge(sem("v_mm"), NQ * (r + 1))
                act.activation(Z[:, 2, MR * r:MR * r + MR], PS[:, 3 * (r % 2), 0:MR], ACT.Copy).then_inc(sem("k1_ready"), 1)
            Um = U[:].rearrange("p n w -> p w n")
            for g in range(1, 32, 2):
                act.wait_ge(sem("mx_mm"), g + 1)
                act.activation(Um[:, 4 * g:4 * g + 4, :], PS[:, g % 4, :].rearrange("p (w n) -> p w n", w=4), ACT.Copy).then_inc(sem("mx_ev1"), 1)

            def inverse_evacs(layer):
                for g in range(1, NTR, 2):
                    act.wait_ge(sem("tr_mm"), layer * NTR + g + 1)
                    act.activation(Af[:, 512 * g:512 * (g + 1)], PS[:, g % 4, :], ACT.Copy).then_inc(sem("tr_ev1"), 1)
                for k in range(NIM):
                    act.wait_ge(sem("i1_mm"), 32 * layer + k + 1)
                    if k >= 3:
                        act.wait_ge(sem("i2_mm"), 32 * layer + k - 2)
                    act.activation(DB[0:66, k % 3, :], PS[0:66, 4 + k % 2, :], ACT.Copy).then_inc(sem("i1_ev"), 1)
                    if layer == 1:
                        if k >= 1:
                            gelu(k - 1)
                if layer == 1:
                    gelu(NIM - 1)

            def gelu(k):
                act.wait_ge(sem("y1_ready"), k + 1)
                v = Vn[:, 4 * k:4 * k + 4, :]
                act.activation(v, v, ACT.Gelu).then_inc(sem("src_ready"), 1)

            inverse_evacs(0)
            root()
            root()
            act.wait_ge(sem("src_ready"), 1)
            for k in range(1, NIM, 2):
                for i in range(4 * k, 4 * k + 4):
                    ins = act.activation(Vn[:, i, :], U[:, i, :], ACT.Identity, scale=WS[:, 6, i:i + 1], bias=WS[:, 7, i:i + 1])
                ins.then_inc(sem("src_odd"), 1)

            def keep(images):
                for i in range(images.start, images.stop):
                    ins = act.activation(U[:, i, :], U[:, i, :], ACT.Identity, scale=WS[:, 4, i:i + 1], bias=WS[:, 5, i:i + 1])
                ins.then_inc(sem("a_kept"), 1)

            act.wait_ge(sem("src_ready"), NIM // 2)
            keep(slice(0, 24))
            for layer in (1, 2):
                act.wait_ge(sem("a_ready"), layer + 1)
                forward_evacs(act, layer, "f2_mm_m", 1.0)
                if layer == 1:
                    keep(slice(24, 52))
                act.wait_ge(sem("yr_ready"), layer)
                act.activation(Z[:, 0, :], Z[:, 2, :], ACT.Square, accum_out=lay[:, 0:1]).then_inc(sem("vsum"), 1)
                act.wait_ge(sem("yi_ready"), layer)
                act.activation(Af[:, 3 * M:4 * M], Z[:, 1, :], ACT.Square, accum_out=lay[:, 1:2]).then_inc(sem("vsum"), 1)
                root()
                act.wait_ge(sem("rstd_ready"), layer)
                act.activation(Z[:, 1, :], Z[:, 1, :], ACT.Copy, scale=lay[:, 6:7]).then_inc(sem("z1_scaled"), 1)
                inverse_evacs(layer)
                if layer == 1:
                    keep(slice(52, N))
            root()
            act.wait_ge(sem("fin_coef"), 1)
            for g in range(NIM):
                if g % 4 < 3:
                    for i in range(4 * g, 4 * g + 4):
                        ins = act.activation(Vn[:, i, :], Vn[:, i, :], ACT.Identity, scale=WS[:, 3, i:i + 1], bias=WS[:, 7, i:i + 1])
                    ins.then_inc(sem("mn_act"), 1)
            scalar_l1(act)


        @block.vector
        def _(dve):
            st = Steps(dve, sem("dve_step"))
            later = st.later

            dve.wait_ge(sem("w_in"), 16 * (4 + 8 + 10))
            neg, pos = slice(33, 64), slice(31, 0, -1)
            later(dve.tensor_tensor(WP[:, neg, 0, 0], WP[:, neg, 0, 0], WP[:, pos, 0, 0], ALU.add))
            later(dve.tensor_tensor(WP[:, neg, 0, 1], WP[:, neg, 0, 1], WP[:, pos, 0, 1], ALU.subtract))
            later(dve.memset(WP[:, 1:32, 0, :], 0.0))
            later(dve.memset(WP[:, 0, 0, 1:2], 0.0))
            for w in range(3):
                q = QKV[:, w]
                later(dve.tensor_tensor(q[:, 17:32, 0, 0], q[:, 17:32, 0, 0], q[:, 15:0:-1, 0, 0], ALU.add))
                later(dve.tensor_tensor(q[:, 17:32, 0, 1], q[:, 17:32, 0, 1], q[:, 15:0:-1, 0, 1], ALU.subtract))
                later(dve.tensor_scalar(q[:, 16:32, 0, :], q[:, 16:32, 0, :], 0.5, None, ALU.mult))
                later(dve.memset(q[:, 1:16, 0, :], 0.0))
                later(dve.memset(q[:, 0, 0, 1:2], 0.0))
            ks, qs, psw, vs = (headc[0:NH, i:i + 1] for i in range(4))
            WPf = V[0:NH, 0:2 * M].rearrange("p (m c) -> p m c", c=2)
            P3k = P3.rearrange("p c (k x) -> p c k x", x=KX)
            for c in range(2):
                later(dve.tensor_scalar(P3[:, c, :], WPf[:, :, c], vs, None, ALU.mult))
            for h, (r0, q0) in enumerate(((0, 0), (48, 16))):
                wr, wi = WP[:, r0:r0 + 16, 0:LX, 0], WP[:, r0:r0 + 16, 0:LX, 1]
                vr, vi = QKV[:, 2, q0:q0 + 16, :, 0], QKV[:, 2, q0:q0 + 16, :, 1]
                t1 = T1[:, 0:272].rearrange("p (k x) -> p k x", x=LX)
                er, ei = (P3k[:, c, r0:r0 + 16, 0:LX] for c in range(2))
                later(dve.tensor_scalar(wr, wr, psw, None, ALU.add))
                if h:
                    later(dve.tensor_scalar(wr[:, :, 0:1], wr[:, :, 0:1], psw, None, ALU.add))
                for a, b, e, op in ((wr, vr, er, ALU.add), (wi, vi, er, ALU.subtract), (wr, vi, ei, ALU.add), (wi, vr, ei, ALU.add)):
                    later(dve.tensor_tensor(t1, a, b, ALU.mult))
                    later(dve.tensor_tensor(e, e, t1, op))
            later(dve.tensor_tensor(P3[:, 2, :], P3[:, 0, :], P3[:, 1, :], ALU.add))
            dve.tensor_tensor(P3[:, 1, :], P3[:, 1, :], P3[:, 0, :], ALU.subtract).then_inc(sem("e_ready"), 1)
            flat = V[0:NH, 4224:7488].rearrange("p (w m c) -> p w m c", w=3, c=2)
            ar, ai, br, bi = flat[:, 0, :, 0], flat[:, 0, :, 1], flat[:, 1, :, 0], flat[:, 1, :, 1]
            later(dve.tensor_tensor(CR, ar, br, ALU.mult))
            later(dve.scalar_tensor_tensor(CR, br, qs, CR, ALU.mult, ALU.add))
            later(dve.scalar_tensor_tensor(CR, ar, ks, CR, ALU.mult, ALU.add))
            later(dve.tensor_tensor(T1, ai, bi, ALU.mult))
            later(dve.tensor_tensor(CR, CR, T1, ALU.add))
            later(dve.scalar_tensor_tensor(CI, br, ks, ai, ALU.add, ALU.mult))
            later(dve.scalar_tensor_tensor(T1, ar, qs, bi, ALU.add, ALU.mult))
            later(dve.tensor_tensor(CI, CI, T1, ALU.subtract))
            for c in (CR, CI):
                later(dve.tensor_scalar(c, c, 128.0, None, ALU.mult))
                later(dve.tensor_scalar(c[:, 0:1], c[:, 0:1], 0.5, None, ALU.mult))
                later(dve.memset(c.rearrange("p (k x) -> p k x", x=LX)[:, 1:16, 0:1], 0.0))
            dve.memset(T2[:, 0:1], 0.0).then_inc(sem("c_ready"), 1)
            later(dve.scalar_tensor_tensor(qk, headw[:, 0, :], 64.0, headw[:, 1, :], ALU.mult, ALU.mult))
            later(dve.tensor_tensor(pv, headw[:, 2, :], headw[:, 3, :], ALU.mult))

            def half_evac(layer, k):
                dve.wait_ge(sem("f1_mm"), 32 * layer + k + 1)
                dve.tensor_copy(A[:, 4 * k:4 * k + 4, :].rearrange("p n k -> p (n k)"), PS[:, k % 4, 0:264]).then_inc(sem("f1_ev"), 1)

            dve.wait_ge(sem("sq_mm"), 16)
            dve.wait_ge(sem("f1_ev"), 32)
            m1, m2, Rx, Cx, mg, eg, Rf, Cf = (SG[:, i, :] for i in range(8))
            later(dve.tensor_copy(m1, A[:, :, 0]))
            later(dve.tensor_copy(m2, PS[:, 4, 0:128]))
            later(dve.tensor_reduce(G8[:, 0:4], m1.rearrange("p (b t) -> p b t", b=B), AX.X, ALU.add))
            dve.tensor_reduce(G8[:, 4:8], m2.rearrange("p (b t) -> p b t", b=B), AX.X, ALU.add).then_inc(sem("g8_ready"), 1)
            dve.wait_ge(sem("g8_mm"), 1)
            rv, mean, rr, cc = rc[:, 0:4], rc[:, 4:8], rc[:, 8:12], rc[:, 12:16]
            later(dve.tensor_copy(mean, PS[:, 6, 0:4]))
            later(dve.tensor_tensor(rv, mean, mean, ALU.mult))
            later(dve.tensor_tensor(rv, PS[:, 6, 4:8], rv, ALU.subtract))
            dve.tensor_scalar(rv, rv, EPS, None, ALU.add).then_inc(sem("var_ready"), 1)
            dve.wait_ge(sem("root_ready"), 1)
            later(dve.reciprocal(rr, rv))
            later(dve.scalar_tensor_tensor(cc, mean, -1.0, rr, ALU.mult, ALU.mult))
            bt = lambda a: a.rearrange("p (b t) -> p b t", b=B)
            rb, cb = rr.unsqueeze(2).broadcast_to([128, B, T]), cc.unsqueeze(2).broadcast_to([128, B, T])
            later(dve.tensor_copy(bt(Rf), rb))
            later(dve.tensor_copy(bt(Cf), cb))
            later(dve.tensor_tensor(mg, Rf, m1, ALU.mult))
            later(dve.tensor_tensor(mg, mg, Cf, ALU.add))
            later(dve.tensor_tensor(Rx, Rf, m2, ALU.mult))
            later(dve.scalar_tensor_tensor(Cx, Cf, 2.0, m1, ALU.mult, ALU.mult))
            later(dve.tensor_tensor(Rx, Rx, Cx, ALU.add))
            later(dve.tensor_tensor(Rx, Rx, Rf, ALU.mult))
            later(dve.tensor_tensor(Cx, Cf, Cf, ALU.mult))
            dve.tensor_tensor(eg, Rx, Cx, ALU.add).then_inc(sem("rc_ready"), 1)
            for b in range(B):
                a = A[:, T * b:T * b + T, :].rearrange("p n k -> p (n k)")
                later(dve.tensor_scalar(a, a, rr[:, b:b + 1], None, ALU.mult))
            for b in range(B):
                ins = dve.tensor_scalar(A[:, T * b:T * b + T, 0:1], A[:, T * b:T * b + T, 0:1], cc[:, b:b + 1], None, ALU.add)
            ins.then_inc(sem("a_ready"), 1)
            dve.wait_ge(sem("is_mm"), 1)
            later(dve.tensor_copy(rim, PS[:, 7, 0:128]))
            dve.tensor_copy(cim, PS[:, 7, 128:256]).then_inc(sem("rim_ready"), 1)
            later(dve.tensor_copy(istat[:, 0:2], PS[:, 6, 16:18]))
            later(dve.tensor_tensor(istat[:, 2:3], istat[:, 0:1], istat[:, 0:1], ALU.mult))
            later(dve.tensor_tensor(istat[:, 2:3], istat[:, 1:2], istat[:, 2:3], ALU.subtract))
            dve.tensor_scalar(istat[:, 2:3], istat[:, 2:3], EPS, None, ALU.add).then_inc(sem("var_ready"), 1)
            dve.wait_ge(sem("root_ready"), 2)
            later(dve.reciprocal(istat[:, 3:4], istat[:, 2:3]))
            later(dve.tensor_tensor(alpha, istat[:, 3:4], PAR["norm1_w"], ALU.mult))
            later(dve.tensor_tensor(beta, istat[:, 0:1], alpha, ALU.mult))
            dve.tensor_tensor(beta, PAR["norm1_b"], beta, ALU.subtract).then_inc(sem("alpha_ready"), 1)
            dve.wait_ge(sem("alpha_ready"), 1)

            forward_evacs(dve, 0, "f2_mm_x", alpha)
            all_emptied(dve, "f2_ev", 1, NF2)
            dve.tensor_tensor(Z[:, 0, 0:1], Z[:, 0, 0:1], beta, ALU.add).then_inc(sem("x_beta"), 1)
            dve.wait_ge(sem("x_beta"), 1)
            for c in range(2):
                for h in range(2):
                    ins = dve.tensor_copy(XL[:, c, 272 * h:272 * h + 272].rearrange("p (k x) -> p k x", x=LX),
                                          Zk[:, c, 48 * h:48 * h + 16, 0:LX])
            ins.then_inc(sem("xl_ready"), 1)
            dve.tensor_tensor(XS, Z[:, 0, :], Z[:, 1, :], ALU.add).then_inc(sem("xs_ready"), 1)
            dve.wait_ge(sem("xe_scaled"), 1)
            later(dve.tensor_tensor(XEk[:, 0, neg, 32], XEk[:, 0, neg, 32], XEk[:, 0, pos, 32], ALU.add))
            later(dve.tensor_tensor(XEk[:, 1, neg, 32], XEk[:, 1, neg, 32], XEk[:, 1, pos, 32], ALU.subtract))
            for c in range(2):
                later(dve.tensor_scalar(XEk[:, c, neg, 32], XEk[:, c, neg, 32], 0.5, None, ALU.mult))
                later(dve.memset(XEk[:, c, 1:32, 0:33:32], 0.0))
            later(dve.memset(XEk[:, 1, 0:33:32, 0:33:32], 0.0))
            dve.tensor_copy(XEk[:, 0, 0:33:32, 0:33:32], Zk[:, 0, 0:33:32, 0:33:32]).then_inc(sem("xe_ready"), 1)
            dve.wait_ge(sem("ct_mm"), 1)
            for k in range(NLC):
                w = min(128, ML - 128 * k)
                dve.tensor_copy(CT[0:w, 0, k, :], PS[0:w, 5, 32 * k:32 * k + 32])
                dve.tensor_copy(CT[0:w, 1, k, :], PS[0:w, 5, 160 + 32 * k:192 + 32 * k])
                later(dve.tensor_scalar(CT[0:w, 2, k, :], PS[0:w, 5, 160 + 32 * k:192 + 32 * k], -1.0, None, ALU.mult))
            dve.memset(lay[:, 0:1], 0.0).then_inc(sem("ct_ready"), 1)
            dve.wait_ge(sem("xlt_mm"), 1)
            for i in range(2 * NLC):
                w = 128 if i % NLC < NLC - 1 else ML - 128 * (NLC - 1)
                ins = dve.tensor_copy(XLT[0:w, i // NLC, i % NLC, :], PS[0:w, (3, 4, 7)[i // 4], 128 * (i % 4):128 * (i % 4) + 128])
            ins.then_inc(sem("xlt_ev"), 1)
            dve.wait_ge(sem("xlt_ev"), 1)
            dve.wait_ge(sem("gram_mm"), 1)
            for b in range(B):
                later(dve.tensor_copy(Gd[32 * b:32 * b + 32, :], PS[32 * b:32 * b + 32, 6, 32 * b:32 * b + 32]))

            for z in range(8 * NLC):
                if z % 4 < 3:
                    score_products(dve, z)
            qkb = qk.unsqueeze(2).broadcast_to([128, NH, T])
            later(dve.tensor_tensor(SE, qkb, Gd.unsqueeze(1).broadcast_to([128, NH, T]), ALU.mult))
            dve.wait_ge(sem("s_mm"), 8 * NLC)
            later(dve.tensor_tensor(SD, SE, PS[:, 0:2, :].rearrange("p h (n s) -> p (h n) s", s=T), ALU.add))
            later(dve.tensor_reduce(rmx, SD, AX.X, ALU.max))
            dve.tensor_tensor(SD, SD, rmx.unsqueeze(2).broadcast_to([128, NH, T]), ALU.subtract).then_inc(sem("sd_ready"), 1)
            dve.wait_ge(sem("se_ready"), 1)
            later(dve.tensor_reduce(rmx, SE, AX.X, ALU.add))
            later(dve.reciprocal(rmx, rmx))
            dve.tensor_tensor(SE, SE, rmx.unsqueeze(2).broadcast_to([128, NH, T]), ALU.mult).then_inc(sem("p_ready"), 1)
            dve.wait_ge(sem("p_ready"), 1)
            later(dve.tensor_tensor(SD, SE, pv.unsqueeze(2).broadcast_to([128, NH, T]), ALU.mult))
            later(dve.tensor_reduce(Pb, SD.rearrange("p n s -> p s n"), AX.X, ALU.add))
            later(dve.memset(SG2, 0.0))
            for b in range(B):
                s = slice(32 * b, 32 * b + 32)
                ins = dve.tensor_copy(SG2[s, s], Pb[s, :])
            ins.then_inc(sem("pb_ready"), 1)
            dve.wait_ge(sem("mix_mm"), 1)
            dve.tensor_copy(Pbt, PS[:, 6, 0:128]).then_inc(sem("pbt_ready"), 1)
            dve.wait_ge(sem("pbt_ready"), 1)
            dve.scalar_tensor_tensor(Mt, Pbt, alpha, ident, ALU.mult, ALU.add).then_inc(sem("mt_ready"), 1)
            dve.wait_ge(sem("mix_mm"), 2)
            dve.tensor_copy(istat[:, 0:1], PS[:, 7, 0:1]).then_inc(sem("pbar_ready"), 1)
            def value_sums(r):
                m = slice(MR * r, MR * r + MR)
                dve.wait_ge(sem("k1_ready"), r + 1)
                if r == 0:
                    dve.wait_ge(sem("x_out"), 48)
                dve.tensor_tensor(Z[:, 0, m], Z[:, 2, m], PS[:, 3 * (r % 2) + 2, 0:MR], ALU.subtract)
                later(dve.tensor_tensor(Z[:, 1, m], Z[:, 2, m], PS[:, 3 * (r % 2) + 1, 0:MR], ALU.add))
                dve.tensor_scalar(Z[:, 2, m], Z[:, 0, m], -1.0, None, ALU.mult).then_inc(sem("zv_ev"), 1)

            for k in range(NR * NQ):
                value_products(dve, k, ((slice(0, 2), slice(0, 3)), (slice(2, 3), slice(0, 2))), "y_dve")
                if k % NQ == 1 and k > NQ:
                    value_sums(k // NQ - 1)
            value_sums(NR - 1)
            dve.wait_ge(sem("zv_ev"), NR)
            later(dve.tensor_tensor(Z[:, 0, 0:1], Z[:, 0, 0:1], istat[:, 0:1], ALU.add))
            dve.tensor_scalar(Z[:, 2, 0:1], Z[:, 0, 0:1], -1.0, None, ALU.mult).then_inc(sem("z_ready"), 1)
            Um = U[:].rearrange("p n w -> p w n")
            dve.wait_ge(sem("z_ready"), 1)
            for g in range(0, 32, 2):
                dve.wait_ge(sem("mx_mm"), g + 1)
                dve.tensor_copy(Um[:, 4 * g:4 * g + 4, :], PS[:, g % 4, :].rearrange("p (w n) -> p w n", w=4)).then_inc(sem("mx_ev0"), 1)

            def transposed_evacs(layer):
                for g in range(0, NTR, 2):
                    dve.wait_ge(sem("tr_mm"), layer * NTR + g + 1)
                    w = 512 if g < NTR - 1 else 256
                    dve.tensor_copy(Af[:, 512 * g:512 * g + w], PS[:, g % 4, 0:w]).then_inc(sem("tr_ev0"), 1)

            def image_stats(src, k):
                for j in range(4):
                    ins = dve.bn_stats(ST[:, 4 * k + j, :], src[:, 4 * k + j, :])
                return ins

            def row_moments():
                s = ST[:].rearrange("p n k -> p k n")
                t, m, e = WS[:, 2, :], WS[:, 0, :], WS[:, 1, :]
                later(dve.tensor_tensor(m, s[:, 1], s[:, 4], ALU.add))
                later(dve.tensor_scalar(m, m, 0.5, None, ALU.mult))
                later(dve.tensor_tensor(e, s[:, 2], s[:, 5], ALU.add))
                later(dve.tensor_scalar(e, e, 1.0 / 128, None, ALU.mult))
                for i in (1, 4):
                    later(dve.scalar_tensor_tensor(t, s[:, i], 0.5, s[:, i], ALU.mult, ALU.mult))
                    later(dve.tensor_tensor(e, e, t, ALU.add))

            all_emptied(dve, "mx_ev", 1, 32)
            transposed_evacs(0)
            for k in range(NIM):
                dve.wait_ge(sem("i2_mm"), k + 1)
                u = U[:, 4 * k:4 * k + 4, :]
                dve.tensor_tensor(u, u, PS[:, 6 + k % 2, :].rearrange("p (n w) -> p n w", w=W), ALU.add).then_inc(sem("i2_ev"), 1)
                if k >= 1:
                    dve.wait_ge(sem("i2_ev"), k)
                    image_stats(U, k - 1)
            dve.wait_ge(sem("i2_ev"), NIM)
            later(image_stats(U, NIM - 1))
            row_moments()
            dve.memset(lay[:, 0:1], 0.0).then_inc(sem("mv_ready"), 1)
            dve.wait_ge(sem("mv_mm"), 1)
            mu, e2, r, v = WS[:, 2, :], WS[:, 1, :], WS[:, 4, :], WS[:, 3, :]
            later(dve.tensor_copy(mu, PS[:, 7, 0:128]))
            later(dve.tensor_tensor(v, mu, mu, ALU.mult))
            later(dve.tensor_tensor(e2, PS[:, 7, 128:256], v, ALU.subtract))
            dve.tensor_scalar(v, e2, EPS, None, ALU.add).then_inc(sem("var_ready"), 1)
            dve.wait_ge(sem("root_ready"), 3)
            later(dve.reciprocal(r, v))
            later(dve.tensor_scalar(r, r, PAR["attn_w"], None, ALU.mult))
            later(dve.tensor_tensor(v, r, r, ALU.mult))
            v2, r2, b2 = WS[:, 5, :], WS[:, 6, :], WS[:, 7, :]
            later(dve.tensor_tensor(v2, v, e2, ALU.mult))
            dve.tensor_scalar(v2, v2, EPS, None, ALU.add).then_inc(sem("var_ready"), 1)
            dve.wait_ge(sem("root_ready"), 4)
            later(dve.reciprocal(r2, v2))
            later(dve.tensor_scalar(r2, r2, PAR["norm2_w"], None, ALU.mult))
            later(dve.tensor_tensor(r2, r2, r, ALU.mult))
            later(dve.tensor_tensor(b2, mu, r2, ALU.mult))
            later(dve.tensor_scalar(b2, b2, -1.0, PAR["norm2_b"], ALU.mult, ALU.add))
            later(dve.tensor_tensor(v2, mu, r, ALU.mult))
            later(dve.tensor_scalar(v2, v2, -1.0, PAR["attn_b"], ALU.mult, ALU.add))
            for k in range(NIM):
                if k % 2 == 0:
                    for i in range(4 * k, 4 * k + 4):
                        ins = dve.tensor_scalar(Vn[:, i, :], U[:, i, :], WS[:, 6, i:i + 1], WS[:, 7, i:i + 1], ALU.mult, ALU.add)
                    ins.then_inc(sem("src_ready"), 1)
                if k >= 2:
                    half_evac(1, k - 2)
            half_evac(1, NIM - 2)
            half_evac(1, NIM - 1)
            for layer in (1, 2):
                if layer == 2:
                    for k in range(NIM):
                        half_evac(2, k)
                dve.wait_ge(sem("f1_ev"), 32 * (layer + 1))
                dve.memset(lay[:, 4:5], 0.0).then_inc(sem("a_ready"), 1)
                forward_evacs(dve, layer, "f2_mm_m", 1.0)
                dve.wait_ge(sem("mw_in"), 16 * layer)
                wk = Af[:, 0:2 * M].rearrange("p (k x c) -> p k x c", k=KY, c=2)
                later(dve.tensor_tensor(wk[:, neg, 0, 0], wk[:, neg, 0, 0], wk[:, pos, 0, 0], ALU.add))
                later(dve.tensor_tensor(wk[:, neg, 0, 1], wk[:, neg, 0, 1], wk[:, pos, 0, 1], ALU.subtract))
                later(dve.memset(wk[:, 1:32, 0, :], 0.0))
                later(dve.memset(wk[:, 0, 0, 1:2], 0.0))
                all_emptied(dve, "f2_ev", layer + 1, NF2)
                dve.memset(lay[:, 7:8], 0.0).then_inc(sem("weights_folded"), 1)
                real, imag = mode_products(dve, later, slice(0, MD))
                real()
                later(dve.memset(Z[:, 2, 0:1], 0.0))
                dve.wait_ge(sem("pool_step"), 6 * layer - 2)
                dve.memset(lay[:, 4:5], 0.0).then_inc(sem("yr_ready"), 1)
                imag()
                later(dve.memset(Z[:, 1, 0:1], 0.0))
                dve.wait_ge(sem("pool_step"), 6 * layer)
                dve.memset(lay[:, 5:6], 0.0).then_inc(sem("yi_ready"), 1)
                c0 = Zk[:, 1:3, :, 0]
                later(dve.tensor_tensor(DB[:, 0, 0:128].rearrange("p (c k) -> p c k", c=2), c0, c0, ALU.mult))
                later(dve.tensor_reduce(lay[:, 3:4], DB[:, 0, 0:128], AX.X, ALU.add))
                dve.wait_ge(sem("vsum"), 2 * layer)
                later(dve.tensor_tensor(lay[:, 2:3], lay[:, 0:1], lay[:, 1:2], ALU.add))
                later(dve.tensor_scalar(lay[:, 2:3], lay[:, 2:3], 2.0, EPS, ALU.mult, ALU.add))
                dve.scalar_tensor_tensor(lay[:, 2:3], lay[:, 3:4], -1.5, lay[:, 2:3], ALU.mult, ALU.add).then_inc(sem("var_ready"), 1)
                dve.wait_ge(sem("root_ready"), 4 + layer)
                dve.reciprocal(lay[:, 6:7], lay[:, 2:3]).then_inc(sem("rstd_ready"), 1)
                dve.wait_ge(sem("rstd_ready"), layer)
                later(dve.tensor_scalar(Z[:, 0, :], Z[:, 2, :], lay[:, 6:7], None, ALU.mult))
                dve.wait_ge(sem("z1_scaled"), layer)
                dve.tensor_scalar(Z[:, 2, :], Z[:, 0, :], -1.0, None, ALU.mult).then_inc(sem("z_ready"), 1)
                transposed_evacs(layer)
                sw = PAR["m0sw"] if layer == 1 else PAR["m1sw"]
                for k in range(NIM):
                    dve.wait_ge(sem("i2_mm"), NIM * layer + k + 1)
                    v4 = Vn[:, 4 * k:4 * k + 4, :]
                    y = dve.scalar_tensor_tensor(v4, v4, sw, PS[:, 6 + k % 2, :].rearrange("p (n w) -> p n w", w=W), ALU.mult, ALU.add)
                    y.then_inc(sem("i2_ev"), 1)
                    if layer == 1:
                        dve.wait_ge(sem("i2_ev"), NIM * layer + k + 1)
                        dve.memset(lay[:, 7:8], 0.0).then_inc(sem("y1_ready"), 1)
                    elif k >= 1:
                        dve.wait_ge(sem("i2_ev"), NIM * layer + k)
                        image_stats(Vn, k - 1)
            dve.wait_ge(sem("i2_ev"), 3 * NIM)
            later(image_stats(Vn, NIM - 1))
            row_moments()
            dve.memset(lay[:, 0:1], 0.0).then_inc(sem("mv_ready"), 1)
            dve.wait_ge(sem("mv_mm"), 2)
            later(dve.tensor_copy(mu, PS[:, 0, 0:128]))
            later(dve.tensor_tensor(v, mu, mu, ALU.mult))
            later(dve.tensor_tensor(e2, PS[:, 0, 128:256], v, ALU.subtract))
            dve.tensor_scalar(v, e2, EPS, None, ALU.add).then_inc(sem("var_ready"), 1)
            dve.wait_ge(sem("root_ready"), 7)
            later(dve.reciprocal(v, v))
            later(dve.tensor_scalar(v, v, PAR["mon_w"], None, ALU.mult))
            later(dve.tensor_tensor(b2, mu, v, ALU.mult))
            dve.tensor_scalar(b2, b2, -1.0, PAR["mon_b"], ALU.mult, ALU.add).then_inc(sem("fin_coef"), 1)
            dve.wait_ge(sem("fin_coef"), 1)
            for g in range(NIM + 5):
                if g < NIM and g % 4 == 3:
                    for i in range(4 * g, 4 * g + 4):
                        ins = dve.tensor_scalar(Vn[:, i, :], Vn[:, i, :], WS[:, 3, i:i + 1], WS[:, 7, i:i + 1], ALU.mult, ALU.add)
                    ins.then_inc(sem("mn_dve"), 1)
                if g >= 5:
                    dve.wait_ge(sem("x1_ready"), g - 4)
                    ins = image_stats(U, g - 5)
            later(ins)
            vector_l1(dve, st, image_stats, row_moments)




_INS = ['x', 'L0_conv_norm1_w', 'L0_conv_norm1_b', 'L0_conv_Kcw', 'L0_conv_Ksw', 'L0_conv_Qcw', 'L0_conv_Qsw', 'L0_conv_Vcw',
        'L0_conv_Vsw', 'L0_conv_Pcw', 'L0_conv_Psw', 'L0_conv_attn_w', 'L0_conv_attn_b', 'L0_conv_norm2_w', 'L0_conv_norm2_b',
        'L0_conv_m0cw', 'L0_conv_m0sw', 'L0_conv_m1cw', 'L0_conv_m1sw', 'L0_conv_mon_w', 'L0_conv_mon_b', 'L1_attn_Wq',
        'L1_attn_Wk', 'L1_attn_Wv', 'L1_ffn_gate_w', 'L1_ffn_gate_b', 'L1_ffn_weight1', 'L1_ffn_weight2']


def kernel(**inputs):
    import numpy as _np
    import concourse.bacc as _bacc
    from concourse.bass_utils import run_bass_kernel_spmd as _run

    nc = _bacc.Bacc("TRN2", target_bir_lowering=False, num_devices=1)
    arrays, io = {}, {}
    for name in _INS:
        a = _np.ascontiguousarray(inputs[name])
        arrays[f"in_{name}"] = a
        io[name] = nc.dram_tensor(f"in_{name}", a.shape, mybir.dt.from_np(a.dtype), kind="ExternalInput").ap()
    c = shape_constants()
    arrays["in_consts"] = c
    io["consts"] = nc.dram_tensor("in_consts", c.shape, F32, kind="ExternalInput").ap()
    out = nc.dram_tensor("out_0", (B, T, H, W), F32, kind="ExternalOutput").ap()
    conv_attn_hybrid(nc, io, out)
    r = _run(nc, [arrays], core_ids=[0])
    return r.results[0]["out_0"]
```
